# Optimizing a Trainium2 kernel written in Bass

```python
import numpy as np
import jax
import jax.numpy as jnp

def _softmax(x, axis=-1):
    return jax.nn.softmax(x, axis=axis)

def _gelu(x):
    return jax.nn.gelu(x, approximate=True)

def _silu(x):
    return jax.nn.silu(x)

def _sigmoid(x):
    return jax.nn.sigmoid(x)

def _layernorm(x, axis=-1, eps=1e-05):
    m = jnp.mean(x, axis=axis, keepdims=True)
    v = jnp.var(x, axis=axis, keepdims=True)
    return (x - m) / jnp.sqrt(v + eps)

def _scatter_add(tgt, idx, src, axis=0):
    return tgt.at[idx].add(src)

def _segment_sum(src, seg, n):
    return jax.ops.segment_sum(src, seg, n)
kernel_name = 'mk_flamingo_gated_d2_seqx_r8_74ca0c'

def setup_inputs(seed: int=0):
    np.random.seed(seed)
    _w = jnp.asarray

    def _rec_inputs():
        import jax
        import jax.numpy as jnp
        _rk = jax.random.key(seed)
        x = -0.0003929 + 0.9999 * jax.random.normal(jax.random.fold_in(_rk, 1), (128, 64, 128), jnp.float32)
        _lenS = 64 - jax.random.randint(jax.random.fold_in(_rk, 7), (128,), 0, max(1, 64 // 4) + 1, jnp.int32)
        _lenS2 = 64 - jax.random.randint(jax.random.fold_in(_rk, 8), (128,), 0, max(1, 64 // 4) + 1, jnp.int32)
        _ctx_1024P = jax.random.normal(jax.random.fold_in(_rk, 11), (128, 16, 128), jnp.float32)
        _ctx_1024c = jax.random.dirichlet(jax.random.fold_in(_rk, 511), 0.3 * jnp.ones((16,), jnp.float32), (128, 64))
        _ctx_1024t = jnp.einsum('bsk,bkd->bsd', _ctx_1024c, _ctx_1024P)
        _ctx_1024t = _ctx_1024t * jax.lax.rsqrt(jnp.mean(jnp.square(_ctx_1024t)) + 1e-12) * 0.953939
        ctx_1024 = 2.81802e-05 + 1.00001 * (_ctx_1024t + 0.3 * jax.random.normal(jax.random.fold_in(_rk, 611), (128, 64, 128), jnp.float32))
        _g = jax.random.normal(jax.random.fold_in(_rk, 9001), (2, 2), jnp.float32)
        _g = jnp.sign(_g) * jnp.maximum(jnp.abs(_g), 1.0) + (_g == 0) * 1.0
        g_xattn = _g[0]
        g_ffn = _g[1]
        return (x, ctx_1024, g_xattn, g_ffn)
    x, ctx_1024, g_xattn, g_ffn = _rec_inputs()

    def _L0_xattn_setup():
        import jax, jax.numpy as jnp
        import numpy as np
        N, L, HID, EMB, NH = (4, 512, 128, 128, 16)
        HD = EMB // NH
        key = jax.random.key(seed)
        ks = jax.random.split(key, 11)
        s_in = 1.0 / np.sqrt(HID)
        s_out = 1.0 / np.sqrt(EMB)
        return {'Q': jax.random.normal(ks[0], (N, L, HID), jnp.float32), 'K': jax.random.normal(ks[1], (N, L, HID), jnp.float32), 'V': jax.random.normal(ks[2], (N, L, HID), jnp.float32), 'Wq': jax.random.uniform(ks[3], (EMB, HID), jnp.float32, -s_in, s_in), 'bq': jax.random.uniform(ks[4], (EMB,), jnp.float32, -s_in, s_in), 'Wk': jax.random.uniform(ks[5], (EMB, HID), jnp.float32, -s_in, s_in), 'bk': jax.random.uniform(ks[6], (EMB,), jnp.float32, -s_in, s_in), 'Wv': jax.random.uniform(ks[7], (EMB, HID), jnp.float32, -s_in, s_in), 'bv': jax.random.uniform(ks[8], (EMB,), jnp.float32, -s_in, s_in), 'Wo': jax.random.uniform(ks[9], (HID, EMB), jnp.float32, -s_out, s_out), 'bo': jax.random.uniform(ks[10], (HID,), jnp.float32, -s_out, s_out)}
    _L0_xattn_all = _L0_xattn_setup()
    _L0_xattn_in = {k: v for k, v in _L0_xattn_all.items() if k in ('Wq', 'bq', 'Wk', 'bk', 'Wv', 'bv', 'Wo', 'bo')}
    del _L0_xattn_all

    def _L0_ffn_setup():
        import jax, jax.numpy as jnp
        import numpy as np
        HIDDEN = 128
        NUM_EXPERTS = 8
        TOP_K = 2
        B, S = (2, 256)
        key = jax.random.key(seed)
        k1, k2, k3, k4, k5 = jax.random.split(key, 5)
        d, dff, E = (HIDDEN, 4 * HIDDEN, NUM_EXPERTS)
        x = jax.random.normal(k1, (B, S, d), dtype=jnp.float32)
        W1 = jax.random.normal(k2, (E, d, dff), dtype=jnp.float32) * (1.0 / np.sqrt(d))
        b1 = jax.random.normal(k3, (E, dff), dtype=jnp.float32) * 0.01
        W2 = jax.random.normal(k4, (E, dff, d), dtype=jnp.float32) * (1.0 / np.sqrt(dff))
        b2 = jax.random.normal(k5, (E, d), dtype=jnp.float32) * 0.01
        return {'x': x, 'W1': W1, 'b1': b1, 'W2': W2, 'b2': b2}
    _L0_ffn_all = _L0_ffn_setup()
    _L0_ffn_in = {k: v for k, v in _L0_ffn_all.items() if k in ('W1', 'b1', 'W2', 'b2')}
    del _L0_ffn_all

    def _L1_xattn_setup():
        import jax, jax.numpy as jnp
        import numpy as np
        C = 128
        B, HW, N = (8, 512, 77)
        key = jax.random.key(seed)
        ks = jax.random.split(key, 14)
        s = 1.0 / np.sqrt(C)
        inp = {'vis_features': jax.random.normal(ks[0], (B, HW, C), jnp.float32), 'lang_features': jax.random.normal(ks[1], (B, N, C), jnp.float32), 'W_vk': jax.random.uniform(ks[2], (C, C), jnp.float32, -s, s), 'b_vk': jax.random.uniform(ks[3], (C,), jnp.float32, -s, s), 'W_lk': jax.random.uniform(ks[4], (C, C), jnp.float32, -s, s), 'b_lk': jax.random.uniform(ks[5], (C,), jnp.float32, -s, s), 'W_vv': jax.random.uniform(ks[6], (C, C), jnp.float32, -s, s), 'b_vv': jax.random.uniform(ks[7], (C,), jnp.float32, -s, s), 'W_lv': jax.random.uniform(ks[8], (C, C), jnp.float32, -s, s), 'b_lv': jax.random.uniform(ks[9], (C,), jnp.float32, -s, s)}
        return inp
    _L1_xattn_all = _L1_xattn_setup()
    _L1_xattn_in = {k: v for k, v in _L1_xattn_all.items() if k in ('W_vk', 'b_vk', 'W_lk', 'b_lk', 'W_vv', 'b_vv', 'W_lv', 'b_lv')}
    del _L1_xattn_all

    def _L1_ffn_setup():
        import jax, jax.numpy as jnp
        import numpy as np
        DIM = 128
        INTER = 128
        N_EXPERTS = 8
        TOPK = 2
        N_SHARED = 2
        key = jax.random.key(seed)
        ks = jax.random.split(key, 10)
        s = 0.02
        return {'x': jax.random.normal(ks[0], (4, 256, DIM), dtype=jnp.float32), 'gate_w': jax.random.normal(ks[1], (N_EXPERTS, DIM), dtype=jnp.float32) * s, 'gate_bias': jax.random.normal(ks[2], (N_EXPERTS,), dtype=jnp.float32) * s, 'w1': jax.random.normal(ks[3], (N_EXPERTS, INTER, DIM), dtype=jnp.float32) * s, 'w3': jax.random.normal(ks[4], (N_EXPERTS, INTER, DIM), dtype=jnp.float32) * s, 'w2': jax.random.normal(ks[5], (N_EXPERTS, DIM, INTER), dtype=jnp.float32) * s, 'sw1': jax.random.normal(ks[6], (N_SHARED * INTER, DIM), dtype=jnp.float32) * s, 'sw3': jax.random.normal(ks[7], (N_SHARED * INTER, DIM), dtype=jnp.float32) * s, 'sw2': jax.random.normal(ks[8], (DIM, N_SHARED * INTER), dtype=jnp.float32) * s}
    _L1_ffn_all = _L1_ffn_setup()
    _L1_ffn_in = {k: v for k, v in _L1_ffn_all.items() if k in ('gate_w', 'gate_bias', 'w1', 'w3', 'w2', 'sw1', 'sw3', 'sw2')}
    del _L1_ffn_all
    return {'x': x, 'ctx_1024': ctx_1024, 'g_xattn': g_xattn, 'g_ffn': g_ffn, 'L0_xattn_Wq': _L0_xattn_in['Wq'], 'L0_xattn_bq': _L0_xattn_in['bq'], 'L0_xattn_Wk': _L0_xattn_in['Wk'], 'L0_xattn_bk': _L0_xattn_in['bk'], 'L0_xattn_Wv': _L0_xattn_in['Wv'], 'L0_xattn_bv': _L0_xattn_in['bv'], 'L0_xattn_Wo': _L0_xattn_in['Wo'], 'L0_xattn_bo': _L0_xattn_in['bo'], 'L0_ffn_W1': _L0_ffn_in['W1'], 'L0_ffn_b1': _L0_ffn_in['b1'], 'L0_ffn_W2': _L0_ffn_in['W2'], 'L0_ffn_b2': _L0_ffn_in['b2'], 'L1_xattn_W_vk': _L1_xattn_in['W_vk'], 'L1_xattn_b_vk': _L1_xattn_in['b_vk'], 'L1_xattn_W_lk': _L1_xattn_in['W_lk'], 'L1_xattn_b_lk': _L1_xattn_in['b_lk'], 'L1_xattn_W_vv': _L1_xattn_in['W_vv'], 'L1_xattn_b_vv': _L1_xattn_in['b_vv'], 'L1_xattn_W_lv': _L1_xattn_in['W_lv'], 'L1_xattn_b_lv': _L1_xattn_in['b_lv'], 'L1_ffn_gate_w': _L1_ffn_in['gate_w'], 'L1_ffn_gate_bias': _L1_ffn_in['gate_bias'], 'L1_ffn_w1': _L1_ffn_in['w1'], 'L1_ffn_w3': _L1_ffn_in['w3'], 'L1_ffn_w2': _L1_ffn_in['w2'], 'L1_ffn_sw1': _L1_ffn_in['sw1'], 'L1_ffn_sw3': _L1_ffn_in['sw3'], 'L1_ffn_sw2': _L1_ffn_in['sw2']}

def reference(x, ctx_1024, g_xattn, g_ffn, L0_xattn_Wq, L0_xattn_bq, L0_xattn_Wk, L0_xattn_bk, L0_xattn_Wv, L0_xattn_bv, L0_xattn_Wo, L0_xattn_bo, L0_ffn_W1, L0_ffn_b1, L0_ffn_W2, L0_ffn_b2, L1_xattn_W_vk, L1_xattn_b_vk, L1_xattn_W_lk, L1_xattn_b_lk, L1_xattn_W_vv, L1_xattn_b_vv, L1_xattn_W_lv, L1_xattn_b_lv, L1_ffn_gate_w, L1_ffn_gate_bias, L1_ffn_w1, L1_ffn_w3, L1_ffn_w2, L1_ffn_sw1, L1_ffn_sw3, L1_ffn_sw2):
    import jax
    import jax.numpy as jnp

    def _L0_xattn_ref(Q, K, V, Wq, bq, Wk, bk, Wv, bv, Wo, bo):
        import jax, jax.numpy as jnp
        import numpy as np
        N, L, HID, EMB, NH = (4, 512, 128, 128, 16)
        HD = EMB // NH
        n, ql = (Q.shape[0], Q.shape[1])
        q = (Q @ Wq.T + bq).reshape(n, ql, NH, HD)
        k = (K @ Wk.T + bk).reshape(n, K.shape[1], NH, HD)
        v = (V @ Wv.T + bv).reshape(n, V.shape[1], NH, HD)
        attn = jnp.einsum('nlhd,nled->nlhe', q, k) / jnp.sqrt(jnp.asarray(HD, q.dtype))
        attn = jax.nn.softmax(attn, axis=-1)
        ctx = jnp.einsum('nlhe,nled->nlhd', attn, v)
        ctx = ctx.reshape(n, ql, NH * HD)
        return ctx @ Wo.T + bo

    def _L0_ffn_ref(x, W1, b1, W2, b2):
        import jax, jax.numpy as jnp
        import numpy as np
        HIDDEN = 128
        NUM_EXPERTS = 8
        TOP_K = 2
        B, S = (2, 256)
        Bm, Sm, d = x.shape
        E = W1.shape[0]
        x_flat = x.reshape(-1, d)
        h = jnp.mod(x_flat[:, :TOP_K].sum(axis=1).astype(jnp.int32), E)
        sel = jnp.stack([h, jnp.mod(h + 1, E)], axis=1)

        def step(acc, params):
            e, W1e, b1e, W2e, b2e = params
            w = jnp.any(sel == e, axis=1).astype(x.dtype) / TOP_K
            y = jnp.maximum(x_flat @ W1e + b1e, 0.0) @ W2e + b2e
            return (acc + w[:, None] * y, None)
        init = jnp.zeros_like(x_flat)
        out_flat, _ = jax.lax.scan(step, init, (jnp.arange(E), W1, b1, W2, b2))
        return out_flat.reshape(Bm, Sm, d)

    def _L1_xattn_ref(vis_features, lang_features, W_vk, b_vk, W_lk, b_lk, W_vv, b_vv, W_lv, b_lv):
        import jax, jax.numpy as jnp
        import numpy as np
        C = 128
        B, HW, N = (8, 512, 77)
        scale = jnp.asarray(C, vis_features.dtype) ** (-0.5)
        vis_key = jnp.einsum('bsc,dc->bsd', vis_features, W_vk) + b_vk
        lang_key = jnp.einsum('bnc,dc->bnd', lang_features, W_lk) + b_lk
        vis_value = jnp.einsum('bsc,dc->bsd', vis_features, W_vv) + b_vv
        lang_value = jnp.einsum('bnc,dc->bnd', lang_features, W_lv) + b_lv
        attn = jax.nn.softmax(jnp.einsum('bsd,bnd->bsn', vis_key, lang_key) * scale, axis=-1)
        lang_attended_vis = jnp.einsum('bsn,bnc->bsc', attn, lang_value)
        vision_attended_lang = jnp.einsum('bsn,bsc->bnc', attn, vis_value)
        projected = jnp.einsum('bsn,bnc->bsc', attn, vision_attended_lang)
        return lang_attended_vis + projected

    def _L1_ffn_ref(x, gate_w, gate_bias, w1, w3, w2, sw1, sw3, sw2):
        import jax, jax.numpy as jnp
        import numpy as np
        DIM = 128
        INTER = 128
        N_EXPERTS = 8
        TOPK = 2
        N_SHARED = 2
        shape = x.shape
        xt = x.reshape(-1, shape[-1])
        scores = jax.nn.softmax((xt @ gate_w.T).astype(jnp.float32), axis=-1)
        _, idx = jax.lax.top_k(scores + gate_bias, TOPK)
        weights = jnp.take_along_axis(scores, idx, axis=1).astype(x.dtype)
        y = jnp.zeros_like(xt)
        for e in range(N_EXPERTS):
            gate_e = jnp.sum(jnp.where(idx == e, weights, 0.0), axis=1)
            h = jax.nn.silu(xt @ w1[e].T) * (xt @ w3[e].T)
            y = y + gate_e[:, None] * (h @ w2[e].T)
        z = jax.nn.silu(xt @ sw1.T) * (xt @ sw3.T) @ sw2.T
        return (y + z).reshape(shape)
    x = x + jnp.tanh(g_xattn[0]) * _L0_xattn_ref(_layernorm(x, axis=-1), ctx_1024, ctx_1024, L0_xattn_Wq, L0_xattn_bq, L0_xattn_Wk, L0_xattn_bk, L0_xattn_Wv, L0_xattn_bv, L0_xattn_Wo, L0_xattn_bo)
    x = x + jnp.tanh(g_ffn[0]) * _L0_ffn_ref(_layernorm(x, axis=-1), L0_ffn_W1, L0_ffn_b1, L0_ffn_W2, L0_ffn_b2)
    x = x + jnp.tanh(g_xattn[1]) * _L1_xattn_ref(_layernorm(x, axis=-1), ctx_1024, L1_xattn_W_vk, L1_xattn_b_vk, L1_xattn_W_lk, L1_xattn_b_lk, L1_xattn_W_vv, L1_xattn_b_vv, L1_xattn_W_lv, L1_xattn_b_lv)
    x = x + jnp.tanh(g_ffn[1]) * _L1_ffn_ref(_layernorm(x, axis=-1), L1_ffn_gate_w, L1_ffn_gate_bias, L1_ffn_w1, L1_ffn_w3, L1_ffn_w2, L1_ffn_sw1, L1_ffn_sw3, L1_ffn_sw2)
    return x

_drawn_inputs = setup_inputs


def setup_inputs(seed=0):
    import zlib

    import numpy as np

    out = dict(_drawn_inputs(seed))
    spreads = {'g_ffn': (-1.0, 0.6)}
    factors = {'L0_xattn_bq': 5.451,
     'L0_xattn_bk': 5.681,
     'L0_ffn_b1': 8.0,
     'L0_ffn_b2': 8.0,
     'L1_xattn_b_vk': 8.0,
     'L1_xattn_b_lk': 8.0,
     'L1_ffn_gate_w': 8.0,
     'L1_ffn_gate_bias': 8.0,
     'L1_ffn_w1': 8.0,
     'L1_ffn_w3': 8.0,
     'L1_ffn_w2': 8.0,
     'L1_ffn_sw1': 8.0,
     'L1_ffn_sw3': 8.0,
     'L1_ffn_sw2': 8.0}
    for name, (base, spread) in spreads.items():
        noise = np.random.default_rng([zlib.crc32(name.encode()), seed]).standard_normal(out[name].shape)
        drawn = base * np.exp(spread * noise) if base else spread * noise
        out[name] = jnp.asarray(drawn.astype(out[name].dtype))
    for name, factor in factors.items():
        out[name] = (out[name] * factor).astype(out[name].dtype)
    return out
```

```python
from contextlib import ExitStack

import concourse.bass as bass
from concourse import mybir

F32 = mybir.dt.float32
F32R = mybir.dt.float32r
BF16 = mybir.dt.bfloat16
I32 = mybir.dt.int32
ALU = mybir.AluOpType
ACT = mybir.ActivationFunctionType
X = mybir.AxisListType.X

P = 128
D = 128
TILES = 4
CH = TILES * P
SEQ = 64
HEADS, HD = 16, 8
HH = HEADS * HEADS
E0, FJ = 8, 4
E1, UNITS = 8, 10
TRUNC_MAX = 17
MOD_K = 5
EPS = 1e-5

WQ, WKV, WO, WVK, WLK, WVV, WLV, WG = 0, 128, 384, 512, 640, 768, 896, 1024
WSMALL = WG + 8
BQ, BKV, BO, BVV, BLV, BG = 0, 128, 384, 512, 640, 768
BROWS = BG + 8
CB1, CB2, CBVK, CBLK = 0, 32, 40, 41
BCOLS = 42


class Signal:

    def __init__(self, sem, per):
        self.sem, self.per = sem, per

    def at(self, c, k=None):
        return c * self.per + (self.per if k is None else k)


def build(nc, x, ctx_in, g_x, g_f, w_small, w1, w2, w13, w2u, bias_rows, bias_cols, out):
    NT = x.shape[0]
    NC = NT // CH
    x_v = x.rearrange("(c j p) d -> p c j d", j=TILES, p=P)
    ctx_v = ctx_in.rearrange("(c j p) d -> p c j d", j=TILES, p=P)
    out_v = out.rearrange("(c j p) d -> p c j d", j=TILES, p=P)

    with ExitStack() as stack:
        def sb(name, shape, dt=F32):
            return stack.enter_context(nc.sbuf_tensor(name, shape, dt))

        def bank(name):
            return stack.enter_context(nc.psum_tensor(name, [P, CH], F32))

        def sem(name):
            return stack.enter_context(nc.semaphore(name))

        def signal(name, per=1):
            return Signal(sem(name), per)

        wg_raw = sb("wg_raw", [P, E1])
        ws_hi, ws_lo = sb("ws_hi", [P, WSMALL], F32R), sb("ws_lo", [P, WSMALL], F32R)
        w1_hi, w1_lo = sb("w1_hi", [P, E0 * FJ * P], F32R), sb("w1_lo", [P, E0 * FJ * P], F32R)
        w13_hi, w13_lo = sb("w13_hi", [P, UNITS * 2 * P], F32R), sb("w13_lo", [P, UNITS * 2 * P], F32R)
        w2_sb = sb("w2_sb", [P, E0 * FJ, D])
        w2u_sb = sb("w2u_sb", [P, UNITS, D])
        brow = sb("brow", [P, BROWS])
        bcol = sb("bcol", [P, BCOLS])
        gates_raw, tg = sb("gates_raw", [P, 4]), sb("tg", [P, 4])
        tgh = sb("tgh", [P, 1])
        gbo = sb("gbo", [P, D])
        ident = sb("ident", [P, P])
        ident_r = sb("ident_r", [P, P], F32R)
        ident_b = sb("ident_b", [P, P], BF16)
        thr_i, thr = sb("thr_i", [P, TRUNC_MAX], I32), sb("thr", [P, TRUNC_MAX])
        mod_i, modv = sb("mod_i", [P, E0, MOD_K], I32), sb("modv", [P, E0, MOD_K])
        before = sb("before", [P, E1, E1])
        neghalf = sb("neghalf", [P, TILES])

        x0, ctx_a, ctx_c = (sb(n, [P, TILES, D]) for n in ("x0", "ctx_a", "ctx_c"))
        xp, x1, x2, x3 = (sb(n, [P, TILES, D]) for n in ("xp", "x1", "x2", "x3"))
        xn = [sb(f"xn{k}", [P, TILES, D]) for k in range(4)]
        q_sb = sb("q_sb", [P, TILES, D])
        o_sb = q_sb
        kv_sb = sb("kv_sb", [P, TILES, 2 * D])
        vv_sb, lv_sb = (sb(n, [P, TILES, D]) for n in ("vv_sb", "lv_sb"))
        u_sb = lv_sb
        prod = sb("prod", [P, 2, HH * HD])
        s0 = sb("s0", [P, TILES, HEADS, HEADS])
        mx0, sum0, rec0 = (sb(n, [P, TILES, HEADS]) for n in ("mx0", "sum0", "rec0"))
        sc_sb = sb("sc_sb", [P, TILES, SEQ])
        mx1, sum1, rec1 = (sb(n, [P, TILES]) for n in ("mx1", "sum1", "rec1"))
        blockdiag = sb("blockdiag", [P, TILES, P])
        blockdiag_t = sb("blockdiag_t", [P, TILES, P])

        ctx_hi, ctx_lo = sb("ctx_hi", [P, CH], F32R), sb("ctx_lo", [P, CH], F32R)
        ctx2_hi, ctx2_lo = sb("ctx2_hi", [P, CH], F32R), sb("ctx2_lo", [P, CH], F32R)
        xt_hi = [sb(f"xt_hi{k}", [P, CH], F32R) for k in range(3)]
        xt_lo = [sb(f"xt_lo{k}", [P, CH], F32R) for k in range(3)]
        xt_hi, xt_lo = xt_hi + xt_hi[:1], xt_lo + xt_lo[:1]
        ot_hi, ot_lo = ctx_hi, ctx_lo
        vk_t, lk_t = sb("vk_t", [P, CH]), sb("lk_t", [P, CH])
        hidden = sb("hidden", [P, FJ, CH])
        masks = sb("masks", [P, E0, CH], BF16)
        y_term = sb("y_term", [P, 2, CH])
        y_acc = sb("y_acc", [P, CH])
        th, pr, hu = sb("th", [P, 2, CH]), sb("pr", [P, CH]), sb("hu", [P, 2, CH])
        y1_sb = pr
        ws_raw = th[:, :, :].rearrange("p a n -> p (a n)")
        w1_raw = prod[:, :, :].rearrange("p a n -> p (a n)")
        w13_raw = (hidden[:, :, :].rearrange("p a n -> p (a n)"), y_acc[:])

        stats = [sb(f"stats{k}", [P, TILES, 6]) for k in range(4)]
        msum = [sb(f"msum{k}", [P, TILES, 2]) for k in range(4)]
        dmean, var = ([sb(f"{n}{k}", [P, TILES]) for k in range(4)] for n in ("dmean", "var"))
        ve, nmean, rstd, nmr = ([sb(f"{n}{k}", [P, TILES]) for k in range(4)] for n in ("ve", "nmean", "rstd", "nmr"))
        hsum, htr = sb("hsum", [P, TILES]), sb("htr", [P, TILES])
        hge, hle = sb("hge", [P, TILES, TRUNC_MAX]), sb("hle", [P, TILES, TRUNC_MAX])
        heq = sb("heq", [P, TILES, E0, MOD_K])
        onehot = sb("onehot", [P, TILES, E0])
        sel0 = sb("sel0", [P, TILES, E0], BF16)
        lg, sc1, bs1, gate = (sb(n, [P, TILES, E1]) for n in ("lg", "sc1", "bs1", "gate"))
        lmx, lsum, lrec = (sb(n, [P, TILES]) for n in ("lmx", "lsum", "lrec"))
        cmp_gt, cmp_eq = sb("cmp_gt", [P, TILES, E1, E1]), sb("cmp_eq", [P, TILES, E1, E1])
        rank = sb("rank", [P, TILES, E1])
        g_hi, g_lo = sb("g_hi", [P, TILES, E1], F32R), sb("g_lo", [P, TILES, E1], F32R)

        Z = [bank(f"Z{k}") for k in range(4)]
        Y = [bank(f"Y{k}") for k in range(2)]
        M = [bank(f"M{k}") for k in range(2)]

        def tiles(b):
            return b[:, :].rearrange("p (j d) -> p j d", j=TILES)

        s_ws, s_w1, s_w13, s_w2, s_rows, s_cols, s_g = (sem(f"s_{n}") for n in ("ws", "w1", "w13", "w2", "rows", "cols", "g"))
        s_pool, s_act0, s_dve0 = sem("s_pool_consts"), sem("s_act_consts"), sem("s_dve_consts")
        POOL_CONSTS, ACT_CONSTS, DVE_CONSTS = 9, 4, 11

        ld_x, ld_ca, ld_cc, st_out = (signal(n, 16) for n in ("ld_x", "ld_ctx_a", "ld_ctx_c", "st_out"))
        ln_stats = [signal(f"ln_stats{k}", 4) for k in range(4)]
        ln_rstd = [signal(f"ln_rstd{k}", 2) for k in range(4)]
        ln_done = [signal(f"ln_done{k}") for k in range(4)]
        pe_ctxt, pe_ctx2t = signal("pe_ctxt"), signal("pe_ctx2t")
        pe_xt = [signal(f"pe_xt{k}") for k in range(4)]
        hi_ctx, hi_ctx2, hi_o = signal("hi_ctx"), signal("hi_ctx2"), signal("hi_o")
        lo_ctx, lo_ctx2, lo_o = signal("lo_ctx"), signal("lo_ctx2"), signal("lo_o")
        hi_xt = [signal(f"hi_xt{k}") for k in range(4)]
        lo_xt = [signal(f"lo_xt{k}") for k in range(4)]
        pe_q, pe_kv = signal("pe_q"), signal("pe_kv", 2)
        qkv = signal("qkv_ready", 3)
        pool_xp = signal("pool_xp")
        pool_qk, pool_av = signal("pool_qk", TILES), signal("pool_av", TILES)
        score0 = signal("score0", TILES)
        sub0 = signal("sub0", 4)
        exp0 = signal("exp0", 2)
        rec0_s = signal("rec0_s", 4)
        av_sum = signal("av_sum", TILES)
        o_ready = signal("o_ready", 2)
        pe_ot, pe_wo, x1_s = signal("pe_ot"), signal("pe_wo"), signal("x1_ready")
        sel_s = signal("sel0_ready", 9)
        pe_mask, mask_s = signal("pe_mask", E0), signal("mask_ready", E0)
        pe_z, relu_s = signal("pe_z", E0 * FJ), signal("relu_ready", E0 * FJ)
        pe_y, term_s, acc_s = signal("pe_y", E0), signal("term_ready", E0), signal("acc_ready", E0 - 1)
        pe_yt, x2_s = signal("pe_yt"), signal("x2_ready")
        pe_vk, pe_lk, pe_vv, pe_lv = (signal(f"pe_{n}") for n in ("vk", "lk", "vv", "lv"))
        vk_s, lk_s, vv_s, lv_s = (signal(f"{n}_ready") for n in ("vk", "lk", "vv", "lv"))
        pe_sc, sub1, exp1 = signal("pe_scores"), signal("sub1", 2), signal("exp1")
        bd_s = signal("blockdiag_ready", 4)
        pe_val, u_s, pe_bdt, bdt_s = signal("pe_val"), signal("u_ready"), signal("pe_bdt"), signal("bdt_ready")
        pe_att, x3_s = signal("pe_att"), signal("x3_ready")
        pe_lg, lsub, lexp = signal("pe_logits"), signal("lsub", 2), signal("lexp")
        route = signal("route", 12)
        pe_ab, tanh_s = signal("pe_ab", UNITS), signal("tanh_ready", UNITS)
        pr_s, hu_s, hg_s = signal("pr_ready", UNITS), signal("hu_ready", UNITS), signal("hu_gated", E1)
        pe_g, pe_f = signal("pe_gate", E1), signal("pe_ffn1", UNITS)
        y1_s, pe_out, out_s = signal("y1_ready"), signal("pe_out"), signal("out_ready")

        block = stack.enter_context(nc.Block())

        def run(eng, body):
            for i in (-2, -1, 0, 1):
                body(i)
            with eng.Fori(2, NC - 2) as i:
                body(i)
            for i in (NC - 2, NC - 1, NC):
                body(i)

        def exists(c):
            return not isinstance(c, int) or 0 <= c < NC

        def is_step(i, k):
            return isinstance(i, int) and i == k

        @block.sync
        def _(sp):
            sp.dma_start(ws_raw, w_small[:, 0:WG]).then_inc(s_ws, 16)
            sp.dma_start(wg_raw[:], w_small[:, WG:WSMALL]).then_inc(s_ws, 16)
            sp.dma_start(brow[:], bias_rows.partition_broadcast(P)).then_inc(s_rows, 16)
            sp.dma_start(bcol[:], bias_cols).then_inc(s_cols, 16)
            sp.dma_start(gates_raw[:, 0:2], g_x.partition_broadcast(P)).then_inc(s_g, 16)
            sp.dma_start(gates_raw[:, 2:4], g_f.partition_broadcast(P)).then_inc(s_g, 16)

            def body(i):
                if exists(i + 2):
                    c = i + 2
                    if exists(c - 1):
                        sp.wait_ge(ln_done[0].sem, ln_done[0].at(c - 1))
                    if exists(c - 1):
                        sp.wait_ge(pool_xp.sem, pool_xp.at(c - 1))
                    sp.dma_start(x0[:], x_v[:, bass.ds(c, 1)].rearrange("p c j d -> p (c j) d")).then_inc(ld_x.sem, 16)
                    if exists(c - 1):
                        sp.wait_ge(pe_ctxt.sem, pe_ctxt.at(c - 1))
                    sp.dma_start(ctx_a[:], ctx_v[:, bass.ds(c, 1)].rearrange("p c j d -> p (c j) d")).then_inc(ld_ca.sem, 16)
                if exists(i):
                    if exists(i - 1):
                        sp.wait_ge(pe_ctx2t.sem, pe_ctx2t.at(i - 1))
                    sp.dma_start(ctx_c[:], ctx_v[:, bass.ds(i, 1)].rearrange("p c j d -> p (c j) d")).then_inc(ld_cc.sem, 16)
                if exists(i - 1):
                    c = i - 1
                    sp.wait_ge(out_s.sem, out_s.at(c))
                    sp.dma_start(out_v[:, bass.ds(c, 1)].rearrange("p c j d -> p (c j) d"), x3[:]).then_inc(st_out.sem, 16)

            body(-2)
            sp.dma_start(w1_raw, w1).then_inc(s_w1, 16)
            sp.dma_start(w2_sb[:, :, :].rearrange("p a n -> p (a n)"), w2).then_inc(s_w2, 16)
            sp.dma_start(w13_raw[0], w13[:, 0:FJ * CH]).then_inc(s_w13, 16)
            sp.dma_start(w13_raw[1], w13[:, FJ * CH:UNITS * 2 * P]).then_inc(s_w13, 16)
            sp.dma_start(w2u_sb[:, :, :].rearrange("p a n -> p (a n)"), w2u).then_inc(s_w2, 16)
            for i in (-1, 0, 1):
                body(i)
            with sp.Fori(2, NC - 2) as i:
                body(i)
            for i in (NC - 2, NC - 1, NC):
                body(i)
            sp.wait_ge(st_out.sem, st_out.at(NC - 1))

        @block.gpsimd
        def _(pool):
            pool.memset(ident[:], 0.0).then_inc(s_pool, 1)
            pool.memset(before[:], 1.0).then_inc(s_pool, 1)
            pool.wait_ge(s_pool, 2)
            pool.affine_select(out=ident[:], in_=ident[:], compare_op=ALU.not_equal, fill=1.0, base=0,
                               pattern=[[-1, P]], channel_multiplier=1).then_inc(s_pool, 1)
            pool.affine_select(out=before[:], in_=before[:], compare_op=ALU.is_ge, fill=0.0, base=-1,
                               pattern=[[1, E1], [-1, E1]], channel_multiplier=0).then_inc(s_pool, 1)
            pool.iota(thr_i[:], pattern=[[1, TRUNC_MAX]], base=1, channel_multiplier=0).then_inc(s_pool, 1)
            pool.iota(mod_i[:], pattern=[[1, E0], [E0, MOD_K]], base=-2 * E0, channel_multiplier=0).then_inc(s_pool, 1)
            pool.memset(neghalf[:], -0.5).then_inc(s_pool, 1)
            pool.memset(blockdiag[:, 0:2, :], 0.0).then_inc(s_pool, 1)
            pool.memset(blockdiag[:, 2:4, :], 0.0).then_inc(s_pool, 1)
            pool.wait_ge(s_pool, POOL_CONSTS)

            def norm(k, c):
                pool.wait_ge(ln_stats[k].sem, ln_stats[k].at(c))
                pool.tensor_tensor(out=rstd[k][:], in0=ve[k][:], in1=neghalf[:], op=ALU.pow).then_inc(ln_rstd[k].sem, 1)
                pool.wait_ge(ln_rstd[k].sem, ln_rstd[k].at(c, 1))
                if exists(c - 1):
                    pool.wait_ge(ln_done[k].sem, ln_done[k].at(c - 1))
                pool.tensor_tensor(out=nmr[k][:], in0=nmean[k][:], in1=rstd[k][:], op=ALU.mult).then_inc(ln_rstd[k].sem, 1)

            def times_k(c, t):
                pool.wait_ge(qkv.sem, qkv.at(c, 2 + t // 2))
                if t < 2:
                    if exists(c - 1):
                        pool.wait_ge(av_sum.sem, av_sum.at(c - 1, 3 + t))
                else:
                    pool.wait_ge(score0.sem, score0.at(c, t - 1))
                q = q_sb[:, t, :].rearrange("p (h d) -> p h d", h=HEADS)
                k = kv_sb[:, t, 0:D].rearrange("p (e d) -> p e d", e=HEADS)
                pool.tensor_tensor(out=prod[:, t % 2, :].rearrange("p (h e d) -> p h e d", h=HEADS, e=HEADS),
                                   in0=q.unsqueeze(2).broadcast_to([P, HEADS, HEADS, HD]),
                                   in1=k.unsqueeze(1).broadcast_to([P, HEADS, HEADS, HD]),
                                   op=ALU.mult).then_inc(pool_qk.sem, 1)

            def times_v(c, t):
                pool.wait_ge(exp0.sem, exp0.at(c, 1 + t // 2))
                if t < 2:
                    pool.wait_ge(score0.sem, score0.at(c, 3 + t))
                else:
                    pool.wait_ge(av_sum.sem, av_sum.at(c, t - 1))
                v = kv_sb[:, t, D:2 * D].rearrange("p (d e) -> p d e", e=HEADS)
                pool.tensor_tensor(out=prod[:, t % 2, :].rearrange("p (h d e) -> p h d e", h=HEADS, e=HEADS),
                                   in0=s0[:, t, :, :].unsqueeze(2).broadcast_to([P, HEADS, HD, HEADS]),
                                   in1=v.unsqueeze(1).broadcast_to([P, HEADS, HD, HEADS]),
                                   op=ALU.mult).then_inc(pool_av.sem, 1)

            def add(c, e):
                pool.wait_ge(term_s.sem, term_s.at(c, e + 1))
                if e > 1:
                    pool.wait_ge(acc_s.sem, acc_s.at(c, e - 1))
                else:
                    if exists(c - 1):
                        pool.wait_ge(pe_yt.sem, pe_yt.at(c - 1))
                first = y_term[:, 0, :] if e == 1 else y_acc[:]
                pool.tensor_tensor(out=y_acc[:], in0=first, in1=y_term[:, e % 2, :], op=ALU.add).then_inc(acc_s.sem, 1)

            def body(i):
                a, b, c = i + 1, i, i - 1
                if exists(a):
                    if exists(a - 1):
                        pool.wait_ge(x1_s.sem, x1_s.at(a - 1))
                    pool.wait_ge(ld_x.sem, ld_x.at(a))
                    if isinstance(a, int) and a == 0:
                        pool.wait_ge(s_dve0, DVE_CONSTS)
                        pool.wait_ge(s_act0, ACT_CONSTS)
                    pool.tensor_tensor(out=xp[:], in0=x0[:], in1=gbo[:].unsqueeze(1).broadcast_to([P, TILES, D]),
                                       op=ALU.add).then_inc(pool_xp.sem, 1)
                    times_k(a, 0)
                    times_k(a, 1)
                if exists(b):
                    add(b, 1)
                if exists(a):
                    times_k(a, 2)
                if exists(b):
                    add(b, 2)
                    add(b, 3)
                if exists(a):
                    times_k(a, 3)
                if exists(b):
                    add(b, 4)
                if exists(a):
                    times_v(a, 0)
                if exists(b):
                    add(b, 5)
                if exists(a):
                    times_v(a, 1)
                if exists(c):
                    norm(3, c)
                if exists(b):
                    add(b, 6)
                    add(b, 7)
                if exists(a):
                    times_v(a, 2)
                    times_v(a, 3)
                if exists(b):
                    norm(2, b)
                if exists(a):
                    norm(1, a)
                if exists(i + 2):
                    norm(0, i + 2)

            run(pool, body)

        @block.scalar
        def _(act):
            def weights():
                act.wait_ge(s_g, 32)
                act.activation(tg[:], gates_raw[:], ACT.Tanh).then_inc(s_act0, 1)
                act.wait_ge(s_ws, 32)
                act.activation(ws_hi[:, WG:WSMALL], wg_raw[:], ACT.Copy)
                act.activation(ws_hi[:, 0:WG], ws_raw, ACT.Copy).then_inc(s_act0, 1)
                act.wait_ge(s_w1, 16)
                act.activation(w1_hi[:], w1_raw, ACT.Copy).then_inc(s_act0, 1)
                act.wait_ge(s_w13, 32)
                act.activation(w13_hi[:, 0:FJ * CH], w13_raw[0], ACT.Copy)
                act.activation(w13_hi[:, FJ * CH:UNITS * 2 * P], w13_raw[1], ACT.Copy).then_inc(s_act0, 1)

            def normed(k, src, c):
                act.wait_ge(ln_rstd[k].sem, ln_rstd[k].at(c))
                for j in range(TILES):
                    last = act.activation(xn[k][:, j, :], src[:, j, :], ACT.Identity, bias=nmr[k][:, j:j + 1],
                                          scale=rstd[k][:, j:j + 1])
                last.then_inc(ln_done[k].sem, 1)

            def high(bank_, hi, pe, done, c):
                act.wait_ge(pe.sem, pe.at(c))
                act.activation(hi[:], bank_[:], ACT.Copy).then_inc(done.sem, 1)

            def relus(b, e):
                for j in range(FJ):
                    n = e * FJ + j
                    act.wait_ge(pe_z.sem, pe_z.at(b, n + 1))
                    if e > 0:
                        act.wait_ge(pe_y.sem, pe_y.at(b, e))
                    else:
                        if exists(b - 1):
                            act.wait_ge(pe_y.sem, pe_y.at(b - 1))
                    act.activation(hidden[:, j, :], Z[j][:], ACT.Relu, bias=bcol[:, CB1 + n:CB1 + n + 1]).then_inc(relu_s.sem, 1)

            def tanhs(c, u):
                act.wait_ge(pe_ab.sem, pe_ab.at(c, u + 1))
                if u >= 2:
                    act.wait_ge(pr_s.sem, pr_s.at(c, u - 1))
                else:
                    if exists(c - 1):
                        act.wait_ge(pr_s.sem, pr_s.at(c - 1, UNITS - 1 + u))
                act.activation(th[:, u % 2, :], Z[2 * (u % 2)][:], ACT.Tanh, scale=0.5).then_inc(tanh_s.sem, 1)

            def exp_heads(a, pair):
                act.wait_ge(sub0.sem, sub0.at(a, 2 * pair + 2))
                s = s0[:, 2 * pair:2 * pair + 2, :, :].rearrange("p t h e -> p (t h e)")
                act.activation(s, s, ACT.Exp, scale=HD ** -0.5).then_inc(exp0.sem, 1)

            def body(i):
                a, b, c = i + 1, i, i - 1
                if exists(b):
                    relus(b, 0)
                if exists(a):
                    if exists(a - 1):
                        act.wait_ge(pe_wo.sem, pe_wo.at(a - 1))
                    high(M[0], ctx_hi, pe_ctxt, hi_ctx, a)
                    if exists(a - 3):
                        act.wait_ge(pe_ab.sem, pe_ab.at(a - 3))
                    high(M[1], xt_hi[0], pe_xt[0], hi_xt[0], a)
                if exists(b):
                    relus(b, 1)
                if exists(c):
                    if exists(c - 1):
                        act.wait_ge(pe_vv.sem, pe_vv.at(c - 1))
                    high(M[1], xt_hi[2], pe_xt[2], hi_xt[2], c)
                    if exists(c - 1):
                        act.wait_ge(pe_lv.sem, pe_lv.at(c - 1))
                    high(M[0], ctx2_hi, pe_ctx2t, hi_ctx2, c)
                if exists(b):
                    relus(b, 2)
                if exists(c):
                    act.wait_ge(pe_vk.sem, pe_vk.at(c))
                    if exists(c - 1):
                        act.wait_ge(pe_sc.sem, pe_sc.at(c - 1))
                    act.activation(vk_t[:], M[1][:], ACT.Identity, bias=bcol[:, CBVK:CBVK + 1]).then_inc(vk_s.sem, 1)
                    act.wait_ge(pe_lk.sem, pe_lk.at(c))
                    act.activation(lk_t[:], M[0][:], ACT.Identity, bias=bcol[:, CBLK:CBLK + 1]).then_inc(lk_s.sem, 1)
                if exists(b):
                    relus(b, 3)
                    relus(b, 4)
                if exists(c):
                    act.wait_ge(sub1.sem, sub1.at(c))
                    act.activation(sc_sb[:], sc_sb[:], ACT.Exp, scale=D ** -0.5).then_inc(exp1.sem, 1)
                    act.wait_ge(pe_bdt.sem, pe_bdt.at(c))
                    if exists(c - 1):
                        act.wait_ge(pe_att.sem, pe_att.at(c - 1))
                    act.activation(blockdiag_t[:, :, :].rearrange("p j n -> p (j n)"), M[1][:], ACT.Copy).then_inc(bdt_s.sem, 1)
                if exists(b):
                    relus(b, 5)
                if exists(a):
                    exp_heads(a, 0)
                if exists(b):
                    relus(b, 6)
                    relus(b, 7)
                if exists(c):
                    if exists(c - 1):
                        act.wait_ge(pe_xt[3].sem, pe_xt[3].at(c - 1))
                    normed(3, x3, c)
                    if exists(c + 2):
                        act.wait_ge(pe_q.sem, pe_q.at(c + 2))
                    high(M[1], xt_hi[3], pe_xt[3], hi_xt[3], c)
                    act.wait_ge(lsub.sem, lsub.at(c))
                    act.activation(lg[:], lg[:], ACT.Exp).then_inc(lexp.sem, 1)
                    tanhs(c, 0)
                    tanhs(c, 1)
                if exists(a):
                    exp_heads(a, 1)
                if exists(c):
                    for u in (2, 3, 4):
                        tanhs(c, u)
                if exists(a):
                    act.wait_ge(pe_kv.sem, pe_kv.at(a))
                    high(M[0], ot_hi, pe_ot, hi_o, a)
                if exists(c):
                    for u in (5, 6):
                        tanhs(c, u)
                if exists(b):
                    if exists(b - 1):
                        act.wait_ge(pe_xt[2].sem, pe_xt[2].at(b - 1))
                    normed(2, x2, b)
                if exists(c):
                    for u in (7, 8):
                        tanhs(c, u)
                if exists(a):
                    if exists(a - 1):
                        act.wait_ge(pe_xt[1].sem, pe_xt[1].at(a - 1))
                    if exists(a - 1):
                        act.wait_ge(sel_s.sem, sel_s.at(a - 1))
                    normed(1, x1, a)
                if exists(c):
                    tanhs(c, 9)
                    act.wait_ge(pe_f.sem, pe_f.at(c))
                    act.wait_ge(hu_s.sem, hu_s.at(c))
                    act.activation(y1_sb[:], Y[0][:], ACT.Copy).then_inc(y1_s.sem, 1)
                if exists(i + 2):
                    if exists(i + 1):
                        act.wait_ge(pe_xt[0].sem, pe_xt[0].at(i + 1))
                    normed(0, x0, i + 2)
                if is_step(i, -2):
                    weights()
                if exists(a):
                    if exists(a - 1):
                        act.wait_ge(pe_z.sem, pe_z.at(a - 1))
                    high(M[1], xt_hi[1], pe_xt[1], hi_xt[1], a)
                    for e in range(E0):
                        act.wait_ge(pe_mask.sem, pe_mask.at(a, e + 1))
                        if exists(a - 1):
                            act.wait_ge(term_s.sem, term_s.at(a - 1, e + 1))
                        act.activation(masks[:, e, :], Z[e % 4][:], ACT.Copy).then_inc(mask_s.sem, 1)

            act.wait_ge(s_cols, 16)
            run(act, body)

        @block.vector
        def _(dve):
            def consts():
                def step(ins):
                    ins.then_inc(s_dve0, 1)

                dve.wait_ge(s_pool, POOL_CONSTS)
                step(dve.tensor_copy(ident_r[:], ident[:]))
                step(dve.tensor_copy(ident_b[:], ident[:]))
                step(dve.tensor_copy(thr[:], thr_i[:]))
                step(dve.tensor_copy(modv[:], mod_i[:]))
                dve.wait_ge(s_act0, 1)
                dve.wait_ge(s_rows, 16)
                step(dve.tensor_scalar(gbo[:], brow[:, BO:BO + D], tg[:, 0:1], None, ALU.mult))
                step(dve.tensor_scalar(tgh[:], tg[:, 2:3], 0.5, None, ALU.mult))
                dve.wait_ge(s_act0, 2)
                step(dve.tensor_tensor(out=ws_lo[:, 0:WG], in0=ws_raw, in1=ws_hi[:, 0:WG].bitcast(F32), op=ALU.subtract))
                step(dve.tensor_tensor(out=ws_lo[:, WG:WSMALL], in0=wg_raw[:], in1=ws_hi[:, WG:WSMALL].bitcast(F32), op=ALU.subtract))
                dve.wait_ge(s_act0, 3)
                step(dve.tensor_tensor(out=w1_lo[:], in0=w1_raw,
                                       in1=w1_hi[:].bitcast(F32), op=ALU.subtract))
                dve.wait_ge(s_act0, 4)
                for raw, ns in zip(w13_raw, (slice(0, FJ * CH), slice(FJ * CH, UNITS * 2 * P))):
                    step(dve.tensor_tensor(out=w13_lo[:, ns], in0=raw, in1=w13_hi[:, ns].bitcast(F32), op=ALU.subtract))
                dve.wait_ge(s_dve0, DVE_CONSTS)

            def norm_stats(k, src, c):
                for j in range(TILES):
                    last = dve.bn_stats(stats[k][:, j, :], src[:, j, :])
                last.then_inc(ln_stats[k].sem, 1)
                dve.wait_ge(ln_stats[k].sem, ln_stats[k].at(c, 1))
                even, odd = stats[k][:, :, 1:3], stats[k][:, :, 4:6]
                dve.tensor_tensor(out=dmean[k][:], in0=even[:, :, 0], in1=odd[:, :, 0], op=ALU.subtract)
                dve.tensor_tensor(out=msum[k][:], in0=even, in1=odd, op=ALU.add).then_inc(ln_stats[k].sem, 1)
                dve.wait_ge(ln_stats[k].sem, ln_stats[k].at(c, 2))
                if exists(c - 1):
                    dve.wait_ge(ln_rstd[k].sem, ln_rstd[k].at(c - 1))
                dve.scalar_tensor_tensor(out=dmean[k][:], in0=dmean[k][:], scalar=0.25, in1=dmean[k][:], op0=ALU.mult, op1=ALU.mult)
                dve.tensor_scalar(nmean[k][:], msum[k][:, :, 0], -0.5, None, ALU.mult)
                dve.tensor_scalar(var[k][:], msum[k][:, :, 1], 1.0 / D, EPS, ALU.mult, ALU.add).then_inc(ln_stats[k].sem, 1)
                dve.wait_ge(ln_stats[k].sem, ln_stats[k].at(c, 3))
                dve.tensor_tensor(out=ve[k][:], in0=dmean[k][:], in1=var[k][:], op=ALU.add).then_inc(ln_stats[k].sem, 1)

            def low(bank_, hi, lo, hi_done, done, c):
                dve.wait_ge(hi_done.sem, hi_done.at(c))
                dve.tensor_tensor(out=lo[:], in0=bank_[:], in1=hi[:].bitcast(F32), op=ALU.subtract).then_inc(done.sem, 1)

            def expert_out(b, e):
                dve.wait_ge(pe_y.sem, pe_y.at(b, e + 1))
                if e == 0:
                    dve.wait_ge(mask_s.sem, mask_s.at(b))
                if e >= 2:
                    dve.wait_ge(acc_s.sem, acc_s.at(b, e - 1 if e > 2 else 1))
                else:
                    if exists(b - 1):
                        dve.wait_ge(acc_s.sem, acc_s.at(b - 1))
                dve.scalar_tensor_tensor(out=y_term[:, e % 2, :], in0=Y[e % 2][:], scalar=bcol[:, CB2 + e:CB2 + e + 1],
                                         in1=masks[:, e, :], op0=ALU.add, op1=ALU.mult).then_inc(term_s.sem, 1)

            def head_scores(a, t):
                dve.wait_ge(pool_qk.sem, pool_qk.at(a, t + 1))
                if t == 0:
                    if exists(a - 1):
                        dve.wait_ge(pool_av.sem, pool_av.at(a - 1))
                dve.tensor_reduce(out=s0[:, t, :, :].rearrange("p h e -> p (h e)"),
                                  in_=prod[:, t % 2, :].rearrange("p (g d) -> p g d", d=HD),
                                  axis=X, op=ALU.add).then_inc(score0.sem, 1)

            def head_max(a, pair):
                ts = slice(2 * pair, 2 * pair + 2)
                dve.wait_ge(score0.sem, score0.at(a, 2 * pair + 2))
                dve.tensor_reduce(out=mx0[:, ts, :], in_=s0[:, ts, :, :], axis=X, op=ALU.max).then_inc(sub0.sem, 1)
                dve.wait_ge(sub0.sem, sub0.at(a, 2 * pair + 1))
                s = s0[:, ts, :, :].rearrange("p t h e -> p (t h) e")
                m = mx0[:, ts, :].rearrange("p t h -> p (t h)")
                dve.tensor_tensor(out=s, in0=s, in1=m.unsqueeze(2).broadcast_to([P, 2 * HEADS, HEADS]),
                                  op=ALU.subtract).then_inc(sub0.sem, 1)

            def head_sum(a, pair):
                ts = slice(2 * pair, 2 * pair + 2)
                dve.wait_ge(exp0.sem, exp0.at(a, pair + 1))
                dve.tensor_reduce(out=sum0[:, ts, :], in_=s0[:, ts, :, :], axis=X, op=ALU.add).then_inc(rec0_s.sem, 1)
                dve.wait_ge(rec0_s.sem, rec0_s.at(a, 2 * pair + 1))
                dve.reciprocal(rec0[:, ts, :], sum0[:, ts, :]).then_inc(rec0_s.sem, 1)

            def head_out(a, t):
                dve.wait_ge(pool_av.sem, pool_av.at(a, t + 1))
                if t == 0:
                    dve.wait_ge(pool_qk.sem, pool_qk.at(a))
                dve.tensor_reduce(out=o_sb[:, t, :], in_=prod[:, t % 2, :].rearrange("p (g e) -> p g e", e=HEADS),
                                  axis=X, op=ALU.add).then_inc(av_sum.sem, 1)

            def head_scale(a, pair):
                ts = slice(2 * pair, 2 * pair + 2)
                dve.wait_ge(av_sum.sem, av_sum.at(a, 2 * pair + 2))
                dve.wait_ge(rec0_s.sem, rec0_s.at(a, 2 * pair + 2))
                o = o_sb[:, ts, :].rearrange("p t (h d) -> p (t h) d", h=HEADS)
                r = rec0[:, ts, :].rearrange("p t h -> p (t h)")
                dve.tensor_tensor(out=o, in0=o, in1=r.unsqueeze(2).broadcast_to([P, 2 * HEADS, HD]),
                                  op=ALU.mult).then_inc(o_ready.sem, 1)

            def biased(bank_, row, dst, pe, done, c):
                dve.wait_ge(pe.sem, pe.at(c))
                dve.tensor_tensor(out=dst[:], in0=tiles(bank_), in1=brow[:, row:row + D].unsqueeze(1).broadcast_to([P, TILES, D]),
                                  op=ALU.add).then_inc(done.sem, 1)

            def unit_open(c, u):
                dve.wait_ge(tanh_s.sem, tanh_s.at(c, u + 1))
                if u > 0:
                    dve.wait_ge(hu_s.sem, hu_s.at(c, u))
                else:
                    if exists(c - 1):
                        dve.wait_ge(pe_out.sem, pe_out.at(c - 1))
                dve.scalar_tensor_tensor(out=pr[:], in0=th[:, u % 2, :], scalar=1.0, in1=Z[2 * (u % 2)][:],
                                         op0=ALU.add, op1=ALU.mult).then_inc(pr_s.sem, 1)
                dve.wait_ge(pr_s.sem, pr_s.at(c, u + 1))
                if u >= 2:
                    dve.wait_ge(pe_f.sem, pe_f.at(c, u - 1))
                else:
                    if exists(c - 1):
                        dve.wait_ge(pe_f.sem, pe_f.at(c - 1, UNITS - 1 + u))
                dve.scalar_tensor_tensor(out=hu[:, u % 2, :], in0=pr[:], scalar=0.5, in1=Z[2 * (u % 2) + 1][:],
                                         op0=ALU.mult, op1=ALU.mult).then_inc(hu_s.sem, 1)

            def unit_gate(c, u):
                dve.wait_ge(hu_s.sem, hu_s.at(c, u + 1))
                dve.wait_ge(pe_g.sem, pe_g.at(c, u + 1))
                dve.tensor_tensor(out=hu[:, u % 2, :], in0=hu[:, u % 2, :], in1=Y[1][:], op=ALU.mult).then_inc(hg_s.sem, 1)

            def unit(c, u):
                unit_open(c, u)
                if u < E1:
                    unit_gate(c, u)

            def select_experts(a):
                s = sel_s.sem
                dve.wait_ge(ln_done[1].sem, ln_done[1].at(a))
                dve.tensor_tensor(out=hsum[:], in0=xn[1][:, :, 0], in1=xn[1][:, :, 1], op=ALU.add).then_inc(s, 1)
                dve.wait_ge(sel_s.sem, sel_s.at(a, 1))
                hs = hsum[:].unsqueeze(2).broadcast_to([P, TILES, TRUNC_MAX])
                th_ = thr[:].unsqueeze(1).broadcast_to([P, TILES, TRUNC_MAX])
                dve.tensor_tensor(out=hge[:], in0=hs, in1=th_, op=ALU.is_ge).then_inc(s, 1)
                dve.scalar_tensor_tensor(out=hle[:], in0=hs, scalar=-1.0, in1=th_, op0=ALU.mult, op1=ALU.is_ge).then_inc(s, 1)
                dve.wait_ge(sel_s.sem, sel_s.at(a, 3))
                dve.tensor_tensor(out=hge[:], in0=hge[:], in1=hle[:], op=ALU.subtract).then_inc(s, 1)
                dve.wait_ge(sel_s.sem, sel_s.at(a, 4))
                dve.tensor_reduce(out=htr[:], in_=hge[:], axis=X, op=ALU.add).then_inc(s, 1)
                dve.wait_ge(sel_s.sem, sel_s.at(a, 5))
                dve.tensor_tensor(out=heq[:], in0=htr[:].unsqueeze(2).unsqueeze(3).broadcast_to([P, TILES, E0, MOD_K]),
                                  in1=modv[:].unsqueeze(1).broadcast_to([P, TILES, E0, MOD_K]), op=ALU.is_equal).then_inc(s, 1)
                dve.wait_ge(sel_s.sem, sel_s.at(a, 6))
                dve.tensor_reduce(out=onehot[:], in_=heq[:], axis=X, op=ALU.add).then_inc(s, 1)
                dve.wait_ge(sel_s.sem, sel_s.at(a, 7))
                if exists(a - 1):
                    dve.wait_ge(pe_mask.sem, pe_mask.at(a - 1))
                dve.tensor_tensor(out=sel0[:, :, 1:E0], in0=onehot[:, :, 1:E0], in1=onehot[:, :, 0:E0 - 1], op=ALU.add).then_inc(s, 1)
                dve.tensor_tensor(out=sel0[:, :, 0], in0=onehot[:, :, 0], in1=onehot[:, :, E0 - 1], op=ALU.add).then_inc(s, 1)

            def logits_max(c):
                dve.wait_ge(pe_lg.sem, pe_lg.at(c))
                l = M[0][:, 0:TILES * E1].rearrange("p (j e) -> p j e", e=E1)
                dve.tensor_reduce(out=lmx[:], in_=l, axis=X, op=ALU.max).then_inc(lsub.sem, 1)
                dve.wait_ge(lsub.sem, lsub.at(c, 1))
                dve.tensor_tensor(out=lg[:], in0=l, in1=lmx[:].unsqueeze(2).broadcast_to([P, TILES, E1]),
                                  op=ALU.subtract).then_inc(lsub.sem, 1)

            def route_tokens(c):
                r = route.sem
                dve.wait_ge(lexp.sem, lexp.at(c))
                dve.tensor_reduce(out=lsum[:], in_=lg[:], axis=X, op=ALU.add).then_inc(r, 1)
                dve.wait_ge(route.sem, route.at(c, 1))
                dve.reciprocal(lrec[:], lsum[:]).then_inc(r, 1)
                dve.wait_ge(route.sem, route.at(c, 2))
                dve.tensor_tensor(out=sc1[:], in0=lg[:], in1=lrec[:].unsqueeze(2).broadcast_to([P, TILES, E1]), op=ALU.mult).then_inc(r, 1)
                dve.wait_ge(route.sem, route.at(c, 3))
                dve.tensor_tensor(out=bs1[:], in0=sc1[:], in1=brow[:, BG:BG + E1].unsqueeze(1).broadcast_to([P, TILES, E1]),
                                  op=ALU.add).then_inc(r, 1)
                dve.wait_ge(route.sem, route.at(c, 4))
                own = bs1[:].unsqueeze(3).broadcast_to([P, TILES, E1, E1])
                other = bs1[:].unsqueeze(2).broadcast_to([P, TILES, E1, E1])
                dve.tensor_tensor(out=cmp_gt[:], in0=other, in1=own, op=ALU.is_gt).then_inc(r, 1)
                dve.tensor_tensor(out=cmp_eq[:], in0=other, in1=own, op=ALU.is_equal).then_inc(r, 1)
                dve.wait_ge(route.sem, route.at(c, 6))
                dve.tensor_tensor(out=cmp_eq[:], in0=cmp_eq[:], in1=before[:].unsqueeze(1).broadcast_to([P, TILES, E1, E1]),
                                  op=ALU.mult).then_inc(r, 1)
                dve.wait_ge(route.sem, route.at(c, 7))
                dve.tensor_tensor(out=cmp_gt[:], in0=cmp_gt[:], in1=cmp_eq[:], op=ALU.add).then_inc(r, 1)
                dve.wait_ge(route.sem, route.at(c, 8))
                dve.tensor_reduce(out=rank[:], in_=cmp_gt[:], axis=X, op=ALU.add).then_inc(r, 1)
                dve.wait_ge(route.sem, route.at(c, 9))
                dve.scalar_tensor_tensor(out=gate[:], in0=rank[:], scalar=2.0, in1=sc1[:], op0=ALU.is_lt, op1=ALU.mult).then_inc(r, 1)
                dve.wait_ge(route.sem, route.at(c, 10))
                if exists(c - 1):
                    dve.wait_ge(pe_g.sem, pe_g.at(c - 1))
                dve.tensor_copy(g_hi[:], gate[:]).then_inc(r, 1)
                dve.wait_ge(route.sem, route.at(c, 11))
                dve.tensor_tensor(out=g_lo[:], in0=gate[:], in1=g_hi[:].bitcast(F32), op=ALU.subtract).then_inc(r, 1)

            def residual(bank_, gate_col, prev, dst, pe, done, c):
                dve.wait_ge(pe.sem, pe.at(c))
                dve.scalar_tensor_tensor(out=dst[:, :, :].rearrange("p j d -> p (j d)"), in0=bank_[:], scalar=gate_col,
                                         in1=prev[:, :, :].rearrange("p j d -> p (j d)"),
                                         op0=ALU.mult, op1=ALU.add).then_inc(done.sem, 1)

            def body(i):
                a, b, c = i + 1, i, i - 1
                A, B, C = exists(a), exists(b), exists(c)
                if A:
                    if exists(a - 1):
                        dve.wait_ge(pe_wo.sem, pe_wo.at(a - 1))
                    low(M[0], ctx_hi, ctx_lo, hi_ctx, lo_ctx, a)
                    if exists(a - 3):
                        dve.wait_ge(pe_ab.sem, pe_ab.at(a - 3))
                    low(M[1], xt_hi[0], xt_lo[0], hi_xt[0], lo_xt[0], a)
                if B:
                    expert_out(b, 0)
                if A:
                    dve.wait_ge(pe_q.sem, pe_q.at(a))
                    if exists(a - 1):
                        dve.wait_ge(pe_ot.sem, pe_ot.at(a - 1))
                    dve.tensor_tensor(out=q_sb[:], in0=tiles(M[0]), in1=brow[:, BQ:BQ + D].unsqueeze(1).broadcast_to([P, TILES, D]),
                                      op=ALU.add).then_inc(qkv.sem, 1)
                    if exists(a - 1):
                        dve.wait_ge(pool_av.sem, pool_av.at(a - 1))
                    for half in range(2):
                        dve.wait_ge(pe_kv.sem, pe_kv.at(a, half + 1))
                        dve.tensor_tensor(out=kv_sb[:, 2 * half:2 * half + 2, :],
                                          in0=M[1 - half][:, :].rearrange("p (j d) -> p j d", j=2),
                                          in1=brow[:, BKV:BKV + 2 * D].unsqueeze(1).broadcast_to([P, 2, 2 * D]),
                                          op=ALU.add).then_inc(qkv.sem, 1)
                if C:
                    if exists(c - 1):
                        dve.wait_ge(pe_vv.sem, pe_vv.at(c - 1))
                    low(M[1], xt_hi[2], xt_lo[2], hi_xt[2], lo_xt[2], c)
                    if exists(c - 1):
                        dve.wait_ge(pe_lv.sem, pe_lv.at(c - 1))
                    low(M[0], ctx2_hi, ctx2_lo, hi_ctx2, lo_ctx2, c)
                if B:
                    expert_out(b, 1)
                if C:
                    if exists(c - 1):
                        dve.wait_ge(pe_val.sem, pe_val.at(c - 1))
                    biased(M[1], BVV, vv_sb, pe_vv, vv_s, c)
                    if exists(c - 1):
                        dve.wait_ge(pe_att.sem, pe_att.at(c - 1))
                    biased(M[0], BLV, lv_sb, pe_lv, lv_s, c)
                if A:
                    head_scores(a, 0)
                if B:
                    expert_out(b, 2)
                if A:
                    head_scores(a, 1)
                    head_max(a, 0)
                if B:
                    expert_out(b, 3)
                if C:
                    dve.wait_ge(pe_sc.sem, pe_sc.at(c))
                    s = M[1][:, 0:TILES * SEQ].rearrange("p (j n) -> p j n", n=SEQ)
                    dve.tensor_reduce(out=mx1[:], in_=s, axis=X, op=ALU.max).then_inc(sub1.sem, 1)
                    dve.wait_ge(sub1.sem, sub1.at(c, 1))
                    dve.tensor_tensor(out=sc_sb[:], in0=s, in1=mx1[:].unsqueeze(2).broadcast_to([P, TILES, SEQ]),
                                      op=ALU.subtract).then_inc(sub1.sem, 1)
                if A:
                    head_scores(a, 2)
                if C:
                    dve.wait_ge(exp1.sem, exp1.at(c))
                    dve.tensor_reduce(out=sum1[:], in_=sc_sb[:], axis=X, op=ALU.add).then_inc(bd_s.sem, 1)
                    dve.wait_ge(bd_s.sem, bd_s.at(c, 1))
                    dve.reciprocal(rec1[:], sum1[:]).then_inc(bd_s.sem, 1)
                    dve.wait_ge(bd_s.sem, bd_s.at(c, 2))
                    if exists(c - 1):
                        dve.wait_ge(pe_bdt.sem, pe_bdt.at(c - 1))
                    for h in range(2):
                        ps = slice(h * SEQ, (h + 1) * SEQ)
                        dve.tensor_tensor(out=blockdiag[ps, :, h * SEQ:(h + 1) * SEQ], in0=sc_sb[ps, :, :],
                                          in1=rec1[ps, :].unsqueeze(2).broadcast_to([SEQ, TILES, SEQ]),
                                          op=ALU.mult).then_inc(bd_s.sem, 1)
                if B:
                    expert_out(b, 4)
                if C:
                    dve.wait_ge(pe_val.sem, pe_val.at(c))
                    dve.wait_ge(lv_s.sem, lv_s.at(c))
                    dve.tensor_tensor(out=u_sb[:], in0=tiles(M[0]), in1=lv_sb[:], op=ALU.add).then_inc(u_s.sem, 1)
                if A:
                    head_scores(a, 3)
                    head_max(a, 1)
                if B:
                    expert_out(b, 5)
                if C:
                    if exists(c - 1):
                        dve.wait_ge(st_out.sem, st_out.at(c - 1))
                    residual(M[0], tg[:, 1:2], x2, x3, pe_att, x3_s, c)
                    dve.wait_ge(x3_s.sem, x3_s.at(c))
                    norm_stats(3, x3, c)
                if A:
                    head_sum(a, 0)
                    head_out(a, 0)
                if B:
                    expert_out(b, 6)
                if A:
                    head_out(a, 1)
                    head_scale(a, 0)
                if B:
                    expert_out(b, 7)
                if C:
                    if exists(c + 2):
                        dve.wait_ge(pe_q.sem, pe_q.at(c + 2))
                    low(M[1], xt_hi[3], xt_lo[3], hi_xt[3], lo_xt[3], c)
                    logits_max(c)
                    unit_open(c, 0)
                    route_tokens(c)
                if B:
                    if exists(c):
                        dve.wait_ge(x3_s.sem, x3_s.at(c))
                    dve.wait_ge(x1_s.sem, x1_s.at(b))
                    residual(M[1], tgh[:, 0:1], x1, x2, pe_yt, x2_s, b)
                if C:
                    unit_gate(c, 0)
                    unit(c, 1)
                if B:
                    dve.wait_ge(x2_s.sem, x2_s.at(b))
                    norm_stats(2, x2, b)
                if C:
                    unit(c, 2)
                if A:
                    head_sum(a, 1)
                if C:
                    unit(c, 3)
                if A:
                    head_out(a, 2)
                    head_out(a, 3)
                    head_scale(a, 1)
                if C:
                    unit(c, 4)
                if A:
                    dve.wait_ge(pe_kv.sem, pe_kv.at(a))
                    low(M[0], ot_hi, ot_lo, hi_o, lo_o, a)
                if C:
                    unit(c, 5)
                if A:
                    if exists(a - 1):
                        dve.wait_ge(x2_s.sem, x2_s.at(a - 1))
                    dve.wait_ge(pool_xp.sem, pool_xp.at(a))
                    residual(M[1], tg[:, 0:1], xp, x1, pe_wo, x1_s, a)
                    dve.wait_ge(x1_s.sem, x1_s.at(a))
                    norm_stats(1, x1, a)
                if C:
                    for u in (6, 7, 8):
                        unit(c, u)
                if A:
                    select_experts(a)
                if C:
                    unit(c, 9)
                if exists(i + 2):
                    dve.wait_ge(ld_x.sem, ld_x.at(i + 2))
                    norm_stats(0, x0, i + 2)
                if is_step(i, -2):
                    consts()
                if A:
                    if exists(a - 1):
                        dve.wait_ge(pe_z.sem, pe_z.at(a - 1))
                    low(M[1], xt_hi[1], xt_lo[1], hi_xt[1], lo_xt[1], a)
                if C:
                    dve.wait_ge(ln_done[3].sem, ln_done[3].at(c))
                    residual(M[0], tg[:, 3:4], x3, x3, pe_out, out_s, c)

            dve.wait_ge(s_rows, 16)
            dve.wait_ge(s_cols, 16)
            run(dve, body)

        @block.tensor
        def _(pe):
            def transposes(bank_, src):
                for j in range(TILES):
                    last = pe.transpose(bank_[:, j * P:(j + 1) * P], src[:, j, :], ident[:])
                return last

            def three(dst, l_hi, l_lo, r_hi, r_lo):
                pe.matmul(dst, l_hi, r_hi, start=True, stop=False)
                pe.matmul(dst, l_lo, r_hi, start=False, stop=False)
                return pe.matmul(dst, l_hi, r_lo, start=False, stop=True)

            def by_token(bank_, col, t_hi, t_lo, w, width, which=range(TILES)):
                for n, j in enumerate(which):
                    js = slice(j * P, (j + 1) * P)
                    last = three(bank_[:, n * width:(n + 1) * width], t_hi[:, js], t_lo[:, js],
                                 ws_hi[:, w:w + width], ws_lo[:, w:w + width])
                return last

            def by_width(bank_, w_hi, w_lo, w, t_hi, t_lo):
                return three(bank_[:], w_hi[:, w:w + P], w_lo[:, w:w + P], t_hi[:], t_lo[:])

            def ffn0(b, e):
                for j in range(FJ):
                    n = e * FJ + j
                    if e > 0:
                        pe.wait_ge(relu_s.sem, relu_s.at(b, n + 1 - FJ))
                    else:
                        if j == 0:
                            pe.wait_ge(hi_xt[1].sem, hi_xt[1].at(b))
                            pe.wait_ge(lo_xt[1].sem, lo_xt[1].at(b))
                        pe.wait_ge(mask_s.sem, mask_s.at(b, E0 - FJ + j + 1))
                    by_width(Z[j], w1_hi, w1_lo, n * P, xt_hi[1], xt_lo[1]).then_inc(pe_z.sem, 1)
                if e >= 2:
                    pe.wait_ge(term_s.sem, term_s.at(b, e - 1))
                elif e == 0:
                    if exists(b - 2):
                        pe.wait_ge(y1_s.sem, y1_s.at(b - 2))
                else:
                    if exists(b - 2):
                        pe.wait_ge(hg_s.sem, hg_s.at(b - 2))
                for j in range(FJ):
                    n = e * FJ + j
                    pe.wait_ge(relu_s.sem, relu_s.at(b, n + 1))
                    last = pe.matmul(Y[e % 2][:], w2_sb[:, n, :], hidden[:, j, :], start=(j == 0), stop=(j == FJ - 1))
                last.then_inc(pe_y.sem, 1)

            def unit_in(c, u):
                if u >= 2:
                    pe.wait_ge(hu_s.sem, hu_s.at(c, u - 1))
                else:
                    if exists(c + 1):
                        pe.wait_ge(relu_s.sem, relu_s.at(c + 1))
                    if exists(c + 1):
                        pe.wait_ge(mask_s.sem, mask_s.at(c + 1))
                if u == 0:
                    pe.wait_ge(hi_xt[3].sem, hi_xt[3].at(c))
                    pe.wait_ge(lo_xt[3].sem, lo_xt[3].at(c))
                z = 2 * (u % 2)
                by_width(Z[z], w13_hi, w13_lo, 2 * u * P, xt_hi[3], xt_lo[3])
                by_width(Z[z + 1], w13_hi, w13_lo, (2 * u + 1) * P, xt_hi[3], xt_lo[3]).then_inc(pe_ab.sem, 1)

            def gate_rows(c, u):
                if u > 0:
                    pe.wait_ge(hg_s.sem, hg_s.at(c, u))
                else:
                    pe.wait_ge(route.sem, route.at(c))
                    if exists(c + 1):
                        pe.wait_ge(term_s.sem, term_s.at(c + 1))
                for j in range(TILES):
                    js = slice(j * P, (j + 1) * P)
                    pe.matmul(Y[1][:, js], g_hi[:, j, u:u + 1].broadcast_to([P, P]), ident_r[:], start=True, stop=False)
                    last = pe.matmul(Y[1][:, js], g_lo[:, j, u:u + 1].broadcast_to([P, P]), ident_r[:], start=False, stop=True)
                last.then_inc(pe_g.sem, 1)

            def unit_out(c, u):
                if u == 0:
                    if exists(c + 1):
                        pe.wait_ge(term_s.sem, term_s.at(c + 1))
                    if exists(c - 1):
                        pe.wait_ge(y1_s.sem, y1_s.at(c - 1))
                if u < E1:
                    pe.wait_ge(hg_s.sem, hg_s.at(c, u + 1))
                else:
                    pe.wait_ge(hu_s.sem, hu_s.at(c, u + 1))
                pe.matmul(Y[0][:], w2u_sb[:, u, :], hu[:, u % 2, :], start=(u == 0), stop=(u == UNITS - 1)).then_inc(pe_f.sem, 1)

            def unit_step(c, u):
                if u + 2 < UNITS:
                    unit_in(c, u + 2)
                unit_out(c, u)
                if u + 1 < E1:
                    gate_rows(c, u + 1)

            def body(i):
                a, b, c = i + 1, i, i - 1
                A, B, C = exists(a), exists(b), exists(c)
                if B:
                    ffn0(b, 0)
                if is_step(i, -1):
                    pe.wait_ge(s_pool, POOL_CONSTS)
                    pe.wait_ge(s_dve0, DVE_CONSTS)
                    pe.wait_ge(s_act0, ACT_CONSTS)
                    pe.wait_ge(s_w2, 32)
                if exists(c - 1):
                    pe.wait_ge(out_s.sem, out_s.at(c - 1))
                if A:
                    pe.wait_ge(ld_ca.sem, ld_ca.at(a))
                    transposes(M[0], ctx_a).then_inc(pe_ctxt.sem, 1)
                    pe.wait_ge(ln_done[0].sem, ln_done[0].at(a))
                    if exists(a - 1):
                        pe.wait_ge(lo_xt[1].sem, lo_xt[1].at(a - 1))
                    transposes(M[1], xn[0]).then_inc(pe_xt[0].sem, 1)
                if B:
                    ffn0(b, 1)
                if A:
                    pe.wait_ge(hi_xt[0].sem, hi_xt[0].at(a))
                    pe.wait_ge(lo_xt[0].sem, lo_xt[0].at(a))
                    pe.wait_ge(lo_ctx.sem, lo_ctx.at(a))
                    by_token(M[0], 0, xt_hi[0], xt_lo[0], WQ, D).then_inc(pe_q.sem, 1)
                    by_token(M[1], 0, ctx_hi, ctx_lo, WKV, 2 * D, (0, 1)).then_inc(pe_kv.sem, 1)
                    pe.wait_ge(qkv.sem, qkv.at(a, 1))
                    by_token(M[0], 0, ctx_hi, ctx_lo, WKV, 2 * D, (2, 3)).then_inc(pe_kv.sem, 1)
                if C:
                    pe.wait_ge(ln_done[2].sem, ln_done[2].at(c))
                    if exists(a):
                        pe.wait_ge(qkv.sem, qkv.at(a, 2))
                    transposes(M[1], xn[2]).then_inc(pe_xt[2].sem, 1)
                    pe.wait_ge(ld_cc.sem, ld_cc.at(c))
                    if exists(a):
                        pe.wait_ge(qkv.sem, qkv.at(a, 3))
                    transposes(M[0], ctx_c).then_inc(pe_ctx2t.sem, 1)
                if B:
                    ffn0(b, 2)
                if C:
                    pe.wait_ge(lo_xt[2].sem, lo_xt[2].at(c))
                    by_width(M[1], ws_hi, ws_lo, WVK, xt_hi[2], xt_lo[2]).then_inc(pe_vk.sem, 1)
                    pe.wait_ge(lo_ctx2.sem, lo_ctx2.at(c))
                    by_width(M[0], ws_hi, ws_lo, WLK, ctx2_hi, ctx2_lo).then_inc(pe_lk.sem, 1)
                    pe.wait_ge(vk_s.sem, vk_s.at(c))
                    by_token(M[1], 0, xt_hi[2], xt_lo[2], WVV, D).then_inc(pe_vv.sem, 1)
                    pe.wait_ge(lk_s.sem, lk_s.at(c))
                    by_token(M[0], 0, ctx2_hi, ctx2_lo, WLV, D).then_inc(pe_lv.sem, 1)
                if B:
                    ffn0(b, 3)
                if C:
                    pe.wait_ge(vv_s.sem, vv_s.at(c))
                    for j in range(TILES):
                        for h in range(2):
                            ts = slice(j * P + h * SEQ, j * P + (h + 1) * SEQ)
                            last = pe.matmul(M[1][h * SEQ:(h + 1) * SEQ, j * SEQ:(j + 1) * SEQ], vk_t[:, ts], lk_t[:, ts],
                                             start=True, stop=True)
                    last.then_inc(pe_sc.sem, 1)
                if B:
                    ffn0(b, 4)
                if C:
                    pe.wait_ge(bd_s.sem, bd_s.at(c))
                    pe.wait_ge(lv_s.sem, lv_s.at(c))
                    for j in range(TILES):
                        last = pe.matmul(M[0][:, j * P:(j + 1) * P], blockdiag[:, j, :], vv_sb[:, j, :], start=True, stop=True)
                    last.then_inc(pe_val.sem, 1)
                    transposes(M[1], blockdiag).then_inc(pe_bdt.sem, 1)
                if B:
                    ffn0(b, 5)
                if C:
                    pe.wait_ge(u_s.sem, u_s.at(c))
                    pe.wait_ge(bdt_s.sem, bdt_s.at(c))
                    for j in range(TILES):
                        last = pe.matmul(M[0][:, j * P:(j + 1) * P], blockdiag_t[:, j, :], u_sb[:, j, :], start=True, stop=True)
                    last.then_inc(pe_att.sem, 1)
                if B:
                    ffn0(b, 6)
                    ffn0(b, 7)
                if C:
                    pe.wait_ge(ln_done[3].sem, ln_done[3].at(c))
                    transposes(M[1], xn[3]).then_inc(pe_xt[3].sem, 1)
                    pe.wait_ge(hi_xt[3].sem, hi_xt[3].at(c))
                    pe.wait_ge(lo_xt[3].sem, lo_xt[3].at(c))
                    pe.wait_ge(x3_s.sem, x3_s.at(c))
                    by_token(M[0], 0, xt_hi[3], xt_lo[3], WG, E1).then_inc(pe_lg.sem, 1)
                    unit_in(c, 0)
                    unit_in(c, 1)
                if B:
                    pe.wait_ge(acc_s.sem, acc_s.at(b))
                    if exists(a):
                        pe.wait_ge(qkv.sem, qkv.at(a, 2))
                    for j in range(TILES):
                        last = pe.transpose(M[1][:, j * P:(j + 1) * P], y_acc[:, j * P:(j + 1) * P], ident[:])
                    last.then_inc(pe_yt.sem, 1)
                if C:
                    gate_rows(c, 0)
                    for u in range(4):
                        unit_step(c, u)
                if A:
                    pe.wait_ge(o_ready.sem, o_ready.at(a))
                    if exists(c):
                        pe.wait_ge(lsub.sem, lsub.at(c))
                    transposes(M[0], o_sb).then_inc(pe_ot.sem, 1)
                if C:
                    unit_step(c, 4)
                if A:
                    pe.wait_ge(lo_o.sem, lo_o.at(a))
                    if exists(b):
                        pe.wait_ge(x2_s.sem, x2_s.at(b))
                    by_token(M[1], 0, ot_hi, ot_lo, WO, D).then_inc(pe_wo.sem, 1)
                if C:
                    for u in range(5, UNITS):
                        unit_step(c, u)
                    pe.wait_ge(y1_s.sem, y1_s.at(c))
                    if exists(a):
                        pe.wait_ge(lo_o.sem, lo_o.at(a))
                    for j in range(TILES):
                        last = pe.transpose(M[0][:, j * P:(j + 1) * P], y1_sb[:, j * P:(j + 1) * P], ident[:])
                    last.then_inc(pe_out.sem, 1)
                if A:
                    pe.wait_ge(ln_done[1].sem, ln_done[1].at(a))
                    transposes(M[1], xn[1]).then_inc(pe_xt[1].sem, 1)
                    pe.wait_ge(sel_s.sem, sel_s.at(a))
                    for e in range(E0):
                        if e < FJ:
                            if exists(a - 1):
                                pe.wait_ge(relu_s.sem, relu_s.at(a - 1))
                            if exists(c):
                                pe.wait_ge(hu_s.sem, hu_s.at(c))
                        else:
                            pe.wait_ge(mask_s.sem, mask_s.at(a, e - FJ + 1))
                        for j in range(TILES):
                            last = pe.matmul(Z[e % 4][:, j * P:(j + 1) * P], sel0[:, j, e:e + 1].broadcast_to([P, P]), ident_b[:],
                                             start=True, stop=True)
                        last.then_inc(pe_mask.sem, 1)

            run(pe, body)


def kernel(x, ctx_1024, g_xattn, g_ffn, L0_xattn_Wq, L0_xattn_bq, L0_xattn_Wk, L0_xattn_bk, L0_xattn_Wv, L0_xattn_bv,
           L0_xattn_Wo, L0_xattn_bo, L0_ffn_W1, L0_ffn_b1, L0_ffn_W2, L0_ffn_b2, L1_xattn_W_vk, L1_xattn_b_vk,
           L1_xattn_W_lk, L1_xattn_b_lk, L1_xattn_W_vv, L1_xattn_b_vv, L1_xattn_W_lv, L1_xattn_b_lv, L1_ffn_gate_w,
           L1_ffn_gate_bias, L1_ffn_w1, L1_ffn_w3, L1_ffn_w2, L1_ffn_sw1, L1_ffn_sw3, L1_ffn_sw2):
    import concourse.bacc as bacc
    import numpy as np
    from concourse.bass_utils import run_bass_kernel_spmd

    shape = np.asarray(x).shape
    a = {k: np.asarray(v) for k, v in dict(locals()).items() if k[0] == "L" or k in ("g_xattn", "g_ffn")}

    def width_first(w):
        return np.ascontiguousarray(w.reshape(HEADS, HD, -1).swapaxes(0, 1).reshape(w.shape))

    w_small = np.concatenate([
        a["L0_xattn_Wq"].T, a["L0_xattn_Wk"].T, width_first(a["L0_xattn_Wv"]).T, a["L0_xattn_Wo"].T,
        a["L1_xattn_W_vk"].T, a["L1_xattn_W_lk"].T, a["L1_xattn_W_vv"].T, a["L1_xattn_W_lv"].T, a["L1_ffn_gate_w"].T], axis=1)
    w1 = a["L0_ffn_W1"].transpose(1, 0, 2).reshape(P, -1)
    w2 = a["L0_ffn_W2"].reshape(E0, FJ, P, D).transpose(2, 0, 1, 3).reshape(P, -1)
    up = np.concatenate([a["L1_ffn_w1"], a["L1_ffn_sw1"].reshape(2, P, D)], axis=0)
    gt = np.concatenate([a["L1_ffn_w3"], a["L1_ffn_sw3"].reshape(2, P, D)], axis=0)
    w13 = np.stack([up, gt], axis=1).transpose(3, 0, 1, 2).reshape(P, -1)
    down = np.concatenate([a["L1_ffn_w2"], a["L1_ffn_sw2"].reshape(D, 2, P).transpose(1, 0, 2)], axis=0)
    w2u = down.transpose(2, 0, 1).reshape(P, -1)
    rows = np.concatenate([a["L0_xattn_bq"], a["L0_xattn_bk"], width_first(a["L0_xattn_bv"]), a["L0_xattn_bo"],
                           a["L1_xattn_b_vv"], a["L1_xattn_b_lv"], a["L1_ffn_gate_bias"]])
    cols = np.concatenate([a["L0_ffn_b1"].reshape(E0 * FJ, P), a["L0_ffn_b2"],
                           a["L1_xattn_b_vk"].reshape(1, P), a["L1_xattn_b_lk"].reshape(1, P)], axis=0).T
    arrays = {
        "x": np.asarray(x).reshape(-1, D), "ctx": np.asarray(ctx_1024).reshape(-1, D), "g_x": a["g_xattn"], "g_f": a["g_ffn"],
        "w_small": w_small, "w1": w1, "w2": w2, "w13": w13, "w2u": w2u, "rows": rows, "cols": cols,
    }
    arrays = {f"in_{k}": np.ascontiguousarray(v) for k, v in arrays.items()}
    nc = bacc.Bacc("TRN2", target_bir_lowering=False, num_devices=1)
    ins = [nc.dram_tensor(k, v.shape, mybir.dt.from_np(v.dtype), kind="ExternalInput").ap() for k, v in arrays.items()]
    out = nc.dram_tensor("out_0", arrays["in_x"].shape, F32, kind="ExternalOutput").ap()
    build(nc, *ins, out)
    r = run_bass_kernel_spmd(nc, [arrays], core_ids=[0])
    return r.results[0]["out_0"].reshape(shape)
```

```python
from contextlib import ExitStack

import concourse.bass as bass
from concourse import mybir

F32 = mybir.dt.float32
F32R = mybir.dt.float32r
I32 = mybir.dt.int32
ALU = mybir.AluOpType
ACT = mybir.ActivationFunctionType
X = mybir.AxisListType.X

P = 128
D = 128
TILES = 4
CH = TILES * P
SEQ = 64
HEADS, HD = 16, 8
HH = HEADS * HEADS
E0, FJ = 8, 4
E1, SHARED = 8, 2
UNITS = SHARED + E1
TRUNC_MAX = 17
MOD_K = 5
EPS = 1e-5

WQ, WKV, WO, WVK, WLK, WVV, WLV, WG = 0, 128, 384, 512, 640, 768, 896, 1024
WSMALL = WG + 8
BQ, BKV, BO, BVV, BLV, BG = 0, 128, 384, 512, 640, 768
BROWS = BG + 8
CB1, CBVK, CBLK = 0, 32, 33
BCOLS = 34
BIAS_AFTER = 3


def acc_step(e):
    return e + 1 if e <= BIAS_AFTER else e + 2


class Signal:

    def __init__(self, sem, per):
        self.sem, self.per = sem, per

    def at(self, c, k=None):
        return c * self.per + (self.per if k is None else k)


def build(nc, x, ctx_in, g_x, g_f, w_small, w1, w2, w13, w2u, bias_rows, bias_cols, bias2, out):
    NT = x.shape[0]
    NC = NT // CH
    x_v = x.rearrange("(c j p) d -> p c j d", j=TILES, p=P)
    ctx_v = ctx_in.rearrange("(c j p) d -> p c j d", j=TILES, p=P)
    out_v = out.rearrange("(c j p) d -> p c j d", j=TILES, p=P)

    with ExitStack() as stack:
        def sb(name, shape, dt=F32):
            return stack.enter_context(nc.sbuf_tensor(name, shape, dt))

        def bank(name):
            return stack.enter_context(nc.psum_tensor(name, [P, CH], F32))

        def sem(name):
            return stack.enter_context(nc.semaphore(name))

        def signal(name, per=1):
            return Signal(sem(name), per)

        ws = sb("ws", [P, WSMALL])
        wg_hi, wg_lo = sb("wg_hi", [P, E1], F32R), sb("wg_lo", [P, E1], F32R)
        w1_hi, w1_lo = sb("w1_hi", [P, E0 * FJ * P], F32R), sb("w1_lo", [P, E0 * FJ * P], F32R)
        w13_hi, w13_lo = sb("w13_hi", [P, UNITS * 2 * P], F32R), sb("w13_lo", [P, UNITS * 2 * P], F32R)
        w2_sb = sb("w2_sb", [P, E0 * FJ, D])
        w2u_sb = sb("w2u_sb", [P, UNITS, D])
        b2_sb = sb("b2_sb", [E0, D])
        brow = sb("brow", [P, BROWS])
        bcol = sb("bcol", [P, BCOLS])
        gates_raw, tg = sb("gates_raw", [P, 4]), sb("tg", [P, 4])
        tgh = sb("tgh", [P, 1])
        gbo = sb("gbo", [P, D])
        ident = sb("ident", [P, P])
        thr_i, thr = sb("thr_i", [P, TRUNC_MAX], I32), sb("thr", [P, TRUNC_MAX])
        mod_i, modv = sb("mod_i", [P, E0, MOD_K], I32), sb("modv", [P, E0, MOD_K])
        before = sb("before", [P, E1, E1])
        neghalf = sb("neghalf", [P, TILES])

        x0, ctx_a, ctx_c = (sb(n, [P, TILES, D]) for n in ("x0", "ctx_a", "ctx_c"))
        xp, acc, x2, x3, xd = (sb(n, [P, TILES, D]) for n in ("xp", "acc", "x2", "x3", "xd"))
        xn = [sb(f"xn{k}", [P, TILES, D]) for k in range(4)]
        q_sb = sb("q_sb", [P, TILES, D])
        o_sb = q_sb
        kv_sb = sb("kv_sb", [P, TILES, 2 * D])
        vv_sb, lv_sb = (sb(n, [P, TILES, D]) for n in ("vv_sb", "lv_sb"))
        u_sb = lv_sb
        prod = sb("prod", [P, 2, HH * HD])
        s0 = sb("s0", [P, TILES, HEADS, HEADS])
        mx0, sum0, rec0 = (sb(n, [P, TILES, HEADS]) for n in ("mx0", "sum0", "rec0"))
        sc_sb = sb("sc_sb", [P, TILES, SEQ])
        mx1, sum1, rec1 = (sb(n, [P, TILES]) for n in ("mx1", "sum1", "rec1"))
        blockdiag = sb("blockdiag", [P, TILES, P])
        blockdiag_t = sb("blockdiag_t", [P, TILES, P])

        ctx_t, ctx2_t, xt0, xt2, ot = (sb(n, [P, CH]) for n in ("ctx_t", "ctx2_t", "xt0", "xt2", "ot"))
        xt_hi = {k: sb(f"xt_hi{k}", [P, CH], F32R) for k in (1, 3)}
        xt_lo = {k: sb(f"xt_lo{k}", [P, CH], F32R) for k in (1, 3)}
        vk_t, lk_t = sb("vk_t", [P, CH]), sb("lk_t", [P, CH])
        hidden = sb("hidden", [P, FJ, CH])
        th, pr, hu = sb("th", [P, 2, CH]), sb("pr", [P, CH]), sb("hu", [P, 2, CH])
        sel_t = sb("sel_t", [E0, CH])
        w1_raw = [b[:, :, :].rearrange("p a n -> p (a n)") for b in (hidden, th, hu)]
        w13_raw = [pr[:]] + [b[:, :, :].rearrange("p a n -> p (a n)") for b in (xd, x2, x3, acc)]

        def pieces(raw):
            start = 0
            for piece in raw:
                yield piece, slice(start, start + piece.shape[-1])
                start += piece.shape[-1]

        stats = [sb(f"stats{k}", [P, TILES, 6]) for k in range(4)]
        msum = [sb(f"msum{k}", [P, TILES, 2]) for k in range(4)]
        dmean, var = ([sb(f"{n}{k}", [P, TILES]) for k in range(4)] for n in ("dmean", "var"))
        ve, nmean, rstd, nmr = ([sb(f"{n}{k}", [P, TILES]) for k in range(4)] for n in ("ve", "nmean", "rstd", "nmr"))
        hsum, htr = sb("hsum", [P, TILES]), sb("htr", [P, TILES])
        hge, hle = sb("hge", [P, TILES, TRUNC_MAX]), sb("hle", [P, TILES, TRUNC_MAX])
        heq = sb("heq", [P, TILES, E0, MOD_K])
        onehot = sb("onehot", [P, TILES, E0])
        sel01, sel0 = sb("sel01", [P, TILES, E0]), sb("sel0", [P, TILES, E0])
        lg, sc1, scg, bs1, gate = (sb(n, [P, TILES, E1]) for n in ("lg", "sc1", "scg", "bs1", "gate"))
        lmx, lsum, lrec = (sb(n, [P, TILES]) for n in ("lmx", "lsum", "lrec"))
        cmp_gt, cmp_eq = sb("cmp_gt", [P, TILES, E1, E1]), sb("cmp_eq", [P, TILES, E1, E1])
        rank = sb("rank", [P, TILES, E1])

        Z = [bank(f"Z{k}") for k in range(4)]
        Y, YD = bank("Y"), bank("YD")
        M = [bank(f"M{k}") for k in range(2)]


        def tiles(b):
            return b[:, :].rearrange("p (j d) -> p j d", j=TILES)

        s_ws, s_w2, s_rows, s_cols, s_g = (sem(f"s_{n}") for n in ("ws", "w2", "rows", "cols", "g"))
        s_w1 = [sem(f"s_w1_{n}") for n in range(len(w1_raw))]
        s_w13 = [sem(f"s_w13_{n}") for n in range(len(w13_raw))]
        s_pool, s_act0, s_dve0 = sem("s_pool_consts"), sem("s_act_consts"), sem("s_dve_consts")
        W_PIECES = len(w1_raw) + len(w13_raw)
        POOL_CONSTS, ACT_CONSTS, DVE_CONSTS = 9, 2 + W_PIECES, 5 + W_PIECES

        ld_x, ld_ca, ld_cc, st_out = (signal(n, 16) for n in ("ld_x", "ld_ctx_a", "ld_ctx_c", "st_out"))
        ln_stats = [signal(f"ln_stats{k}", 4) for k in range(4)]
        ln_rstd = [signal(f"ln_rstd{k}", 2) for k in range(4)]
        ln_done = [signal(f"ln_done{k}") for k in range(4)]
        pe_ctxt, pe_ctx2t = signal("pe_ctxt"), signal("pe_ctx2t")
        pe_xt = [signal(f"pe_xt{k}") for k in range(4)]
        ctx_s, ctx2_s, xt0_s, xt2_s, ot_s = (signal(f"{n}_ready") for n in ("ctx_t", "ctx2_t", "xt0", "xt2", "ot"))
        hi_xt = {k: signal(f"hi_xt{k}") for k in (1, 3)}
        lo_xt = {k: signal(f"lo_xt{k}") for k in (1, 3)}
        pe_q, pe_kv = signal("pe_q"), signal("pe_kv", 2)
        qkv = signal("qkv_ready", 3)
        pool_xp = signal("pool_xp")
        pool_qk, pool_av = signal("pool_qk", TILES), signal("pool_av", TILES)
        score0 = signal("score0", TILES)
        sub0 = signal("sub0", 4)
        exp0 = signal("exp0", 2)
        rec0_s = signal("rec0_s", 4)
        av_sum = signal("av_sum", TILES)
        o_ready = signal("o_ready", 2)
        pe_ot, pe_wo, x1_s = signal("pe_ot"), signal("pe_wo"), signal("x1_ready")
        sel_s = signal("sel0_ready", 10)
        pe_selt, selt_s, pe_bias = signal("pe_selt"), signal("selt_ready"), signal("pe_bias")
        pe_z, relu_s = signal("pe_z", E0 * FJ), signal("relu_ready", E0 * FJ)
        pe_y, acc_s = signal("pe_y", E0), signal("acc_step", E0 + 1)
        pe_vk, pe_lk, pe_vv, pe_lv = (signal(f"pe_{n}") for n in ("vk", "lk", "vv", "lv"))
        vk_s, lk_s, vv_s, lv_s = (signal(f"{n}_ready") for n in ("vk", "lk", "vv", "lv"))
        pe_sc, sub1, exp1 = signal("pe_scores"), signal("sub1", 2), signal("exp1")
        bd_s = signal("blockdiag_ready", 4)
        pe_val, u_s, pe_bdt, bdt_s = signal("pe_val"), signal("u_ready"), signal("pe_bdt"), signal("bdt_ready")
        pe_att, x3_s = signal("pe_att"), signal("x3_ready")
        pe_lg, lsub, lexp = signal("pe_logits"), signal("lsub", 2), signal("lexp")
        route = signal("route", 11)
        pe_ab, tanh_s = signal("pe_ab", UNITS), signal("tanh_ready", UNITS)
        pr_s, hu_s = signal("pr_ready", UNITS), signal("hu_ready", UNITS)
        pe_f = signal("pe_ffn1", 1 + E1)
        xd_s = signal("xd_step", 1 + E1)

        block = stack.enter_context(nc.Block())

        def run(eng, body):
            for i in (-2, -1, 0, 1, 2):
                body(i)
            with eng.Fori(3, NC - 2) as i:
                body(i)
            for i in (NC - 2, NC - 1, NC, NC + 1):
                body(i)

        def exists(c):
            return not isinstance(c, int) or 0 <= c < NC

        def unit_out_bank(u):
            return Y if u == UNITS - 1 else YD

        def unit_bank(u):
            return 0 if u == UNITS - 2 else 2

        def is_step(i, k):
            return isinstance(i, int) and i == k

        @block.sync
        def _(sp):
            def body(i):
                if exists(i + 2):
                    c = i + 2
                    if exists(c - 1):
                        sp.wait_ge(ln_done[0].sem, ln_done[0].at(c - 1))
                    if exists(c - 1):
                        sp.wait_ge(pool_xp.sem, pool_xp.at(c - 1))
                    sp.dma_start(x0[:], x_v[:, bass.ds(c, 1)].rearrange("p c j d -> p (c j) d")).then_inc(ld_x.sem, 16)
                    if exists(c - 1):
                        sp.wait_ge(pe_ctxt.sem, pe_ctxt.at(c - 1))
                    sp.dma_start(ctx_a[:], ctx_v[:, bass.ds(c, 1)].rearrange("p c j d -> p (c j) d")).then_inc(ld_ca.sem, 16)
                if exists(i):
                    if exists(i - 1):
                        sp.wait_ge(pe_ctx2t.sem, pe_ctx2t.at(i - 1))
                    sp.dma_start(ctx_c[:], ctx_v[:, bass.ds(i, 1)].rearrange("p c j d -> p (c j) d")).then_inc(ld_cc.sem, 16)
                if exists(i - 2):
                    c = i - 2
                    sp.wait_ge(xd_s.sem, xd_s.at(c))
                    sp.dma_start(out_v[:, bass.ds(c, 1)].rearrange("p c j d -> p (c j) d"), xd[:]).then_inc(st_out.sem, 16)

            body(-2)
            sp.dma_start(ws[:], w_small).then_inc(s_ws, 16)
            sp.dma_start(brow[:], bias_rows.partition_broadcast(P)).then_inc(s_rows, 16)
            sp.dma_start(gates_raw[:, 0:2], g_x.partition_broadcast(P)).then_inc(s_g, 16)
            sp.dma_start(gates_raw[:, 2:4], g_f.partition_broadcast(P)).then_inc(s_g, 16)
            sp.dma_start(bcol[:], bias_cols).then_inc(s_cols, 16)
            for n, (piece, ns) in enumerate(pieces(w1_raw)):
                sp.dma_start(piece, w1[:, ns]).then_inc(s_w1[n], 16)
            sp.dma_start(w2_sb[:, :, :].rearrange("p a n -> p (a n)"), w2).then_inc(s_w2, 16)
            sp.dma_start(b2_sb[:], bias2).then_inc(s_w2, 16)
            for n, (piece, ns) in enumerate(pieces(w13_raw)):
                sp.dma_start(piece, w13[:, ns]).then_inc(s_w13[n], 16)
            sp.dma_start(w2u_sb[:, :, :].rearrange("p a n -> p (a n)"), w2u).then_inc(s_w2, 16)
            for i in (-1, 0, 1, 2):
                body(i)
            with sp.Fori(3, NC - 2) as i:
                body(i)
            for i in (NC - 2, NC - 1, NC, NC + 1):
                body(i)
            sp.wait_ge(st_out.sem, st_out.at(NC - 1))

        @block.gpsimd
        def _(pool):
            pool.memset(ident[:], 0.0).then_inc(s_pool, 1)
            pool.memset(before[:], 1.0).then_inc(s_pool, 1)
            pool.wait_ge(s_pool, 2)
            pool.affine_select(out=ident[:], in_=ident[:], compare_op=ALU.not_equal, fill=1.0, base=0,
                               pattern=[[-1, P]], channel_multiplier=1).then_inc(s_pool, 1)
            pool.affine_select(out=before[:], in_=before[:], compare_op=ALU.is_ge, fill=0.0, base=-1,
                               pattern=[[1, E1], [-1, E1]], channel_multiplier=0).then_inc(s_pool, 1)
            pool.iota(thr_i[:], pattern=[[1, TRUNC_MAX]], base=1, channel_multiplier=0).then_inc(s_pool, 1)
            pool.iota(mod_i[:], pattern=[[1, E0], [E0, MOD_K]], base=-2 * E0, channel_multiplier=0).then_inc(s_pool, 1)
            pool.memset(neghalf[:], -0.5).then_inc(s_pool, 1)
            pool.memset(blockdiag[:, 0:2, :], 0.0).then_inc(s_pool, 1)
            pool.memset(blockdiag[:, 2:4, :], 0.0).then_inc(s_pool, 1)
            pool.wait_ge(s_pool, POOL_CONSTS)

            def norm(k, c):
                pool.wait_ge(ln_stats[k].sem, ln_stats[k].at(c))
                pool.tensor_tensor(out=rstd[k][:], in0=ve[k][:], in1=neghalf[:], op=ALU.pow).then_inc(ln_rstd[k].sem, 1)
                pool.wait_ge(ln_rstd[k].sem, ln_rstd[k].at(c, 1))
                if exists(c - 1):
                    pool.wait_ge(ln_done[k].sem, ln_done[k].at(c - 1))
                pool.tensor_tensor(out=nmr[k][:], in0=nmean[k][:], in1=rstd[k][:], op=ALU.mult).then_inc(ln_rstd[k].sem, 1)

            def times_k(c, t):
                pool.wait_ge(qkv.sem, qkv.at(c, 2 + t // 2))
                if t < 2:
                    if exists(c - 1):
                        pool.wait_ge(av_sum.sem, av_sum.at(c - 1, 3 + t))
                else:
                    pool.wait_ge(score0.sem, score0.at(c, t - 1))
                q = q_sb[:, t, :].rearrange("p (h d) -> p h d", h=HEADS)
                k = kv_sb[:, t, 0:D].rearrange("p (e d) -> p e d", e=HEADS)
                pool.tensor_tensor(out=prod[:, t % 2, :].rearrange("p (h e d) -> p h e d", h=HEADS, e=HEADS),
                                   in0=q.unsqueeze(2).broadcast_to([P, HEADS, HEADS, HD]),
                                   in1=k.unsqueeze(1).broadcast_to([P, HEADS, HEADS, HD]),
                                   op=ALU.mult).then_inc(pool_qk.sem, 1)

            def times_v(c, t):
                pool.wait_ge(exp0.sem, exp0.at(c, 1 + t // 2))
                if t < 2:
                    pool.wait_ge(score0.sem, score0.at(c, 3 + t))
                else:
                    pool.wait_ge(av_sum.sem, av_sum.at(c, t - 1))
                v = kv_sb[:, t, D:2 * D].rearrange("p (d e) -> p d e", e=HEADS)
                pool.tensor_tensor(out=prod[:, t % 2, :].rearrange("p (h d e) -> p h d e", h=HEADS, e=HEADS),
                                   in0=s0[:, t, :, :].unsqueeze(2).broadcast_to([P, HEADS, HD, HEADS]),
                                   in1=v.unsqueeze(1).broadcast_to([P, HEADS, HD, HEADS]),
                                   op=ALU.mult).then_inc(pool_av.sem, 1)

            def body(i):
                a, b, c = i + 1, i, i - 1
                if exists(a):
                    times_k(a, 0)
                    times_k(a, 1)
                    if is_step(i, -1):
                        pool.wait_ge(s_dve0, 3)
                    if exists(b):
                        pool.wait_ge(acc_s.sem, acc_s.at(b, 1))
                    if exists(b):
                        pool.wait_ge(ln_done[1].sem, ln_done[1].at(b))
                    pool.wait_ge(ld_x.sem, ld_x.at(a))
                    pool.tensor_tensor(out=xp[:], in0=x0[:], in1=gbo[:].unsqueeze(1).broadcast_to([P, TILES, D]),
                                       op=ALU.add).then_inc(pool_xp.sem, 1)
                    times_k(a, 2)
                    times_k(a, 3)
                    times_v(a, 0)
                    times_v(a, 1)
                    times_v(a, 2)
                    times_v(a, 3)
                if exists(i + 2):
                    norm(0, i + 2)
                if exists(c):
                    norm(3, c)
                if exists(a):
                    norm(1, a)
                if exists(b):
                    norm(2, b)

            run(pool, body)

        @block.scalar
        def _(act):
            def weights():
                act.wait_ge(s_ws, 16)
                act.activation(wg_hi[:], ws[:, WG:WSMALL], ACT.Copy).then_inc(s_act0, 1)
                for n, (piece, ns) in enumerate(pieces(w1_raw)):
                    act.wait_ge(s_w1[n], 16)
                    act.activation(w1_hi[:, ns], piece, ACT.Copy).then_inc(s_act0, 1)
                for n, (piece, ns) in enumerate(pieces(w13_raw)):
                    act.wait_ge(s_w13[n], 16)
                    act.activation(w13_hi[:, ns], piece, ACT.Copy).then_inc(s_act0, 1)

            def normed(k, src, c):
                act.wait_ge(ln_rstd[k].sem, ln_rstd[k].at(c))
                for j in range(TILES):
                    last = act.activation(xn[k][:, j, :], src[:, j, :], ACT.Identity, bias=nmr[k][:, j:j + 1],
                                          scale=rstd[k][:, j:j + 1])
                last.then_inc(ln_done[k].sem, 1)

            def high(bank_, hi, pe, done, c):
                act.wait_ge(pe.sem, pe.at(c))
                act.activation(hi[:], bank_[:], ACT.Copy).then_inc(done.sem, 1)

            def plain(bank_, dst, pe, done, c):
                act.wait_ge(pe.sem, pe.at(c))
                act.activation(dst[:], bank_[:], ACT.Copy).then_inc(done.sem, 1)

            def relus(b, e):
                for j in range(FJ):
                    n = e * FJ + j
                    act.wait_ge(pe_z.sem, pe_z.at(b, n + 1))
                    if e > 0:
                        act.wait_ge(pe_y.sem, pe_y.at(b, e))
                    else:
                        if exists(b - 1):
                            act.wait_ge(pe_y.sem, pe_y.at(b - 1))
                    act.activation(hidden[:, j, :], Z[j][:], ACT.Relu, bias=bcol[:, CB1 + n:CB1 + n + 1]).then_inc(relu_s.sem, 1)

            def tanhs(c, u):
                act.wait_ge(pe_ab.sem, pe_ab.at(c, u + 1))
                if u >= 2:
                    act.wait_ge(pr_s.sem, pr_s.at(c, u - 1))
                else:
                    if exists(c - 1):
                        act.wait_ge(pr_s.sem, pr_s.at(c - 1, UNITS - 1 + u))
                act.activation(th[:, u % 2, :], Z[unit_bank(u)][:], ACT.Tanh, scale=0.5).then_inc(tanh_s.sem, 1)

            def exp_heads(a, pair):
                act.wait_ge(sub0.sem, sub0.at(a, 2 * pair + 2))
                s = s0[:, 2 * pair:2 * pair + 2, :, :].rearrange("p t h e -> p (t h e)")
                act.activation(s, s, ACT.Exp, scale=HD ** -0.5).then_inc(exp0.sem, 1)

            def mask(b, e):
                act.wait_ge(pe_mask.sem, pe_mask.at(b, e + 1))
                if exists(b - 1):
                    act.wait_ge(term_s.sem, term_s.at(b - 1, e + 1))
                act.activation(masks[:, e, :], MASK_BANK[e][:], ACT.Copy).then_inc(mask_s.sem, 1)

            def body(i):
                a, b, c, d = i + 1, i, i - 1, i - 2
                A, B, C, DD = exists(a), exists(b), exists(c), exists(d)
                if B:
                    relus(b, 0)
                if DD:
                    tanhs(d, 0)
                if A:
                    if exists(a - 1):
                        act.wait_ge(pe_kv.sem, pe_kv.at(a - 1))
                    plain(M[0], ctx_t, pe_ctxt, ctx_s, a)
                    if exists(a - 1):
                        act.wait_ge(pe_q.sem, pe_q.at(a - 1))
                    plain(M[1], xt0, pe_xt[0], xt0_s, a)
                if is_step(i, -1):
                    weights()
                if B:
                    relus(b, 1)
                if C:
                    if exists(c - 1):
                        act.wait_ge(pe_xt[2].sem, pe_xt[2].at(c - 1))
                    normed(2, x2, c)
                if DD:
                    tanhs(d, 1)
                if C:
                    if exists(c - 1):
                        act.wait_ge(pe_vv.sem, pe_vv.at(c - 1))
                    plain(M[1], xt2, pe_xt[2], xt2_s, c)
                    if exists(c - 1):
                        act.wait_ge(pe_lv.sem, pe_lv.at(c - 1))
                    plain(M[0], ctx2_t, pe_ctx2t, ctx2_s, c)
                if B:
                    relus(b, 2)
                if C:
                    act.wait_ge(pe_vk.sem, pe_vk.at(c))
                    if exists(c - 1):
                        act.wait_ge(pe_sc.sem, pe_sc.at(c - 1))
                    act.activation(vk_t[:], M[1][:], ACT.Identity, bias=bcol[:, CBVK:CBVK + 1]).then_inc(vk_s.sem, 1)
                if DD:
                    tanhs(d, 2)
                if C:
                    act.wait_ge(pe_lk.sem, pe_lk.at(c))
                    act.activation(lk_t[:], M[0][:], ACT.Identity, bias=bcol[:, CBLK:CBLK + 1]).then_inc(lk_s.sem, 1)
                if B:
                    act.wait_ge(pe_selt.sem, pe_selt.at(b))
                    if exists(b - 1):
                        act.wait_ge(pe_bias.sem, pe_bias.at(b - 1))
                    act.activation(sel_t[:], M[1][0:E0, :], ACT.Copy).then_inc(selt_s.sem, 1)
                    relus(b, 3)
                if A:
                    exp_heads(a, 0)
                if DD:
                    tanhs(d, 3)
                if B:
                    relus(b, 4)
                if A:
                    exp_heads(a, 1)
                if DD:
                    tanhs(d, 4)
                if C:
                    act.wait_ge(sub1.sem, sub1.at(c))
                    act.activation(sc_sb[:], sc_sb[:], ACT.Exp, scale=D ** -0.5).then_inc(exp1.sem, 1)
                if B:
                    relus(b, 5)
                if C:
                    act.wait_ge(pe_bdt.sem, pe_bdt.at(c))
                    if exists(c - 1):
                        act.wait_ge(pe_att.sem, pe_att.at(c - 1))
                    act.activation(blockdiag_t[:, :, :].rearrange("p j n -> p (j n)"), M[0][:], ACT.Copy).then_inc(bdt_s.sem, 1)
                if DD:
                    tanhs(d, 5)
                if B:
                    relus(b, 6)
                if DD:
                    tanhs(d, 6)
                if exists(i + 2):
                    if exists(i + 1):
                        act.wait_ge(pe_xt[0].sem, pe_xt[0].at(i + 1))
                    normed(0, x0, i + 2)
                if is_step(i, -2):
                    act.wait_ge(s_g, 32)
                    act.activation(tg[:], gates_raw[:], ACT.Tanh).then_inc(s_act0, 1)
                if A:
                    if exists(a - 1):
                        act.wait_ge(pe_wo.sem, pe_wo.at(a - 1))
                    plain(M[1], ot, pe_ot, ot_s, a)
                if B:
                    relus(b, 7)
                if C:
                    if exists(d):
                        act.wait_ge(pe_xt[3].sem, pe_xt[3].at(d))
                    normed(3, x3, c)
                if DD:
                    tanhs(d, 7)
                if DD:
                    tanhs(d, 8)
                if A:
                    if exists(b):
                        act.wait_ge(pe_xt[1].sem, pe_xt[1].at(b))
                    if exists(b):
                        act.wait_ge(sel_s.sem, sel_s.at(b))
                    normed(1, xp, a)
                if C:
                    if exists(d):
                        act.wait_ge(pe_ab.sem, pe_ab.at(d))
                    high(M[1], xt_hi[3], pe_xt[3], hi_xt[3], c)
                if A:
                    if exists(a - 1):
                        act.wait_ge(pe_z.sem, pe_z.at(a - 1))
                    high(M[0], xt_hi[1], pe_xt[1], hi_xt[1], a)
                if DD:
                    tanhs(d, 9)
                if C:
                    act.wait_ge(lsub.sem, lsub.at(c))
                    act.activation(lg[:], lg[:], ACT.Exp).then_inc(lexp.sem, 1)

            act.wait_ge(s_cols, 16)
            run(act, body)

        @block.vector
        def _(dve):
            def consts():
                def step(ins):
                    ins.then_inc(s_dve0, 1)

                dve.wait_ge(s_pool, POOL_CONSTS)
                step(dve.tensor_copy(thr[:], thr_i[:]))
                step(dve.tensor_copy(modv[:], mod_i[:]))
                dve.wait_ge(s_act0, 1)
                dve.wait_ge(s_rows, 16)
                step(dve.tensor_scalar(gbo[:], brow[:, BO:BO + D], tg[:, 0:1], None, ALU.mult))
                step(dve.tensor_scalar(tgh[:], tg[:, 2:3], 0.5, None, ALU.mult))

            def weights():
                def left(lo, raw, hi):
                    dve.tensor_tensor(out=lo, in0=raw, in1=hi.bitcast(F32), op=ALU.subtract).then_inc(s_dve0, 1)

                dve.wait_ge(s_act0, 2)
                left(wg_lo[:], ws[:, WG:WSMALL], wg_hi[:])
                for n, (piece, ns) in enumerate(pieces(w1_raw)):
                    dve.wait_ge(s_act0, 3 + n)
                    left(w1_lo[:, ns], piece, w1_hi[:, ns])
                for n, (piece, ns) in enumerate(pieces(w13_raw)):
                    dve.wait_ge(s_act0, 3 + len(w1_raw) + n)
                    left(w13_lo[:, ns], piece, w13_hi[:, ns])

            def norm_stats(k, src, c):
                for j in range(TILES):
                    last = dve.bn_stats(stats[k][:, j, :], src[:, j, :])
                last.then_inc(ln_stats[k].sem, 1)
                dve.wait_ge(ln_stats[k].sem, ln_stats[k].at(c, 1))
                even, odd = stats[k][:, :, 1:3], stats[k][:, :, 4:6]
                dve.tensor_tensor(out=dmean[k][:], in0=even[:, :, 0], in1=odd[:, :, 0], op=ALU.subtract)
                dve.tensor_tensor(out=msum[k][:], in0=even, in1=odd, op=ALU.add).then_inc(ln_stats[k].sem, 1)
                dve.wait_ge(ln_stats[k].sem, ln_stats[k].at(c, 2))
                if exists(c - 1):
                    dve.wait_ge(ln_rstd[k].sem, ln_rstd[k].at(c - 1))
                dve.scalar_tensor_tensor(out=dmean[k][:], in0=dmean[k][:], scalar=0.25, in1=dmean[k][:], op0=ALU.mult, op1=ALU.mult)
                dve.tensor_scalar(nmean[k][:], msum[k][:, :, 0], -0.5, None, ALU.mult)
                dve.tensor_scalar(var[k][:], msum[k][:, :, 1], 1.0 / D, EPS, ALU.mult, ALU.add).then_inc(ln_stats[k].sem, 1)
                dve.wait_ge(ln_stats[k].sem, ln_stats[k].at(c, 3))
                dve.tensor_tensor(out=ve[k][:], in0=dmean[k][:], in1=var[k][:], op=ALU.add).then_inc(ln_stats[k].sem, 1)

            def low(bank_, hi, lo, hi_done, done, c):
                dve.wait_ge(hi_done.sem, hi_done.at(c))
                dve.tensor_tensor(out=lo[:], in0=bank_[:], in1=hi[:].bitcast(F32), op=ALU.subtract).then_inc(done.sem, 1)

            def expert_out(b, e):
                dve.wait_ge(pe_y.sem, pe_y.at(b, e + 1))
                if e == 0:
                    dve.wait_ge(sel_s.sem, sel_s.at(b))
                    before_, after = xp, acc
                else:
                    dve.wait_ge(acc_s.sem, acc_s.at(b, acc_step(e) - 1))
                    before_, after = acc, x2 if e == E0 - 1 else acc
                if e == E0 - 1:
                    if exists(b - 1):
                        dve.wait_ge(x3_s.sem, x3_s.at(b - 1))
                for j in range(TILES):
                    last = dve.scalar_tensor_tensor(out=after[:, j, :], in0=Y[:, j * P:(j + 1) * P], scalar=sel0[:, j, e:e + 1],
                                                    in1=before_[:, j, :], op0=ALU.mult, op1=ALU.add)
                last.then_inc(acc_s.sem, 1)

            def expert_bias(b):
                dve.wait_ge(pe_bias.sem, pe_bias.at(b))
                dve.wait_ge(acc_s.sem, acc_s.at(b, acc_step(BIAS_AFTER)))
                dve.tensor_tensor(out=acc[:], in0=tiles(M[0]), in1=acc[:], op=ALU.add).then_inc(acc_s.sem, 1)

            def shared_out(d):
                if exists(d - 1):
                    dve.wait_ge(st_out.sem, st_out.at(d - 1))
                residual(YD, tg[:, 3:4], x3, xd, pe_f, xd_s, d, 1)

            def unit_out(d, u):
                bank_ = unit_out_bank(u)
                dve.wait_ge(pe_f.sem, pe_f.at(d, u))
                dve.wait_ge(xd_s.sem, xd_s.at(d, u - 1))
                for j in range(TILES):
                    last = dve.scalar_tensor_tensor(out=xd[:, j, :], in0=bank_[:, j * P:(j + 1) * P],
                                                    scalar=gate[:, j, u - SHARED:u - SHARED + 1],
                                                    in1=xd[:, j, :], op0=ALU.mult, op1=ALU.add)
                last.then_inc(xd_s.sem, 1)

            def keys_values(a, half):
                dve.wait_ge(pe_kv.sem, pe_kv.at(a, half + 1))
                dve.tensor_tensor(out=kv_sb[:, 2 * half:2 * half + 2, :],
                                  in0=M[1 - half][:, :].rearrange("p (j d) -> p j d", j=2),
                                  in1=brow[:, BKV:BKV + 2 * D].unsqueeze(1).broadcast_to([P, 2, 2 * D]),
                                  op=ALU.add).then_inc(qkv.sem, 1)

            def head_scores(a, t):
                dve.wait_ge(pool_qk.sem, pool_qk.at(a, t + 1))
                if t == 0:
                    if exists(a - 1):
                        dve.wait_ge(pool_av.sem, pool_av.at(a - 1))
                dve.tensor_reduce(out=s0[:, t, :, :].rearrange("p h e -> p (h e)"),
                                  in_=prod[:, t % 2, :].rearrange("p (g d) -> p g d", d=HD),
                                  axis=X, op=ALU.add).then_inc(score0.sem, 1)

            def head_max(a, pair):
                ts = slice(2 * pair, 2 * pair + 2)
                dve.wait_ge(score0.sem, score0.at(a, 2 * pair + 2))
                dve.tensor_reduce(out=mx0[:, ts, :], in_=s0[:, ts, :, :], axis=X, op=ALU.max).then_inc(sub0.sem, 1)
                dve.wait_ge(sub0.sem, sub0.at(a, 2 * pair + 1))
                s = s0[:, ts, :, :].rearrange("p t h e -> p (t h) e")
                m = mx0[:, ts, :].rearrange("p t h -> p (t h)")
                dve.tensor_tensor(out=s, in0=s, in1=m.unsqueeze(2).broadcast_to([P, 2 * HEADS, HEADS]),
                                  op=ALU.subtract).then_inc(sub0.sem, 1)

            def head_sum(a, pair):
                ts = slice(2 * pair, 2 * pair + 2)
                dve.wait_ge(exp0.sem, exp0.at(a, pair + 1))
                dve.tensor_reduce(out=sum0[:, ts, :], in_=s0[:, ts, :, :], axis=X, op=ALU.add).then_inc(rec0_s.sem, 1)
                dve.wait_ge(rec0_s.sem, rec0_s.at(a, 2 * pair + 1))
                dve.reciprocal(rec0[:, ts, :], sum0[:, ts, :]).then_inc(rec0_s.sem, 1)

            def head_out(a, t):
                dve.wait_ge(pool_av.sem, pool_av.at(a, t + 1))
                if t == 0:
                    dve.wait_ge(pool_qk.sem, pool_qk.at(a))
                dve.tensor_reduce(out=o_sb[:, t, :], in_=prod[:, t % 2, :].rearrange("p (g e) -> p g e", e=HEADS),
                                  axis=X, op=ALU.add).then_inc(av_sum.sem, 1)

            def head_scale(a, pair):
                ts = slice(2 * pair, 2 * pair + 2)
                dve.wait_ge(av_sum.sem, av_sum.at(a, 2 * pair + 2))
                dve.wait_ge(rec0_s.sem, rec0_s.at(a, 2 * pair + 2))
                o = o_sb[:, ts, :].rearrange("p t (h d) -> p (t h) d", h=HEADS)
                r = rec0[:, ts, :].rearrange("p t h -> p (t h)")
                dve.tensor_tensor(out=o, in0=o, in1=r.unsqueeze(2).broadcast_to([P, 2 * HEADS, HD]),
                                  op=ALU.mult).then_inc(o_ready.sem, 1)

            def biased(bank_, row, dst, pe, done, c):
                dve.wait_ge(pe.sem, pe.at(c))
                dve.tensor_tensor(out=dst[:], in0=tiles(bank_), in1=brow[:, row:row + D].unsqueeze(1).broadcast_to([P, TILES, D]),
                                  op=ALU.add).then_inc(done.sem, 1)

            def unit_open(c, u):
                dve.wait_ge(tanh_s.sem, tanh_s.at(c, u + 1))
                if u > 0:
                    dve.wait_ge(hu_s.sem, hu_s.at(c, u))
                dve.scalar_tensor_tensor(out=pr[:], in0=th[:, u % 2, :], scalar=1.0, in1=Z[unit_bank(u)][:],
                                         op0=ALU.add, op1=ALU.mult).then_inc(pr_s.sem, 1)
                dve.wait_ge(pr_s.sem, pr_s.at(c, u + 1))
                if u >= 2:
                    dve.wait_ge(pe_f.sem, pe_f.at(c, max(1, u - 2)))
                else:
                    if exists(c - 1):
                        dve.wait_ge(pe_f.sem, pe_f.at(c - 1, E1 + u))
                dve.scalar_tensor_tensor(out=hu[:, u % 2, :], in0=pr[:], scalar=0.5, in1=Z[unit_bank(u) + 1][:],
                                         op0=ALU.mult, op1=ALU.mult).then_inc(hu_s.sem, 1)

            def select_experts(a):
                s = sel_s.sem
                dve.wait_ge(ln_done[1].sem, ln_done[1].at(a))
                dve.tensor_tensor(out=hsum[:], in0=xn[1][:, :, 0], in1=xn[1][:, :, 1], op=ALU.add).then_inc(s, 1)
                dve.wait_ge(sel_s.sem, sel_s.at(a, 1))
                hs = hsum[:].unsqueeze(2).broadcast_to([P, TILES, TRUNC_MAX])
                th_ = thr[:].unsqueeze(1).broadcast_to([P, TILES, TRUNC_MAX])
                dve.tensor_tensor(out=hge[:], in0=hs, in1=th_, op=ALU.is_ge).then_inc(s, 1)
                dve.scalar_tensor_tensor(out=hle[:], in0=hs, scalar=-1.0, in1=th_, op0=ALU.mult, op1=ALU.is_ge).then_inc(s, 1)
                dve.wait_ge(sel_s.sem, sel_s.at(a, 3))
                dve.tensor_tensor(out=hge[:], in0=hge[:], in1=hle[:], op=ALU.subtract).then_inc(s, 1)
                dve.wait_ge(sel_s.sem, sel_s.at(a, 4))
                dve.tensor_reduce(out=htr[:], in_=hge[:], axis=X, op=ALU.add).then_inc(s, 1)
                dve.wait_ge(sel_s.sem, sel_s.at(a, 5))
                dve.tensor_tensor(out=heq[:], in0=htr[:].unsqueeze(2).unsqueeze(3).broadcast_to([P, TILES, E0, MOD_K]),
                                  in1=modv[:].unsqueeze(1).broadcast_to([P, TILES, E0, MOD_K]), op=ALU.is_equal).then_inc(s, 1)
                dve.wait_ge(sel_s.sem, sel_s.at(a, 6))
                dve.tensor_reduce(out=onehot[:], in_=heq[:], axis=X, op=ALU.add).then_inc(s, 1)
                dve.wait_ge(sel_s.sem, sel_s.at(a, 7))
                if exists(a - 1):
                    dve.wait_ge(pe_selt.sem, pe_selt.at(a - 1))
                dve.tensor_tensor(out=sel01[:, :, 1:E0], in0=onehot[:, :, 1:E0], in1=onehot[:, :, 0:E0 - 1], op=ALU.add).then_inc(s, 1)
                dve.tensor_tensor(out=sel01[:, :, 0], in0=onehot[:, :, 0], in1=onehot[:, :, E0 - 1], op=ALU.add).then_inc(s, 1)
                dve.wait_ge(sel_s.sem, sel_s.at(a, 9))
                dve.tensor_scalar(sel0[:], sel01[:], tgh[:, 0:1], None, ALU.mult).then_inc(s, 1)

            def logits_max(c):
                dve.wait_ge(pe_lg.sem, pe_lg.at(c))
                l = M[1][:, 0:TILES * E1].rearrange("p (j e) -> p j e", e=E1)
                dve.tensor_reduce(out=lmx[:], in_=l, axis=X, op=ALU.max).then_inc(lsub.sem, 1)
                dve.wait_ge(lsub.sem, lsub.at(c, 1))
                dve.tensor_tensor(out=lg[:], in0=l, in1=lmx[:].unsqueeze(2).broadcast_to([P, TILES, E1]),
                                  op=ALU.subtract).then_inc(lsub.sem, 1)

            def route_tokens(c):
                r = route.sem
                dve.wait_ge(lexp.sem, lexp.at(c))
                dve.tensor_reduce(out=lsum[:], in_=lg[:], axis=X, op=ALU.add).then_inc(r, 1)
                dve.wait_ge(route.sem, route.at(c, 1))
                dve.reciprocal(lrec[:], lsum[:]).then_inc(r, 1)
                dve.wait_ge(route.sem, route.at(c, 2))
                dve.tensor_tensor(out=sc1[:], in0=lg[:], in1=lrec[:].unsqueeze(2).broadcast_to([P, TILES, E1]), op=ALU.mult).then_inc(r, 1)
                dve.wait_ge(route.sem, route.at(c, 3))
                dve.tensor_tensor(out=bs1[:], in0=sc1[:], in1=brow[:, BG:BG + E1].unsqueeze(1).broadcast_to([P, TILES, E1]),
                                  op=ALU.add).then_inc(r, 1)
                dve.tensor_scalar(scg[:], sc1[:], tg[:, 3:4], None, ALU.mult).then_inc(r, 1)
                dve.wait_ge(route.sem, route.at(c, 4))
                own = bs1[:].unsqueeze(3).broadcast_to([P, TILES, E1, E1])
                other = bs1[:].unsqueeze(2).broadcast_to([P, TILES, E1, E1])
                dve.tensor_tensor(out=cmp_gt[:], in0=other, in1=own, op=ALU.is_gt).then_inc(r, 1)
                dve.tensor_tensor(out=cmp_eq[:], in0=other, in1=own, op=ALU.is_equal).then_inc(r, 1)
                dve.wait_ge(route.sem, route.at(c, 7))
                dve.tensor_tensor(out=cmp_eq[:], in0=cmp_eq[:], in1=before[:].unsqueeze(1).broadcast_to([P, TILES, E1, E1]),
                                  op=ALU.mult).then_inc(r, 1)
                dve.wait_ge(route.sem, route.at(c, 8))
                dve.tensor_tensor(out=cmp_gt[:], in0=cmp_gt[:], in1=cmp_eq[:], op=ALU.add).then_inc(r, 1)
                dve.wait_ge(route.sem, route.at(c, 9))
                dve.tensor_reduce(out=rank[:], in_=cmp_gt[:], axis=X, op=ALU.add).then_inc(r, 1)
                dve.wait_ge(route.sem, route.at(c, 10))
                dve.scalar_tensor_tensor(out=gate[:], in0=rank[:], scalar=2.0, in1=scg[:], op0=ALU.is_lt, op1=ALU.mult).then_inc(r, 1)
                dve.wait_ge(route.sem, route.at(c, 11))

            def residual(bank_, gate_col, prev, dst, pe, done, c, k=None):
                dve.wait_ge(pe.sem, pe.at(c, k))
                dve.scalar_tensor_tensor(out=dst[:, :, :].rearrange("p j d -> p (j d)"), in0=bank_[:], scalar=gate_col,
                                         in1=prev[:, :, :].rearrange("p j d -> p (j d)"),
                                         op0=ALU.mult, op1=ALU.add).then_inc(done.sem, 1)

            def body(i):
                a, b, c, d = i + 1, i, i - 1, i - 2
                A, B, C, DD = exists(a), exists(b), exists(c), exists(d)
                if DD:
                    route_tokens(d)
                    unit_open(d, 0)
                if A:
                    dve.wait_ge(pe_q.sem, pe_q.at(a))
                    if exists(a - 1):
                        dve.wait_ge(pe_ot.sem, pe_ot.at(a - 1))
                    dve.tensor_tensor(out=q_sb[:], in0=tiles(M[0]), in1=brow[:, BQ:BQ + D].unsqueeze(1).broadcast_to([P, TILES, D]),
                                      op=ALU.add).then_inc(qkv.sem, 1)
                    if exists(a - 1):
                        dve.wait_ge(pool_av.sem, pool_av.at(a - 1))
                    keys_values(a, 0)
                if B:
                    expert_out(b, 0)
                if A:
                    keys_values(a, 1)
                if DD:
                    unit_open(d, 1)
                if A:
                    head_scores(a, 0)
                if B:
                    expert_out(b, 1)
                if A:
                    head_scores(a, 1)
                if is_step(i, -1):
                    weights()
                if DD:
                    shared_out(d)
                if A:
                    head_max(a, 0)
                if DD:
                    unit_open(d, 2)
                if B:
                    expert_out(b, 2)
                if A:
                    head_scores(a, 2)
                if C:
                    if exists(c - 1):
                        dve.wait_ge(pe_val.sem, pe_val.at(c - 1))
                    biased(M[0], BVV, vv_sb, pe_vv, vv_s, c)
                if DD:
                    unit_out(d, 2)
                    unit_open(d, 3)
                if A:
                    head_scores(a, 3)
                    head_max(a, 1)
                if C:
                    if exists(c - 1):
                        dve.wait_ge(pe_att.sem, pe_att.at(c - 1))
                    biased(M[1], BLV, lv_sb, pe_lv, lv_s, c)
                if B:
                    expert_out(b, 3)
                    expert_bias(b)
                if A:
                    head_sum(a, 0)
                    head_out(a, 0)
                if C:
                    dve.wait_ge(pe_sc.sem, pe_sc.at(c))
                    s = M[1][:, 0:TILES * SEQ].rearrange("p (j n) -> p j n", n=SEQ)
                    dve.tensor_reduce(out=mx1[:], in_=s, axis=X, op=ALU.max).then_inc(sub1.sem, 1)
                    dve.wait_ge(sub1.sem, sub1.at(c, 1))
                    dve.tensor_tensor(out=sc_sb[:], in0=s, in1=mx1[:].unsqueeze(2).broadcast_to([P, TILES, SEQ]),
                                      op=ALU.subtract).then_inc(sub1.sem, 1)
                if DD:
                    unit_out(d, 3)
                    unit_open(d, 4)
                if A:
                    head_sum(a, 1)
                if B:
                    expert_out(b, 4)
                if C:
                    dve.wait_ge(exp1.sem, exp1.at(c))
                    dve.tensor_reduce(out=sum1[:], in_=sc_sb[:], axis=X, op=ALU.add).then_inc(bd_s.sem, 1)
                    dve.wait_ge(bd_s.sem, bd_s.at(c, 1))
                    dve.reciprocal(rec1[:], sum1[:]).then_inc(bd_s.sem, 1)
                    dve.wait_ge(bd_s.sem, bd_s.at(c, 2))
                    if exists(c - 1):
                        dve.wait_ge(pe_val.sem, pe_val.at(c - 1))
                    for h in range(2):
                        ps = slice(h * SEQ, (h + 1) * SEQ)
                        dve.tensor_tensor(out=blockdiag[ps, :, h * SEQ:(h + 1) * SEQ], in0=sc_sb[ps, :, :],
                                          in1=rec1[ps, :].unsqueeze(2).broadcast_to([SEQ, TILES, SEQ]),
                                          op=ALU.mult).then_inc(bd_s.sem, 1)
                if A:
                    head_out(a, 1)
                    head_scale(a, 0)
                if DD:
                    unit_out(d, 4)
                    unit_open(d, 5)
                if A:
                    head_out(a, 2)
                if B:
                    expert_out(b, 5)
                if C:
                    dve.wait_ge(pe_val.sem, pe_val.at(c))
                    dve.wait_ge(lv_s.sem, lv_s.at(c))
                    dve.tensor_tensor(out=u_sb[:], in0=tiles(M[1]), in1=lv_sb[:], op=ALU.add).then_inc(u_s.sem, 1)
                if A:
                    head_out(a, 3)
                    head_scale(a, 1)
                if C:
                    if exists(d):
                        dve.wait_ge(xd_s.sem, xd_s.at(d, 1))
                    residual(M[0], tg[:, 1:2], x2, x3, pe_att, x3_s, c)
                if exists(i + 2):
                    dve.wait_ge(ld_x.sem, ld_x.at(i + 2))
                    norm_stats(0, x0, i + 2)
                if is_step(i, -2):
                    consts()
                if DD:
                    unit_out(d, 5)
                    unit_open(d, 6)
                if B:
                    expert_out(b, 6)
                if C:
                    dve.wait_ge(x3_s.sem, x3_s.at(c))
                    norm_stats(3, x3, c)
                if A:
                    dve.wait_ge(pool_xp.sem, pool_xp.at(a))
                    residual(M[0], tg[:, 0:1], xp, xp, pe_wo, x1_s, a)
                    dve.wait_ge(x1_s.sem, x1_s.at(a))
                    norm_stats(1, xp, a)
                if DD:
                    unit_out(d, 6)
                    unit_open(d, 7)
                if B:
                    expert_out(b, 7)
                if DD:
                    unit_out(d, 7)
                    unit_open(d, 8)
                if C:
                    if exists(d):
                        dve.wait_ge(pe_ab.sem, pe_ab.at(d))
                    low(M[1], xt_hi[3], xt_lo[3], hi_xt[3], lo_xt[3], c)
                if A:
                    if exists(a - 1):
                        dve.wait_ge(pe_z.sem, pe_z.at(a - 1))
                    low(M[0], xt_hi[1], xt_lo[1], hi_xt[1], lo_xt[1], a)
                if DD:
                    unit_open(d, 9)
                if A:
                    select_experts(a)
                if C:
                    logits_max(c)
                if DD:
                    unit_out(d, 8)
                if B:
                    dve.wait_ge(acc_s.sem, acc_s.at(b))
                    norm_stats(2, x2, b)
                if DD:
                    unit_out(d, 9)

            dve.wait_ge(s_rows, 16)
            dve.wait_ge(s_cols, 16)
            run(dve, body)

        @block.tensor
        def _(pe):
            def transposes(bank_, src):
                for j in range(TILES):
                    last = pe.transpose(bank_[:, j * P:(j + 1) * P], src[:, j, :], ident[:])
                return last

            def three(dst, l_hi, l_lo, r_hi, r_lo):
                pe.matmul(dst, l_hi, r_hi, start=True, stop=False)
                pe.matmul(dst, l_lo, r_hi, start=False, stop=False)
                return pe.matmul(dst, l_hi, r_lo, start=False, stop=True)

            def by_token(bank_, t, w, width, which=range(TILES)):
                for n, j in enumerate(which):
                    last = pe.matmul(bank_[:, n * width:(n + 1) * width], t[:, j * P:(j + 1) * P], ws[:, w:w + width],
                                     start=True, stop=True)
                return last

            def by_width(bank_, w_hi, w_lo, w, t_hi, t_lo):
                return three(bank_[:], w_hi[:, w:w + P], w_lo[:, w:w + P], t_hi[:], t_lo[:])

            def ffn0_in(b, e):
                for j in range(FJ):
                    n = e * FJ + j
                    if e > 0:
                        pe.wait_ge(relu_s.sem, relu_s.at(b, n + 1 - FJ))
                        if j == 2:
                            if exists(b - 2):
                                pe.wait_ge(hu_s.sem, hu_s.at(b - 2, e))
                    else:
                        if j == 0:
                            pe.wait_ge(hi_xt[1].sem, hi_xt[1].at(b))
                            pe.wait_ge(lo_xt[1].sem, lo_xt[1].at(b))
                            if is_step(b, 0):
                                pe.wait_ge(s_act0, ACT_CONSTS)
                                pe.wait_ge(s_dve0, DVE_CONSTS)
                                pe.wait_ge(s_w2, 48)
                        if j < 2:
                            if exists(b - 1):
                                pe.wait_ge(relu_s.sem, relu_s.at(b - 1, E0 * FJ))
                            if exists(b - 3):
                                pe.wait_ge(hu_s.sem, hu_s.at(b - 3, UNITS - 1))
                        else:
                            if exists(b - 3):
                                pe.wait_ge(hu_s.sem, hu_s.at(b - 3))
                    by_width(Z[j], w1_hi, w1_lo, n * P, xt_hi[1], xt_lo[1]).then_inc(pe_z.sem, 1)

            def ffn0_out(b, e):
                if e > 0:
                    pe.wait_ge(acc_s.sem, acc_s.at(b, acc_step(e - 1)))
                else:
                    if exists(b - 1):
                        pe.wait_ge(acc_s.sem, acc_s.at(b - 1))
                    if exists(b - 3):
                        pe.wait_ge(xd_s.sem, xd_s.at(b - 3))
                pe.wait_ge(relu_s.sem, relu_s.at(b, FJ * (e + 1)))
                for j in range(TILES):
                    js = slice(j * P, (j + 1) * P)
                    for f in range(FJ):
                        last = pe.matmul(Y[:, js], hidden[:, f, js], w2_sb[:, e * FJ + f, :], start=(f == 0), stop=(f == FJ - 1))
                last.then_inc(pe_y.sem, 1)

            def unit_in(d, u):
                if u < UNITS - 2:
                    if exists(d + 2):
                        pe.wait_ge(relu_s.sem, relu_s.at(d + 2, FJ * (u + 1)))
                    if u > 0:
                        pe.wait_ge(hu_s.sem, hu_s.at(d, u))
                elif u == UNITS - 2:
                    if exists(d + 2):
                        pe.wait_ge(relu_s.sem, relu_s.at(d + 2))
                else:
                    pe.wait_ge(hu_s.sem, hu_s.at(d, u - 1))
                z = unit_bank(u)
                by_width(Z[z], w13_hi, w13_lo, 2 * u * P, xt_hi[3], xt_lo[3])
                by_width(Z[z + 1], w13_hi, w13_lo, (2 * u + 1) * P, xt_hi[3], xt_lo[3]).then_inc(pe_ab.sem, 1)

            def unit_out(d, u):
                bank_ = unit_out_bank(u)
                if u == UNITS - 1:
                    if exists(d + 2):
                        pe.wait_ge(acc_s.sem, acc_s.at(d + 2))
                    if exists(d - 1):
                        pe.wait_ge(xd_s.sem, xd_s.at(d - 1))
                else:
                    pe.wait_ge(xd_s.sem, xd_s.at(d, u - 1))
                pe.wait_ge(hu_s.sem, hu_s.at(d, u + 1))
                for j in range(TILES):
                    js = slice(j * P, (j + 1) * P)
                    last = pe.matmul(bank_[:, js], hu[:, u % 2, js], w2u_sb[:, u, :], start=True, stop=True)
                last.then_inc(pe_f.sem, 1)

            def shared_out(d):
                if exists(d - 1):
                    pe.wait_ge(xd_s.sem, xd_s.at(d - 1, E1))
                pe.wait_ge(hu_s.sem, hu_s.at(d, SHARED))
                for j in range(TILES):
                    js = slice(j * P, (j + 1) * P)
                    for u in range(SHARED):
                        last = pe.matmul(YD[:, js], hu[:, u, js], w2u_sb[:, u, :], start=(u == 0), stop=(u == SHARED - 1))
                last.then_inc(pe_f.sem, 1)

            def body(i):
                a, b, c, d = i + 1, i, i - 1, i - 2
                A, B, C, DD = exists(a), exists(b), exists(c), exists(d)
                if is_step(i, -1):
                    pe.wait_ge(s_pool, POOL_CONSTS)
                if B:
                    ffn0_in(b, 0)
                if DD:
                    if exists(d):
                        pe.wait_ge(hi_xt[3].sem, hi_xt[3].at(d))
                    if exists(d):
                        pe.wait_ge(lo_xt[3].sem, lo_xt[3].at(d))
                    unit_in(d, 0)
                if A:
                    pe.wait_ge(ld_ca.sem, ld_ca.at(a))
                    transposes(M[0], ctx_a).then_inc(pe_ctxt.sem, 1)
                    pe.wait_ge(ln_done[0].sem, ln_done[0].at(a))
                    if exists(d):
                        pe.wait_ge(lsub.sem, lsub.at(d))
                    transposes(M[1], xn[0]).then_inc(pe_xt[0].sem, 1)
                if B:
                    ffn0_out(b, 0)
                if is_step(i, -1):
                    pe.wait_ge(s_ws, 16)
                if A:
                    pe.wait_ge(ctx_s.sem, ctx_s.at(a))
                    pe.wait_ge(xt0_s.sem, xt0_s.at(a))
                    by_token(M[0], xt0, WQ, D).then_inc(pe_q.sem, 1)
                    by_token(M[1], ctx_t, WKV, 2 * D, (0, 1)).then_inc(pe_kv.sem, 1)
                if B:
                    ffn0_in(b, 1)
                if A:
                    pe.wait_ge(qkv.sem, qkv.at(a, 1))
                    by_token(M[0], ctx_t, WKV, 2 * D, (2, 3)).then_inc(pe_kv.sem, 1)
                if DD:
                    unit_in(d, 1)
                if B:
                    ffn0_out(b, 1)
                if C:
                    pe.wait_ge(ln_done[2].sem, ln_done[2].at(c))
                    if exists(a):
                        pe.wait_ge(qkv.sem, qkv.at(a, 3))
                    if exists(d):
                        pe.wait_ge(lsub.sem, lsub.at(d))
                    transposes(M[1], xn[2]).then_inc(pe_xt[2].sem, 1)
                    pe.wait_ge(ld_cc.sem, ld_cc.at(c))
                    transposes(M[0], ctx_c).then_inc(pe_ctx2t.sem, 1)
                if B:
                    ffn0_in(b, 2)
                if C:
                    pe.wait_ge(xt2_s.sem, xt2_s.at(c))
                    pe.matmul(M[1][:], ws[:, WVK:WVK + P], xt2[:], start=True, stop=True).then_inc(pe_vk.sem, 1)
                if DD:
                    shared_out(d)
                    unit_in(d, 2)
                if B:
                    ffn0_out(b, 2)
                if C:
                    pe.wait_ge(ctx2_s.sem, ctx2_s.at(c))
                    pe.matmul(M[0][:], ws[:, WLK:WLK + P], ctx2_t[:], start=True, stop=True).then_inc(pe_lk.sem, 1)
                if B:
                    if not C:
                        if exists(a):
                            pe.wait_ge(qkv.sem, qkv.at(a))
                    pe.wait_ge(sel_s.sem, sel_s.at(b))
                    if exists(c):
                        pe.wait_ge(vk_s.sem, vk_s.at(c))
                    for j in range(TILES):
                        last = pe.transpose(M[1][0:E0, j * P:(j + 1) * P], sel0[:, j, :], ident[:])
                    last.then_inc(pe_selt.sem, 1)
                if B:
                    ffn0_in(b, 3)
                if C:
                    pe.wait_ge(lk_s.sem, lk_s.at(c))
                    by_token(M[0], xt2, WVV, D).then_inc(pe_vv.sem, 1)
                if DD:
                    unit_out(d, 2)
                    unit_in(d, 3)
                if B:
                    ffn0_out(b, 3)
                if C:
                    pe.wait_ge(vk_s.sem, vk_s.at(c))
                    if exists(b):
                        pe.wait_ge(selt_s.sem, selt_s.at(b))
                    by_token(M[1], ctx2_t, WLV, D).then_inc(pe_lv.sem, 1)
                if B:
                    pe.wait_ge(selt_s.sem, selt_s.at(b))
                    if exists(c):
                        pe.wait_ge(vv_s.sem, vv_s.at(c))
                    for j in range(TILES):
                        js = slice(j * P, (j + 1) * P)
                        last = pe.matmul(M[0][:, js], sel_t[:, js], b2_sb[:], start=True, stop=True)
                    last.then_inc(pe_bias.sem, 1)
                if B:
                    ffn0_in(b, 4)
                if C:
                    pe.wait_ge(lv_s.sem, lv_s.at(c))
                    for j in range(TILES):
                        for h in range(2):
                            ts = slice(j * P + h * SEQ, j * P + (h + 1) * SEQ)
                            last = pe.matmul(M[1][h * SEQ:(h + 1) * SEQ, j * SEQ:(j + 1) * SEQ], vk_t[:, ts], lk_t[:, ts],
                                             start=True, stop=True)
                    last.then_inc(pe_sc.sem, 1)
                if DD:
                    unit_out(d, 3)
                    unit_in(d, 4)
                if B:
                    ffn0_out(b, 4)
                if B:
                    ffn0_in(b, 5)
                if C:
                    pe.wait_ge(bd_s.sem, bd_s.at(c))
                    if exists(b):
                        pe.wait_ge(acc_s.sem, acc_s.at(b, acc_step(BIAS_AFTER) + 1))
                    transposes(M[0], blockdiag).then_inc(pe_bdt.sem, 1)
                if DD:
                    unit_out(d, 4)
                    unit_in(d, 5)
                if B:
                    ffn0_out(b, 5)
                if C:
                    for j in range(TILES):
                        last = pe.matmul(M[1][:, j * P:(j + 1) * P], blockdiag[:, j, :], vv_sb[:, j, :], start=True, stop=True)
                    last.then_inc(pe_val.sem, 1)
                if B:
                    ffn0_in(b, 6)
                if C:
                    pe.wait_ge(bdt_s.sem, bdt_s.at(c))
                    pe.wait_ge(u_s.sem, u_s.at(c))
                    for j in range(TILES):
                        last = pe.matmul(M[0][:, j * P:(j + 1) * P], blockdiag_t[:, j, :], u_sb[:, j, :], start=True, stop=True)
                    last.then_inc(pe_att.sem, 1)
                if DD:
                    unit_out(d, 5)
                    unit_in(d, 6)
                if B:
                    ffn0_out(b, 6)
                if A:
                    if exists(c):
                        pe.wait_ge(u_s.sem, u_s.at(c))
                    pe.wait_ge(o_ready.sem, o_ready.at(a))
                    transposes(M[1], o_sb).then_inc(pe_ot.sem, 1)
                if B:
                    ffn0_in(b, 7)
                if A:
                    pe.wait_ge(ot_s.sem, ot_s.at(a))
                    if exists(c):
                        pe.wait_ge(x3_s.sem, x3_s.at(c))
                    by_token(M[0], ot, WO, D).then_inc(pe_wo.sem, 1)
                if DD:
                    unit_out(d, 6)
                    unit_in(d, 7)
                if B:
                    ffn0_out(b, 7)
                if C:
                    pe.wait_ge(ln_done[3].sem, ln_done[3].at(c))
                    if exists(a):
                        pe.wait_ge(ot_s.sem, ot_s.at(a))
                    transposes(M[1], xn[3]).then_inc(pe_xt[3].sem, 1)
                if DD:
                    unit_out(d, 7)
                    unit_in(d, 8)
                    unit_in(d, 9)
                if A:
                    pe.wait_ge(ln_done[1].sem, ln_done[1].at(a))
                    transposes(M[0], xn[1]).then_inc(pe_xt[1].sem, 1)
                if DD:
                    unit_out(d, 8)
                if C:
                    pe.wait_ge(hi_xt[3].sem, hi_xt[3].at(c))
                    pe.wait_ge(lo_xt[3].sem, lo_xt[3].at(c))
                    for j in range(TILES):
                        js = slice(j * P, (j + 1) * P)
                        last = three(M[1][:, j * E1:(j + 1) * E1], xt_hi[3][:, js], xt_lo[3][:, js], wg_hi[:], wg_lo[:])
                    last.then_inc(pe_lg.sem, 1)
                if DD:
                    unit_out(d, 9)

            run(pe, body)


def kernel(x, ctx_1024, g_xattn, g_ffn, L0_xattn_Wq, L0_xattn_bq, L0_xattn_Wk, L0_xattn_bk, L0_xattn_Wv, L0_xattn_bv,
           L0_xattn_Wo, L0_xattn_bo, L0_ffn_W1, L0_ffn_b1, L0_ffn_W2, L0_ffn_b2, L1_xattn_W_vk, L1_xattn_b_vk,
           L1_xattn_W_lk, L1_xattn_b_lk, L1_xattn_W_vv, L1_xattn_b_vv, L1_xattn_W_lv, L1_xattn_b_lv, L1_ffn_gate_w,
           L1_ffn_gate_bias, L1_ffn_w1, L1_ffn_w3, L1_ffn_w2, L1_ffn_sw1, L1_ffn_sw3, L1_ffn_sw2):
    import concourse.bacc as bacc
    import numpy as np
    from concourse.bass_utils import run_bass_kernel_spmd

    shape = np.asarray(x).shape
    a = {k: np.asarray(v) for k, v in dict(locals()).items() if k[0] == "L" or k in ("g_xattn", "g_ffn")}

    def width_first(w):
        return np.ascontiguousarray(w.reshape(HEADS, HD, -1).swapaxes(0, 1).reshape(w.shape))

    w_small = np.concatenate([
        a["L0_xattn_Wq"].T, a["L0_xattn_Wk"].T, width_first(a["L0_xattn_Wv"]).T, a["L0_xattn_Wo"].T,
        a["L1_xattn_W_vk"].T, a["L1_xattn_W_lk"].T, a["L1_xattn_W_vv"].T, a["L1_xattn_W_lv"].T, a["L1_ffn_gate_w"].T], axis=1)
    w1 = a["L0_ffn_W1"].transpose(1, 0, 2).reshape(P, -1)
    w2 = a["L0_ffn_W2"].reshape(E0, FJ, P, D).transpose(2, 0, 1, 3).reshape(P, -1)
    up = np.concatenate([a["L1_ffn_sw1"].reshape(SHARED, P, D), a["L1_ffn_w1"]], axis=0)
    gt = np.concatenate([a["L1_ffn_sw3"].reshape(SHARED, P, D), a["L1_ffn_w3"]], axis=0)
    w13 = np.stack([up, gt], axis=1).transpose(3, 0, 1, 2).reshape(P, -1)
    down = np.concatenate([a["L1_ffn_sw2"].reshape(D, SHARED, P).transpose(1, 0, 2), a["L1_ffn_w2"]], axis=0)
    w2u = down.transpose(2, 0, 1).reshape(P, -1)
    rows = np.concatenate([a["L0_xattn_bq"], a["L0_xattn_bk"], width_first(a["L0_xattn_bv"]), a["L0_xattn_bo"],
                           a["L1_xattn_b_vv"], a["L1_xattn_b_lv"], a["L1_ffn_gate_bias"]])
    cols = np.concatenate([a["L0_ffn_b1"].reshape(E0 * FJ, P), a["L1_xattn_b_vk"].reshape(1, P), a["L1_xattn_b_lk"].reshape(1, P)], axis=0).T
    arrays = {
        "x": np.asarray(x).reshape(-1, D), "ctx": np.asarray(ctx_1024).reshape(-1, D), "g_x": a["g_xattn"], "g_f": a["g_ffn"],
        "w_small": w_small, "w1": w1, "w2": w2, "w13": w13, "w2u": w2u, "rows": rows, "cols": cols, "b2": a["L0_ffn_b2"],
    }
    arrays = {f"in_{k}": np.ascontiguousarray(v) for k, v in arrays.items()}
    nc = bacc.Bacc("TRN2", target_bir_lowering=False, num_devices=1)
    ins = [nc.dram_tensor(k, v.shape, mybir.dt.from_np(v.dtype), kind="ExternalInput").ap() for k, v in arrays.items()]
    out = nc.dram_tensor("out_0", arrays["in_x"].shape, F32, kind="ExternalOutput").ap()
    build(nc, *ins, out)
    r = run_bass_kernel_spmd(nc, [arrays], core_ids=[0])
    return r.results[0]["out_0"].reshape(shape)
```

```python
from contextlib import ExitStack

import concourse.bass as bass
from concourse import mybir

F32 = mybir.dt.float32
F32R = mybir.dt.float32r
I32 = mybir.dt.int32
ALU = mybir.AluOpType
ACT = mybir.ActivationFunctionType
X = mybir.AxisListType.X

P = 128
D = 128
TILES = 4
CH = TILES * P
SEQ = 64
HEADS, HD = 16, 8
HH = HEADS * HEADS
E0, FJ = 8, 4
E1, SHARED = 8, 2
UNITS = SHARED + E1
TRUNC_MAX = 17
MOD_K = 5
EPS = 1e-5

WQ, WKV, WO, WVK, WLK, WVV, WLV, WG = 0, 128, 384, 512, 640, 768, 896, 1024
WSMALL = WG + 8
BQ, BKV, BO, BVV, BLV, BG = 0, 128, 384, 512, 640, 768
BROWS = BG + 8
CB1, CBVK, CBLK = 0, 32, 33
BCOLS = 34
BIAS_AFTER = 3


def acc_step(e):
    return e + 1 if e <= BIAS_AFTER else e + 2


class Signal:

    def __init__(self, sem, per):
        self.sem, self.per = sem, per

    def at(self, c, k=None):
        return c * self.per + (self.per if k is None else k)


def build(nc, x, ctx_in, g_x, g_f, w_small, w1, w2, w13, w2u, bias_rows, bias_cols, bias2, out):
    NT = x.shape[0]
    NC = NT // CH
    x_v = x.rearrange("(c j p) d -> p c j d", j=TILES, p=P)
    ctx_v = ctx_in.rearrange("(c j p) d -> p c j d", j=TILES, p=P)
    out_v = out.rearrange("(c j p) d -> p c j d", j=TILES, p=P)

    with ExitStack() as stack:
        def sb(name, shape, dt=F32):
            return stack.enter_context(nc.sbuf_tensor(name, shape, dt))

        def bank(name):
            return stack.enter_context(nc.psum_tensor(name, [P, CH], F32))

        def sem(name):
            return stack.enter_context(nc.semaphore(name))

        def signal(name, per=1):
            return Signal(sem(name), per)

        ws = sb("ws", [P, WSMALL])
        wg_parts, wg_high = sb("wg_parts", [P, 2 * E1], F32R), sb("wg_high", [P, 2 * E1], F32R)
        w1_hi, w1_lo = sb("w1_hi", [P, E0 * FJ * P], F32R), sb("w1_lo", [P, E0 * FJ * P], F32R)
        w13_hi, w13_lo = sb("w13_hi", [P, UNITS * 2 * P], F32R), sb("w13_lo", [P, UNITS * 2 * P], F32R)
        w2_sb = sb("w2_sb", [P, E0 * FJ, D])
        w2u_sb = sb("w2u_sb", [P, UNITS, D])
        b2_sb = sb("b2_sb", [E0, D])
        brow = sb("brow", [P, BROWS])
        bcol = sb("bcol", [P, BCOLS])
        gates_raw, tg = sb("gates_raw", [P, 4]), sb("tg", [P, 4])
        tgh = sb("tgh", [P, 1])
        gbo = sb("gbo", [P, D])
        ident = sb("ident", [P, P])
        thr_i, thr = sb("thr_i", [P, TRUNC_MAX], I32), sb("thr", [P, TRUNC_MAX])
        mod_i, modv = sb("mod_i", [P, E0, MOD_K], I32), sb("modv", [P, E0, MOD_K])
        before = sb("before", [P, E1, E1])
        neghalf = sb("neghalf", [P, TILES])

        x0, ctx_a, ctx_c = (sb(n, [P, TILES, D]) for n in ("x0", "ctx_a", "ctx_c"))
        xp, acc, x2, x3, xd = (sb(n, [P, TILES, D]) for n in ("xp", "acc", "x2", "x3", "xd"))
        xn = [sb(f"xn{k}", [P, TILES, D]) for k in range(4)]
        q_sb = sb("q_sb", [P, TILES, D])
        o_sb = q_sb
        kv_sb = sb("kv_sb", [P, TILES, 2 * D])
        vv_sb, lv_sb = (sb(n, [P, TILES, D]) for n in ("vv_sb", "lv_sb"))
        u_sb = lv_sb
        prod = sb("prod", [P, 2, HH * HD])
        s0 = sb("s0", [P, TILES, HEADS, HEADS])
        mx0, sum0, rec0 = (sb(n, [P, TILES, HEADS]) for n in ("mx0", "sum0", "rec0"))
        sc_sb = sb("sc_sb", [P, TILES, SEQ])
        mx1, sum1, rec1 = (sb(n, [P, TILES]) for n in ("mx1", "sum1", "rec1"))
        blockdiag = sb("blockdiag", [P, TILES, P])
        blockdiag_t = sb("blockdiag_t", [P, TILES, P])

        ctx_t, ctx2_t, xt0, xt2, ot = (sb(n, [P, CH]) for n in ("ctx_t", "ctx2_t", "xt0", "xt2", "ot"))
        xt_hi = {k: sb(f"xt_hi{k}", [P, CH], F32R) for k in (1, 3)}
        xt_lo = {k: sb(f"xt_lo{k}", [P, CH], F32R) for k in (1, 3)}
        vk_t, lk_t = sb("vk_t", [P, CH]), sb("lk_t", [P, CH])
        hidden = sb("hidden", [P, FJ, CH])
        th, pr, hu = sb("th", [P, 2, CH]), sb("pr", [P, CH]), sb("hu", [P, 2, CH])
        sel_t = sb("sel_t", [E0, CH])
        w1_raw = [b[:, :, :].rearrange("p a n -> p (a n)") for b in (hidden, th, hu)]
        w13_raw = [pr[:]] + [b[:, :, :].rearrange("p a n -> p (a n)") for b in (xd, x2, x3)] + [vk_t[:]]

        def pieces(raw):
            start = 0
            for piece in raw:
                yield piece, slice(start, start + piece.shape[-1])
                start += piece.shape[-1]

        stats = [sb(f"stats{k}", [P, TILES, 6]) for k in range(4)]
        msum = [sb(f"msum{k}", [P, TILES, 2]) for k in range(4)]
        dmean, var = ([sb(f"{n}{k}", [P, TILES]) for k in range(4)] for n in ("dmean", "var"))
        ve, nmean, rstd, nmr = ([sb(f"{n}{k}", [P, TILES]) for k in range(4)] for n in ("ve", "nmean", "rstd", "nmr"))
        hsum, htr = sb("hsum", [P, TILES]), sb("htr", [P, TILES])
        hge, hle = sb("hge", [P, TILES, TRUNC_MAX]), sb("hle", [P, TILES, TRUNC_MAX])
        heq = sb("heq", [P, TILES, E0, MOD_K])
        onehot = sb("onehot", [P, TILES, E0])
        sel01, sel0 = sb("sel01", [P, TILES, E0]), sb("sel0", [P, TILES, E0])
        lg_sum, lg, sc1, scg, bs1, gate = (sb(n, [P, TILES, E1]) for n in ("lg_sum", "lg", "sc1", "scg", "bs1", "gate"))
        lmx, lsum, lrec = (sb(n, [P, TILES]) for n in ("lmx", "lsum", "lrec"))
        cmp_gt, cmp_eq = sb("cmp_gt", [P, TILES, E1, E1]), sb("cmp_eq", [P, TILES, E1, E1])
        rank = sb("rank", [P, TILES, E1])

        Z = [bank(f"Z{k}") for k in range(4)]
        Y, YD = bank("Y"), bank("YD")
        M = [bank(f"M{k}") for k in range(2)]


        def tiles(b):
            return b[:, :].rearrange("p (j d) -> p j d", j=TILES)

        s_ws, s_w2, s_rows, s_cols, s_g = (sem(f"s_{n}") for n in ("ws", "w2", "rows", "cols", "g"))
        s_w1 = [sem(f"s_w1_{n}") for n in range(len(w1_raw))]
        s_w13 = [sem(f"s_w13_{n}") for n in range(len(w13_raw))]
        s_pool, s_act0, s_dve0 = sem("s_pool_consts"), sem("s_act_consts"), sem("s_dve_consts")
        W_PIECES = len(w1_raw) + len(w13_raw)
        POOL_CONSTS, ACT_CONSTS, DVE_CONSTS = 9, 2 + W_PIECES, 5 + W_PIECES

        ld_x, ld_ca, ld_cc, st_out = (signal(n, 16) for n in ("ld_x", "ld_ctx_a", "ld_ctx_c", "st_out"))
        ln_stats = [signal(f"ln_stats{k}", 4) for k in range(4)]
        ln_rstd = [signal(f"ln_rstd{k}", 2) for k in range(4)]
        ln_done = [signal(f"ln_done{k}") for k in range(4)]
        pe_ctxt, pe_ctx2t = signal("pe_ctxt"), signal("pe_ctx2t")
        pe_xt = [signal(f"pe_xt{k}") for k in range(4)]
        ctx_s, ctx2_s, xt0_s, xt2_s, ot_s = (signal(f"{n}_ready") for n in ("ctx_t", "ctx2_t", "xt0", "xt2", "ot"))
        hi_xt = {k: signal(f"hi_xt{k}") for k in (1, 3)}
        lo_xt = {k: signal(f"lo_xt{k}") for k in (1, 3)}
        pe_q, pe_kv = signal("pe_q"), signal("pe_kv", 2)
        qkv = signal("qkv_ready", 3)
        pool_xp = signal("pool_xp")
        own_prod = sem("own_prod")
        pool_qk, pool_av = signal("pool_qk", TILES), signal("pool_av", TILES)
        score0 = signal("score0", TILES)
        sub0 = signal("sub0", 4)
        exp0 = signal("exp0", 2)
        rec0_s = signal("rec0_s", 4)
        av_sum = signal("av_sum", TILES)
        o_ready = signal("o_ready", 2)
        pe_ot, pe_wo, x1_s = signal("pe_ot"), signal("pe_wo"), signal("x1_ready")
        sel_s = signal("sel0_ready", 10)
        pe_selt, selt_s, pe_bias = signal("pe_selt"), signal("selt_ready"), signal("pe_bias")
        pe_z, relu_s = signal("pe_z", E0 * FJ), signal("relu_ready", E0 * FJ)
        pe_y, acc_s = signal("pe_y", E0), signal("acc_step", E0 + 1)
        pe_vk, pe_lk, pe_vv, pe_lv = (signal(f"pe_{n}") for n in ("vk", "lk", "vv", "lv"))
        vk_s, lk_s, vv_s, lv_s = (signal(f"{n}_ready") for n in ("vk", "lk", "vv", "lv"))
        pe_sc, sub1, exp1 = signal("pe_scores"), signal("sub1", 2), signal("exp1")
        bd_s = signal("blockdiag_ready", 4)
        pe_val, u_s, pe_bdt, bdt_s = signal("pe_val"), signal("u_ready"), signal("pe_bdt"), signal("bdt_ready")
        pe_att, x3_s = signal("pe_att"), signal("x3_ready")
        pe_lg, lsub, lexp = signal("pe_logits"), signal("lsub", 3), signal("lexp")
        route = signal("route", 11)
        pe_ab, tanh_s = signal("pe_ab", UNITS), signal("tanh_ready", UNITS)
        pr_s, hu_s = signal("pr_ready", UNITS), signal("hu_ready", UNITS)
        pe_f = signal("pe_ffn1", 1 + E1)
        xd_s = signal("xd_step", 1 + E1)

        block = stack.enter_context(nc.Block())

        def run(eng, body):
            for i in (-2, -1, 0, 1, 2):
                body(i)
            with eng.Fori(3, NC - 2) as i:
                body(i)
            for i in (NC - 2, NC - 1, NC, NC + 1):
                body(i)

        def exists(c):
            return not isinstance(c, int) or 0 <= c < NC

        def tail(d):
            return not exists(d + 2)

        def unit_bank(d, u):
            return 2 * (u % 2) if tail(d) else 0 if u == UNITS - 2 else 2

        def unit_out_bank(d, u):
            return (YD, Y)[u % 2] if tail(d) or u == UNITS - 1 else YD

        def product_k(eng, t):
            q = q_sb[:, t, :].rearrange("p (h d) -> p h d", h=HEADS)
            k = kv_sb[:, t, 0:D].rearrange("p (e d) -> p e d", e=HEADS)
            return eng.tensor_tensor(out=prod[:, t % 2, :].rearrange("p (h e d) -> p h e d", h=HEADS, e=HEADS),
                                     in0=q.unsqueeze(2).broadcast_to([P, HEADS, HEADS, HD]),
                                     in1=k.unsqueeze(1).broadcast_to([P, HEADS, HEADS, HD]),
                                     op=ALU.mult)

        def product_v(eng, t):
            v = kv_sb[:, t, D:2 * D].rearrange("p (d e) -> p d e", e=HEADS)
            return eng.tensor_tensor(out=prod[:, t % 2, :].rearrange("p (h d e) -> p h d e", h=HEADS, e=HEADS),
                                     in0=s0[:, t, :, :].unsqueeze(2).broadcast_to([P, HEADS, HD, HEADS]),
                                     in1=v.unsqueeze(1).broadcast_to([P, HEADS, HD, HEADS]),
                                     op=ALU.mult)

        def is_step(i, k):
            return isinstance(i, int) and i == k

        @block.sync
        def _(sp):
            sp.dma_start(gates_raw[:, 0:2], g_x.partition_broadcast(P)).then_inc(s_g, 16)
            sp.dma_start(gates_raw[:, 2:4], g_f.partition_broadcast(P)).then_inc(s_g, 16)

            def body(i):
                if exists(i + 2):
                    c = i + 2
                    if exists(c - 1):
                        sp.wait_ge(ln_done[0].sem, ln_done[0].at(c - 1))
                    if exists(c - 1):
                        sp.wait_ge(pool_xp.sem, pool_xp.at(c - 1))
                    sp.dma_start(x0[:], x_v[:, bass.ds(c, 1)].rearrange("p c j d -> p (c j) d")).then_inc(ld_x.sem, 16)
                    if exists(c - 1):
                        sp.wait_ge(pe_ctxt.sem, pe_ctxt.at(c - 1))
                    sp.dma_start(ctx_a[:], ctx_v[:, bass.ds(c, 1)].rearrange("p c j d -> p (c j) d")).then_inc(ld_ca.sem, 16)
                if exists(i):
                    if exists(i - 1):
                        sp.wait_ge(pe_ctx2t.sem, pe_ctx2t.at(i - 1))
                    sp.dma_start(ctx_c[:], ctx_v[:, bass.ds(i, 1)].rearrange("p c j d -> p (c j) d")).then_inc(ld_cc.sem, 16)
                if exists(i - 2):
                    c = i - 2
                    sp.wait_ge(xd_s.sem, xd_s.at(c))
                    sp.dma_start(out_v[:, bass.ds(c, 1)].rearrange("p c j d -> p (c j) d"), xd[:]).then_inc(st_out.sem, 16)

            body(-2)
            sp.dma_start(ws[:], w_small).then_inc(s_ws, 16)
            sp.dma_start(brow[:], bias_rows.partition_broadcast(P)).then_inc(s_rows, 16)
            sp.dma_start(bcol[:], bias_cols).then_inc(s_cols, 16)
            for n, (piece, ns) in enumerate(pieces(w1_raw)):
                sp.dma_start(piece, w1[:, ns]).then_inc(s_w1[n], 16)
            sp.dma_start(w2_sb[:, :, :].rearrange("p a n -> p (a n)"), w2).then_inc(s_w2, 16)
            sp.dma_start(b2_sb[:], bias2).then_inc(s_w2, 16)
            for n, (piece, ns) in enumerate(pieces(w13_raw)):
                sp.dma_start(piece, w13[:, ns]).then_inc(s_w13[n], 16)
            sp.dma_start(w2u_sb[:, :, :].rearrange("p a n -> p (a n)"), w2u).then_inc(s_w2, 16)
            for i in (-1, 0, 1, 2):
                body(i)
            with sp.Fori(3, NC - 2) as i:
                body(i)
            for i in (NC - 2, NC - 1, NC, NC + 1):
                body(i)
            sp.wait_ge(st_out.sem, st_out.at(NC - 1))

        @block.gpsimd
        def _(pool):
            pool.memset(ident[:], 0.0).then_inc(s_pool, 1)
            pool.memset(before[:], 1.0).then_inc(s_pool, 1)
            pool.wait_ge(s_pool, 2)
            pool.affine_select(out=ident[:], in_=ident[:], compare_op=ALU.not_equal, fill=1.0, base=0,
                               pattern=[[-1, P]], channel_multiplier=1).then_inc(s_pool, 1)
            pool.affine_select(out=before[:], in_=before[:], compare_op=ALU.is_ge, fill=0.0, base=-1,
                               pattern=[[1, E1], [-1, E1]], channel_multiplier=0).then_inc(s_pool, 1)
            pool.iota(thr_i[:], pattern=[[1, TRUNC_MAX]], base=1, channel_multiplier=0).then_inc(s_pool, 1)
            pool.iota(mod_i[:], pattern=[[1, E0], [E0, MOD_K]], base=-2 * E0, channel_multiplier=0).then_inc(s_pool, 1)
            pool.memset(neghalf[:], -0.5).then_inc(s_pool, 1)
            pool.memset(blockdiag[:, 0:2, :], 0.0).then_inc(s_pool, 1)
            pool.memset(blockdiag[:, 2:4, :], 0.0).then_inc(s_pool, 1)
            pool.wait_ge(s_pool, POOL_CONSTS)

            def norm(k, c):
                pool.wait_ge(ln_stats[k].sem, ln_stats[k].at(c))
                pool.tensor_tensor(out=rstd[k][:], in0=ve[k][:], in1=neghalf[:], op=ALU.pow).then_inc(ln_rstd[k].sem, 1)
                pool.wait_ge(ln_rstd[k].sem, ln_rstd[k].at(c, 1))
                if exists(c - 1):
                    pool.wait_ge(ln_done[k].sem, ln_done[k].at(c - 1))
                pool.tensor_tensor(out=nmr[k][:], in0=nmean[k][:], in1=rstd[k][:], op=ALU.mult).then_inc(ln_rstd[k].sem, 1)

            def times_k(c, t):
                pool.wait_ge(qkv.sem, qkv.at(c, 2 + t // 2))
                if t < 2:
                    if exists(c - 1):
                        pool.wait_ge(av_sum.sem, av_sum.at(c - 1, 3 + t))
                else:
                    pool.wait_ge(score0.sem, score0.at(c, t - 1))
                product_k(pool, t).then_inc(pool_qk.sem, 1)

            def times_v(c, t):
                pool.wait_ge(exp0.sem, exp0.at(c, 1 + t // 2))
                if t < 2:
                    pool.wait_ge(score0.sem, score0.at(c, 3 + t))
                else:
                    pool.wait_ge(av_sum.sem, av_sum.at(c, t - 1))
                product_v(pool, t).then_inc(pool_av.sem, 1)

            def first_times():
                if exists(0):
                    pool.wait_ge(qkv.sem, qkv.at(0, 2))
                product_k(pool, 0).then_inc(pool_qk.sem, 2)
                pool.wait_ge(s_dve0, 3)
                add_x0(0)
                if exists(0):
                    pool.wait_ge(qkv.sem, qkv.at(0, 3))
                if exists(0):
                    pool.wait_ge(score0.sem, score0.at(0, 2))
                product_k(pool, 2).then_inc(pool_qk.sem, 2)
                if exists(0):
                    pool.wait_ge(exp0.sem, exp0.at(0, 1))
                if exists(0):
                    pool.wait_ge(score0.sem, score0.at(0, 4))
                product_v(pool, 0).then_inc(pool_av.sem, 2)
                norm(0, 1)
                if exists(0):
                    pool.wait_ge(exp0.sem, exp0.at(0, 2))
                if exists(0):
                    pool.wait_ge(av_sum.sem, av_sum.at(0, 2))
                product_v(pool, 2).then_inc(pool_av.sem, 2)

            def add_x0(a):
                if exists(a - 1):
                    pool.wait_ge(acc_s.sem, acc_s.at(a - 1, 1))
                if exists(a - 1):
                    pool.wait_ge(ln_done[1].sem, ln_done[1].at(a - 1))
                pool.wait_ge(ld_x.sem, ld_x.at(a))
                pool.tensor_tensor(out=xp[:], in0=x0[:], in1=gbo[:].unsqueeze(1).broadcast_to([P, TILES, D]),
                                   op=ALU.add).then_inc(pool_xp.sem, 1)

            def body(i):
                p, a, b, c = i + 2, i + 1, i, i - 1
                first = is_step(a, 0)
                A = exists(a)
                if first:
                    first_times()
                if A and not first:
                    times_k(a, 0)
                if exists(c):
                    norm(2, c)
                if A and not first:
                    times_k(a, 1)
                    times_k(a, 2)
                    add_x0(a)
                    times_k(a, 3)
                    times_v(a, 0)
                if exists(p) and not first:
                    norm(0, p)
                if A and not first:
                    times_v(a, 1)
                    times_v(a, 2)
                    times_v(a, 3)
                if exists(c):
                    norm(3, c)
                if A:
                    norm(1, a)

            run(pool, body)

        @block.scalar
        def _(act):
            def weights():
                act.wait_ge(s_ws, 16)
                act.activation(wg_parts[:, 0:E1], ws[:, WG:WSMALL], ACT.Copy)
                act.activation(wg_high[:, E1:2 * E1], ws[:, WG:WSMALL], ACT.Copy, scale=0.0)
                act.activation(wg_high[:, 0:E1], ws[:, WG:WSMALL], ACT.Copy).then_inc(s_act0, 1)
                for n, (piece, ns) in enumerate(pieces(w1_raw)):
                    act.wait_ge(s_w1[n], 16)
                    act.activation(w1_hi[:, ns], piece, ACT.Copy).then_inc(s_act0, 1)
                for n, (piece, ns) in enumerate(pieces(w13_raw)):
                    act.wait_ge(s_w13[n], 16)
                    act.activation(w13_hi[:, ns], piece, ACT.Copy).then_inc(s_act0, 1)

            def normed(k, src, c):
                act.wait_ge(ln_rstd[k].sem, ln_rstd[k].at(c))
                for j in range(TILES):
                    last = act.activation(xn[k][:, j, :], src[:, j, :], ACT.Identity, bias=nmr[k][:, j:j + 1],
                                          scale=rstd[k][:, j:j + 1])
                last.then_inc(ln_done[k].sem, 1)

            def high(bank_, hi, pe, done, c):
                act.wait_ge(pe.sem, pe.at(c))
                act.activation(hi[:], bank_[:], ACT.Copy).then_inc(done.sem, 1)

            def plain(bank_, dst, pe, done, c):
                act.wait_ge(pe.sem, pe.at(c))
                act.activation(dst[:], bank_[:], ACT.Copy).then_inc(done.sem, 1)

            def relus(b, e, js=range(FJ)):
                for j in js:
                    n = e * FJ + j
                    act.wait_ge(pe_z.sem, pe_z.at(b, n + 1))
                    if e > 0:
                        act.wait_ge(pe_y.sem, pe_y.at(b, e))
                    else:
                        if exists(b - 1):
                            act.wait_ge(pe_y.sem, pe_y.at(b - 1))
                    act.activation(hidden[:, j, :], Z[j][:], ACT.Relu, bias=bcol[:, CB1 + n:CB1 + n + 1]).then_inc(relu_s.sem, 1)

            def tanhs(c, u):
                act.wait_ge(pe_ab.sem, pe_ab.at(c, u + 1))
                if u >= 2:
                    act.wait_ge(pr_s.sem, pr_s.at(c, u - 1))
                else:
                    if exists(c - 1):
                        act.wait_ge(pr_s.sem, pr_s.at(c - 1, UNITS - 1 + u))
                act.activation(th[:, u % 2, :], Z[unit_bank(c, u)][:], ACT.Tanh, scale=0.5).then_inc(tanh_s.sem, 1)

            def exp_heads(a, pair):
                act.wait_ge(sub0.sem, sub0.at(a, 2 * pair + 2))
                s = s0[:, 2 * pair:2 * pair + 2, :, :].rearrange("p t h e -> p (t h e)")
                act.activation(s, s, ACT.Exp, scale=HD ** -0.5).then_inc(exp0.sem, 1)

            def body(i):
                p, a, b, c, d = i + 2, i + 1, i, i - 1, i - 2
                A, B, C, DD = exists(a), exists(b), exists(c), exists(d)
                if is_step(i, 0):
                    act.wait_ge(s_cols, 16)
                if B:
                    relus(b, 0)
                if DD:
                    tanhs(d, 0)
                    if exists(d):
                        act.wait_ge(lsub.sem, lsub.at(d))
                    act.activation(lg[:], lg[:], ACT.Exp).then_inc(lexp.sem, 1)
                if B:
                    relus(b, 1)
                if C:
                    if exists(c - 1):
                        act.wait_ge(pe_xt[2].sem, pe_xt[2].at(c - 1))
                    normed(2, x2, c)
                if DD:
                    tanhs(d, 1)
                if A:
                    exp_heads(a, 0)
                if B:
                    relus(b, 2, (0, 1))
                if C:
                    if exists(c - 1):
                        act.wait_ge(pe_vv.sem, pe_vv.at(c - 1))
                    plain(M[1], xt2, pe_xt[2], xt2_s, c)
                    if exists(c - 1):
                        act.wait_ge(pe_lv.sem, pe_lv.at(c - 1))
                    plain(M[0], ctx2_t, pe_ctx2t, ctx2_s, c)
                if B:
                    relus(b, 2, (2, 3))
                if C:
                    act.wait_ge(pe_vk.sem, pe_vk.at(c))
                    if exists(c - 1):
                        act.wait_ge(pe_sc.sem, pe_sc.at(c - 1))
                    act.activation(vk_t[:], M[1][:], ACT.Identity, bias=bcol[:, CBVK:CBVK + 1]).then_inc(vk_s.sem, 1)
                if DD:
                    tanhs(d, 2)
                if B:
                    relus(b, 3, (0, 1))
                if C:
                    act.wait_ge(pe_lk.sem, pe_lk.at(c))
                    act.activation(lk_t[:], M[0][:], ACT.Identity, bias=bcol[:, CBLK:CBLK + 1]).then_inc(lk_s.sem, 1)
                if B:
                    act.wait_ge(pe_selt.sem, pe_selt.at(b))
                    if exists(b - 1):
                        act.wait_ge(pe_bias.sem, pe_bias.at(b - 1))
                    act.activation(sel_t[:], M[1][0:E0, :], ACT.Copy).then_inc(selt_s.sem, 1)
                    relus(b, 3, (2, 3))
                if A:
                    exp_heads(a, 1)
                if DD:
                    tanhs(d, 3)
                if B:
                    relus(b, 4)
                if exists(p):
                    if exists(p - 1):
                        act.wait_ge(pe_xt[0].sem, pe_xt[0].at(p - 1))
                    normed(0, x0, p)
                if DD:
                    tanhs(d, 4)
                if C:
                    act.wait_ge(sub1.sem, sub1.at(c))
                    act.activation(sc_sb[:], sc_sb[:], ACT.Exp, scale=D ** -0.5).then_inc(exp1.sem, 1)
                if B:
                    relus(b, 5, (0, 1))
                if exists(p):
                    if exists(p - 1):
                        act.wait_ge(pe_kv.sem, pe_kv.at(p - 1))
                    plain(M[0], ctx_t, pe_ctxt, ctx_s, p)
                    if exists(p - 1):
                        act.wait_ge(pe_q.sem, pe_q.at(p - 1))
                    plain(M[1], xt0, pe_xt[0], xt0_s, p)
                if B:
                    relus(b, 5, (2, 3))
                if C:
                    act.wait_ge(pe_bdt.sem, pe_bdt.at(c))
                    if exists(c - 1):
                        act.wait_ge(pe_att.sem, pe_att.at(c - 1))
                    act.activation(blockdiag_t[:, :, :].rearrange("p j n -> p (j n)"), M[0][:], ACT.Copy).then_inc(bdt_s.sem, 1)
                if DD:
                    tanhs(d, 5)
                if B:
                    relus(b, 6)
                if A:
                    if exists(a - 1):
                        act.wait_ge(pe_wo.sem, pe_wo.at(a - 1))
                    plain(M[1], ot, pe_ot, ot_s, a)
                if DD:
                    tanhs(d, 6)
                if B:
                    relus(b, 7)
                if DD and tail(d):
                    tanhs(d, 7)
                    tanhs(d, 8)
                if C:
                    if exists(d):
                        act.wait_ge(pe_xt[3].sem, pe_xt[3].at(d))
                    normed(3, x3, c)
                if DD and not tail(d):
                    tanhs(d, 7)
                if A:
                    if exists(b):
                        act.wait_ge(pe_xt[1].sem, pe_xt[1].at(b))
                    if exists(b):
                        act.wait_ge(sel_s.sem, sel_s.at(b))
                    normed(1, xp, a)
                if DD and not tail(d):
                    tanhs(d, 8)
                if A:
                    if exists(a - 1):
                        act.wait_ge(pe_z.sem, pe_z.at(a - 1))
                    high(M[0], xt_hi[1], pe_xt[1], hi_xt[1], a)
                if DD and tail(d):
                    tanhs(d, 9)
                if DD and not tail(d):
                    tanhs(d, 9)
                if C:
                    if exists(d):
                        act.wait_ge(pe_ab.sem, pe_ab.at(d))
                    high(M[1], xt_hi[3], pe_xt[3], hi_xt[3], c)
                if is_step(i, -2):
                    weights()

            act.wait_ge(s_g, 32)
            act.activation(tg[:], gates_raw[:], ACT.Tanh).then_inc(s_act0, 1)
            run(act, body)

        @block.vector
        def _(dve):
            def consts():
                def step(ins):
                    ins.then_inc(s_dve0, 1)

                dve.wait_ge(s_pool, POOL_CONSTS)
                step(dve.tensor_copy(thr[:], thr_i[:]))
                step(dve.tensor_copy(modv[:], mod_i[:]))
                dve.wait_ge(s_act0, 1)
                dve.wait_ge(s_rows, 16)
                step(dve.tensor_scalar(gbo[:], brow[:, BO:BO + D], tg[:, 0:1], None, ALU.mult))
                step(dve.tensor_scalar(tgh[:], tg[:, 2:3], 0.5, None, ALU.mult))

            def left(n, lo, raw, hi):
                dve.wait_ge(s_act0, n + 2)
                dve.tensor_tensor(out=lo, in0=raw, in1=hi.bitcast(F32), op=ALU.subtract).then_inc(s_dve0, 1)

            def norm_stats(k, src, c):
                for j in range(TILES):
                    last = dve.bn_stats(stats[k][:, j, :], src[:, j, :])
                last.then_inc(ln_stats[k].sem, 1)
                dve.wait_ge(ln_stats[k].sem, ln_stats[k].at(c, 1))
                even, odd = stats[k][:, :, 1:3], stats[k][:, :, 4:6]
                dve.tensor_tensor(out=dmean[k][:], in0=even[:, :, 0], in1=odd[:, :, 0], op=ALU.subtract)
                dve.tensor_tensor(out=msum[k][:], in0=even, in1=odd, op=ALU.add).then_inc(ln_stats[k].sem, 1)
                dve.wait_ge(ln_stats[k].sem, ln_stats[k].at(c, 2))
                if exists(c - 1):
                    dve.wait_ge(ln_rstd[k].sem, ln_rstd[k].at(c - 1))
                dve.scalar_tensor_tensor(out=dmean[k][:], in0=dmean[k][:], scalar=0.25, in1=dmean[k][:], op0=ALU.mult, op1=ALU.mult)
                dve.tensor_scalar(nmean[k][:], msum[k][:, :, 0], -0.5, None, ALU.mult)
                dve.tensor_scalar(var[k][:], msum[k][:, :, 1], 1.0 / D, EPS, ALU.mult, ALU.add).then_inc(ln_stats[k].sem, 1)
                dve.wait_ge(ln_stats[k].sem, ln_stats[k].at(c, 3))
                dve.tensor_tensor(out=ve[k][:], in0=dmean[k][:], in1=var[k][:], op=ALU.add).then_inc(ln_stats[k].sem, 1)

            def low(bank_, hi, lo, hi_done, done, c):
                dve.wait_ge(hi_done.sem, hi_done.at(c))
                dve.tensor_tensor(out=lo[:], in0=bank_[:], in1=hi[:].bitcast(F32), op=ALU.subtract).then_inc(done.sem, 1)

            def expert_out(b, e):
                dve.wait_ge(pe_y.sem, pe_y.at(b, e + 1))
                if e == 0:
                    dve.wait_ge(sel_s.sem, sel_s.at(b))
                    before_, after = xp, acc
                else:
                    dve.wait_ge(acc_s.sem, acc_s.at(b, acc_step(e) - 1))
                    before_, after = acc, x2 if e == E0 - 1 else acc
                if e == E0 - 1:
                    if exists(b - 1):
                        dve.wait_ge(x3_s.sem, x3_s.at(b - 1))
                for j in range(TILES):
                    last = dve.scalar_tensor_tensor(out=after[:, j, :], in0=Y[:, j * P:(j + 1) * P], scalar=sel0[:, j, e:e + 1],
                                                    in1=before_[:, j, :], op0=ALU.mult, op1=ALU.add)
                last.then_inc(acc_s.sem, 1)

            def expert_bias(b):
                dve.wait_ge(pe_bias.sem, pe_bias.at(b))
                dve.wait_ge(acc_s.sem, acc_s.at(b, acc_step(BIAS_AFTER)))
                dve.tensor_tensor(out=acc[:], in0=tiles(M[0]), in1=acc[:], op=ALU.add).then_inc(acc_s.sem, 1)

            def shared_out(d):
                if exists(d - 1):
                    dve.wait_ge(st_out.sem, st_out.at(d - 1))
                residual(YD, tg[:, 3:4], x3, xd, pe_f, xd_s, d, 1)

            def unit_out(d, u):
                bank_ = unit_out_bank(d, u)
                dve.wait_ge(pe_f.sem, pe_f.at(d, u))
                dve.wait_ge(xd_s.sem, xd_s.at(d, u - 1))
                for j in range(TILES):
                    last = dve.scalar_tensor_tensor(out=xd[:, j, :], in0=bank_[:, j * P:(j + 1) * P],
                                                    scalar=gate[:, j, u - SHARED:u - SHARED + 1],
                                                    in1=xd[:, j, :], op0=ALU.mult, op1=ALU.add)
                last.then_inc(xd_s.sem, 1)

            def keys_values(a, half):
                dve.wait_ge(pe_kv.sem, pe_kv.at(a, half + 1))
                dve.tensor_tensor(out=kv_sb[:, 2 * half:2 * half + 2, :],
                                  in0=M[1][:, :].rearrange("p (j d) -> p j d", j=2),
                                  in1=brow[:, BKV:BKV + 2 * D].unsqueeze(1).broadcast_to([P, 2, 2 * D]),
                                  op=ALU.add).then_inc(qkv.sem, 1)

            def sum_k(t):
                return dve.tensor_reduce(out=s0[:, t, :, :].rearrange("p h e -> p (h e)"),
                                         in_=prod[:, t % 2, :].rearrange("p (g d) -> p g d", d=HD), axis=X, op=ALU.add)

            def sum_v(t):
                return dve.tensor_reduce(out=o_sb[:, t, :], in_=prod[:, t % 2, :].rearrange("p (g e) -> p g e", e=HEADS),
                                         axis=X, op=ALU.add)

            def head_scores(a, t):
                dve.wait_ge(pool_qk.sem, pool_qk.at(a, t + 1))
                if t == 0:
                    if exists(a - 1):
                        dve.wait_ge(pool_av.sem, pool_av.at(a - 1))
                sum_k(t).then_inc(score0.sem, 1)

            def head_max(a, pair):
                ts = slice(2 * pair, 2 * pair + 2)
                dve.wait_ge(score0.sem, score0.at(a, 2 * pair + 2))
                dve.tensor_reduce(out=mx0[:, ts, :], in_=s0[:, ts, :, :], axis=X, op=ALU.max).then_inc(sub0.sem, 1)
                dve.wait_ge(sub0.sem, sub0.at(a, 2 * pair + 1))
                s = s0[:, ts, :, :].rearrange("p t h e -> p (t h) e")
                m = mx0[:, ts, :].rearrange("p t h -> p (t h)")
                dve.tensor_tensor(out=s, in0=s, in1=m.unsqueeze(2).broadcast_to([P, 2 * HEADS, HEADS]),
                                  op=ALU.subtract).then_inc(sub0.sem, 1)

            def head_sum(a, pair):
                ts = slice(2 * pair, 2 * pair + 2)
                dve.wait_ge(exp0.sem, exp0.at(a, pair + 1))
                dve.tensor_reduce(out=sum0[:, ts, :], in_=s0[:, ts, :, :], axis=X, op=ALU.add).then_inc(rec0_s.sem, 1)
                dve.wait_ge(rec0_s.sem, rec0_s.at(a, 2 * pair + 1))
                dve.reciprocal(rec0[:, ts, :], sum0[:, ts, :]).then_inc(rec0_s.sem, 1)

            def head_out(a, t):
                dve.wait_ge(pool_av.sem, pool_av.at(a, t + 1))
                if t == 0:
                    dve.wait_ge(pool_qk.sem, pool_qk.at(a))
                sum_v(t).then_inc(av_sum.sem, 1)

            def head_scale(a, pair):
                ts = slice(2 * pair, 2 * pair + 2)
                dve.wait_ge(av_sum.sem, av_sum.at(a, 2 * pair + 2))
                dve.wait_ge(rec0_s.sem, rec0_s.at(a, 2 * pair + 2))
                o = o_sb[:, ts, :].rearrange("p t (h d) -> p (t h) d", h=HEADS)
                r = rec0[:, ts, :].rearrange("p t h -> p (t h)")
                dve.tensor_tensor(out=o, in0=o, in1=r.unsqueeze(2).broadcast_to([P, 2 * HEADS, HD]),
                                  op=ALU.mult).then_inc(o_ready.sem, 1)

            def first_heads():
                if exists(0):
                    dve.wait_ge(qkv.sem, qkv.at(0, 2))
                for pair in range(2):
                    even, odd = 2 * pair, 2 * pair + 1
                    if pair == 1:
                        if exists(0):
                            dve.wait_ge(qkv.sem, qkv.at(0, 3))
                        if exists(0):
                            dve.wait_ge(score0.sem, score0.at(0, 1))
                    product_k(dve, odd).then_inc(own_prod, 1)
                    dve.wait_ge(own_prod, pair + 1)
                    sum_k(odd).then_inc(score0.sem, 1)
                    if exists(0):
                        dve.wait_ge(pool_qk.sem, pool_qk.at(0, even + 2))
                    sum_k(even).then_inc(score0.sem, 1)
                    head_max(0, pair)
                if exists(1):
                    dve.wait_ge(ld_x.sem, ld_x.at(1))
                norm_stats(0, x0, 1)
                for pair in range(2):
                    even, odd = 2 * pair, 2 * pair + 1
                    head_sum(0, pair)
                    if exists(0):
                        dve.wait_ge(score0.sem, score0.at(0, 3))
                    product_v(dve, odd).then_inc(own_prod, 1)
                    if exists(0):
                        dve.wait_ge(pool_av.sem, pool_av.at(0, even + 2))
                    if exists(0):
                        dve.wait_ge(pool_qk.sem, pool_qk.at(0))
                    sum_v(even).then_inc(av_sum.sem, 1)
                    dve.wait_ge(own_prod, pair + 3)
                    sum_v(odd).then_inc(av_sum.sem, 1)
                    head_scale(0, pair)

            def biased(bank_, row, dst, pe, done, c):
                dve.wait_ge(pe.sem, pe.at(c))
                dve.tensor_tensor(out=dst[:], in0=tiles(bank_), in1=brow[:, row:row + D].unsqueeze(1).broadcast_to([P, TILES, D]),
                                  op=ALU.add).then_inc(done.sem, 1)

            def unit_open(c, u):
                dve.wait_ge(tanh_s.sem, tanh_s.at(c, u + 1))
                if u > 0:
                    dve.wait_ge(hu_s.sem, hu_s.at(c, u))
                dve.scalar_tensor_tensor(out=pr[:], in0=th[:, u % 2, :], scalar=1.0, in1=Z[unit_bank(c, u)][:],
                                         op0=ALU.add, op1=ALU.mult).then_inc(pr_s.sem, 1)
                dve.wait_ge(pr_s.sem, pr_s.at(c, u + 1))
                if u >= 2:
                    dve.wait_ge(pe_f.sem, pe_f.at(c, max(1, u - 2)))
                else:
                    if exists(c - 1):
                        dve.wait_ge(pe_f.sem, pe_f.at(c - 1, E1 + u))
                dve.scalar_tensor_tensor(out=hu[:, u % 2, :], in0=pr[:], scalar=0.5, in1=Z[unit_bank(c, u) + 1][:],
                                         op0=ALU.mult, op1=ALU.mult).then_inc(hu_s.sem, 1)

            def units(d, u):
                if tail(d):
                    unit_open(d, u)
                    unit_out(d, u - 1)
                else:
                    unit_out(d, u - 1)
                    unit_open(d, u)

            def select_experts(a):
                s = sel_s.sem
                dve.wait_ge(ln_done[1].sem, ln_done[1].at(a))
                dve.tensor_tensor(out=hsum[:], in0=xn[1][:, :, 0], in1=xn[1][:, :, 1], op=ALU.add).then_inc(s, 1)
                dve.wait_ge(sel_s.sem, sel_s.at(a, 1))
                hs = hsum[:].unsqueeze(2).broadcast_to([P, TILES, TRUNC_MAX])
                th_ = thr[:].unsqueeze(1).broadcast_to([P, TILES, TRUNC_MAX])
                dve.tensor_tensor(out=hge[:], in0=hs, in1=th_, op=ALU.is_ge).then_inc(s, 1)
                dve.scalar_tensor_tensor(out=hle[:], in0=hs, scalar=-1.0, in1=th_, op0=ALU.mult, op1=ALU.is_ge).then_inc(s, 1)
                dve.wait_ge(sel_s.sem, sel_s.at(a, 3))
                dve.tensor_tensor(out=hge[:], in0=hge[:], in1=hle[:], op=ALU.subtract).then_inc(s, 1)
                dve.wait_ge(sel_s.sem, sel_s.at(a, 4))
                dve.tensor_reduce(out=htr[:], in_=hge[:], axis=X, op=ALU.add).then_inc(s, 1)
                dve.wait_ge(sel_s.sem, sel_s.at(a, 5))
                dve.tensor_tensor(out=heq[:], in0=htr[:].unsqueeze(2).unsqueeze(3).broadcast_to([P, TILES, E0, MOD_K]),
                                  in1=modv[:].unsqueeze(1).broadcast_to([P, TILES, E0, MOD_K]), op=ALU.is_equal).then_inc(s, 1)
                dve.wait_ge(sel_s.sem, sel_s.at(a, 6))
                dve.tensor_reduce(out=onehot[:], in_=heq[:], axis=X, op=ALU.add).then_inc(s, 1)
                dve.wait_ge(sel_s.sem, sel_s.at(a, 7))
                if exists(a - 1):
                    dve.wait_ge(pe_selt.sem, pe_selt.at(a - 1))
                dve.tensor_tensor(out=sel01[:, :, 1:E0], in0=onehot[:, :, 1:E0], in1=onehot[:, :, 0:E0 - 1], op=ALU.add).then_inc(s, 1)
                dve.tensor_tensor(out=sel01[:, :, 0], in0=onehot[:, :, 0], in1=onehot[:, :, E0 - 1], op=ALU.add).then_inc(s, 1)
                dve.wait_ge(sel_s.sem, sel_s.at(a, 9))
                dve.tensor_scalar(sel0[:], sel01[:], tgh[:, 0:1], None, ALU.mult).then_inc(s, 1)

            def logits_max(c):
                dve.wait_ge(pe_lg.sem, pe_lg.at(c))
                l = M[1][:, 0:2 * TILES * E1].rearrange("p (j h e) -> p j h e", h=2, e=E1)
                dve.tensor_reduce(out=lg_sum[:], in_=l.rearrange("p j h e -> p j e h"), axis=X, op=ALU.add).then_inc(lsub.sem, 1)
                dve.wait_ge(lsub.sem, lsub.at(c, 1))
                dve.tensor_reduce(out=lmx[:], in_=lg_sum[:], axis=X, op=ALU.max).then_inc(lsub.sem, 1)
                dve.wait_ge(lsub.sem, lsub.at(c, 2))
                dve.tensor_tensor(out=lg[:], in0=lg_sum[:], in1=lmx[:].unsqueeze(2).broadcast_to([P, TILES, E1]),
                                  op=ALU.subtract).then_inc(lsub.sem, 1)

            def route_tokens(c):
                r = route.sem
                dve.wait_ge(lexp.sem, lexp.at(c))
                dve.tensor_reduce(out=lsum[:], in_=lg[:], axis=X, op=ALU.add).then_inc(r, 1)
                dve.wait_ge(route.sem, route.at(c, 1))
                dve.reciprocal(lrec[:], lsum[:]).then_inc(r, 1)
                dve.wait_ge(route.sem, route.at(c, 2))
                dve.tensor_tensor(out=sc1[:], in0=lg[:], in1=lrec[:].unsqueeze(2).broadcast_to([P, TILES, E1]), op=ALU.mult).then_inc(r, 1)
                dve.wait_ge(route.sem, route.at(c, 3))
                dve.tensor_tensor(out=bs1[:], in0=sc1[:], in1=brow[:, BG:BG + E1].unsqueeze(1).broadcast_to([P, TILES, E1]),
                                  op=ALU.add).then_inc(r, 1)
                dve.tensor_scalar(scg[:], sc1[:], tg[:, 3:4], None, ALU.mult).then_inc(r, 1)
                dve.wait_ge(route.sem, route.at(c, 4))
                own = bs1[:].unsqueeze(3).broadcast_to([P, TILES, E1, E1])
                other = bs1[:].unsqueeze(2).broadcast_to([P, TILES, E1, E1])
                dve.tensor_tensor(out=cmp_gt[:], in0=other, in1=own, op=ALU.is_gt).then_inc(r, 1)
                dve.tensor_tensor(out=cmp_eq[:], in0=other, in1=own, op=ALU.is_equal).then_inc(r, 1)
                dve.wait_ge(route.sem, route.at(c, 7))
                dve.tensor_tensor(out=cmp_eq[:], in0=cmp_eq[:], in1=before[:].unsqueeze(1).broadcast_to([P, TILES, E1, E1]),
                                  op=ALU.mult).then_inc(r, 1)
                dve.wait_ge(route.sem, route.at(c, 8))
                dve.tensor_tensor(out=cmp_gt[:], in0=cmp_gt[:], in1=cmp_eq[:], op=ALU.add).then_inc(r, 1)
                dve.wait_ge(route.sem, route.at(c, 9))
                dve.tensor_reduce(out=rank[:], in_=cmp_gt[:], axis=X, op=ALU.add).then_inc(r, 1)
                dve.wait_ge(route.sem, route.at(c, 10))
                dve.scalar_tensor_tensor(out=gate[:], in0=rank[:], scalar=2.0, in1=scg[:], op0=ALU.is_lt, op1=ALU.mult).then_inc(r, 1)
                dve.wait_ge(route.sem, route.at(c, 11))

            def residual(bank_, gate_col, prev, dst, pe, done, c, k=None):
                dve.wait_ge(pe.sem, pe.at(c, k))
                dve.scalar_tensor_tensor(out=dst[:, :, :].rearrange("p j d -> p (j d)"), in0=bank_[:], scalar=gate_col,
                                         in1=prev[:, :, :].rearrange("p j d -> p (j d)"),
                                         op0=ALU.mult, op1=ALU.add).then_inc(done.sem, 1)

            def body(i):
                p, a, b, c, d = i + 2, i + 1, i, i - 1, i - 2
                A, B, C, DD = exists(a), exists(b), exists(c), exists(d)
                first = is_step(a, 0)
                if first:
                    first_heads()
                if B:
                    select_experts(b)
                if is_step(i, 0):
                    for n, (piece, ns) in enumerate(pieces(w13_raw)):
                        left(1 + len(w1_raw) + n, w13_lo[:, ns], piece, w13_hi[:, ns])
                if DD:
                    logits_max(d)
                    unit_open(d, 0)
                if A and not first:
                    head_scores(a, 0)
                if B:
                    expert_out(b, 0)
                if A and not first:
                    head_scores(a, 1)
                    head_max(a, 0)
                if DD:
                    unit_open(d, 1)
                    route_tokens(d)
                if B:
                    expert_out(b, 1)
                if A and not first:
                    head_scores(a, 2)
                if DD:
                    shared_out(d)
                if DD:
                    unit_open(d, 2)
                if A and not first:
                    head_scores(a, 3)
                    head_max(a, 1)
                if B:
                    expert_out(b, 2)
                if A and not first:
                    head_sum(a, 0)
                    head_out(a, 0)
                if C:
                    if exists(c - 1):
                        dve.wait_ge(pe_val.sem, pe_val.at(c - 1))
                    biased(M[0], BVV, vv_sb, pe_vv, vv_s, c)
                if exists(p) and not first:
                    if exists(p):
                        dve.wait_ge(ld_x.sem, ld_x.at(p))
                    norm_stats(0, x0, p)
                if DD:
                    units(d, 3)
                if C:
                    if exists(c - 1):
                        dve.wait_ge(pe_att.sem, pe_att.at(c - 1))
                    biased(M[1], BLV, lv_sb, pe_lv, lv_s, c)
                if B:
                    expert_out(b, 3)
                    expert_bias(b)
                if A and not first:
                    head_sum(a, 1)
                    head_out(a, 1)
                if C:
                    dve.wait_ge(pe_sc.sem, pe_sc.at(c))
                    s = M[1][:, 0:TILES * SEQ].rearrange("p (j n) -> p j n", n=SEQ)
                    dve.tensor_reduce(out=mx1[:], in_=s, axis=X, op=ALU.max).then_inc(sub1.sem, 1)
                    dve.wait_ge(sub1.sem, sub1.at(c, 1))
                    dve.tensor_tensor(out=sc_sb[:], in0=s, in1=mx1[:].unsqueeze(2).broadcast_to([P, TILES, SEQ]),
                                      op=ALU.subtract).then_inc(sub1.sem, 1)
                if DD:
                    units(d, 4)
                if A and not first:
                    head_scale(a, 0)
                if B:
                    expert_out(b, 4)
                if C:
                    dve.wait_ge(exp1.sem, exp1.at(c))
                    dve.tensor_reduce(out=sum1[:], in_=sc_sb[:], axis=X, op=ALU.add).then_inc(bd_s.sem, 1)
                    dve.wait_ge(bd_s.sem, bd_s.at(c, 1))
                    dve.reciprocal(rec1[:], sum1[:]).then_inc(bd_s.sem, 1)
                    dve.wait_ge(bd_s.sem, bd_s.at(c, 2))
                    if exists(c - 1):
                        dve.wait_ge(pe_val.sem, pe_val.at(c - 1))
                    for h in range(2):
                        ps = slice(h * SEQ, (h + 1) * SEQ)
                        dve.tensor_tensor(out=blockdiag[ps, :, h * SEQ:(h + 1) * SEQ], in0=sc_sb[ps, :, :],
                                          in1=rec1[ps, :].unsqueeze(2).broadcast_to([SEQ, TILES, SEQ]),
                                          op=ALU.mult).then_inc(bd_s.sem, 1)
                if A and not first:
                    head_out(a, 2)
                if DD:
                    units(d, 5)
                if A and not first:
                    head_out(a, 3)
                    head_scale(a, 1)
                if B:
                    expert_out(b, 5)
                if C:
                    dve.wait_ge(pe_val.sem, pe_val.at(c))
                    dve.wait_ge(lv_s.sem, lv_s.at(c))
                    dve.tensor_tensor(out=u_sb[:], in0=tiles(M[1]), in1=lv_sb[:], op=ALU.add).then_inc(u_s.sem, 1)
                    if exists(d):
                        dve.wait_ge(xd_s.sem, xd_s.at(d, 1))
                    residual(M[0], tg[:, 1:2], x2, x3, pe_att, x3_s, c)
                if DD:
                    units(d, 6)
                if C:
                    dve.wait_ge(x3_s.sem, x3_s.at(c))
                    norm_stats(3, x3, c)
                if B:
                    expert_out(b, 6)
                if A:
                    dve.wait_ge(pool_xp.sem, pool_xp.at(a))
                    residual(M[0], tg[:, 0:1], xp, xp, pe_wo, x1_s, a)
                if is_step(i, -2):
                    dve.wait_ge(s_rows, 16)
                if first:
                    if exists(a):
                        dve.wait_ge(x1_s.sem, x1_s.at(a))
                    norm_stats(1, xp, a)
                if exists(p):
                    if exists(p - 1):
                        dve.wait_ge(pool_av.sem, pool_av.at(p - 1))
                    keys_values(p, 0)
                if A and not first:
                    if exists(a):
                        dve.wait_ge(x1_s.sem, x1_s.at(a))
                    norm_stats(1, xp, a)
                if exists(p):
                    dve.wait_ge(pe_q.sem, pe_q.at(p))
                    if exists(p - 1):
                        dve.wait_ge(pe_ot.sem, pe_ot.at(p - 1))
                    dve.tensor_tensor(out=q_sb[:], in0=tiles(M[0]), in1=brow[:, BQ:BQ + D].unsqueeze(1).broadcast_to([P, TILES, D]),
                                      op=ALU.add).then_inc(qkv.sem, 1)
                    keys_values(p, 1)
                if is_step(i, -2):
                    consts()
                if is_step(i, -1):
                    left(0, wg_parts[:, E1:2 * E1], ws[:, WG:WSMALL], wg_parts[:, 0:E1])
                    for n, (piece, ns) in enumerate(pieces(w1_raw)):
                        left(1 + n, w1_lo[:, ns], piece, w1_hi[:, ns])
                if DD:
                    units(d, 7)
                if B:
                    expert_out(b, 7)
                if DD:
                    units(d, 8)
                if A:
                    if exists(a - 1):
                        dve.wait_ge(pe_z.sem, pe_z.at(a - 1))
                    low(M[0], xt_hi[1], xt_lo[1], hi_xt[1], lo_xt[1], a)
                if DD and tail(d):
                    unit_open(d, 9)
                    unit_out(d, 8)
                    unit_out(d, 9)
                if DD and not tail(d):
                    unit_open(d, 9)
                if C:
                    if exists(d):
                        dve.wait_ge(pe_ab.sem, pe_ab.at(d))
                    low(M[1], xt_hi[3], xt_lo[3], hi_xt[3], lo_xt[3], c)
                if DD and not tail(d):
                    unit_out(d, 8)
                if B:
                    dve.wait_ge(acc_s.sem, acc_s.at(b))
                    norm_stats(2, x2, b)
                if DD and not tail(d):
                    unit_out(d, 9)

            run(dve, body)

        @block.tensor
        def _(pe):
            def transposes(bank_, src):
                for j in range(TILES):
                    last = pe.transpose(bank_[:, j * P:(j + 1) * P], src[:, j, :], ident[:])
                return last

            def three(dst, l_hi, l_lo, r_hi, r_lo):
                pe.matmul(dst, l_hi, r_hi, start=True, stop=False)
                pe.matmul(dst, l_lo, r_hi, start=False, stop=False)
                return pe.matmul(dst, l_hi, r_lo, start=False, stop=True)

            def by_token(bank_, t, w, width, which=range(TILES)):
                for n, j in enumerate(which):
                    last = pe.matmul(bank_[:, n * width:(n + 1) * width], t[:, j * P:(j + 1) * P], ws[:, w:w + width],
                                     start=True, stop=True)
                return last

            def by_width(bank_, w_hi, w_lo, w, t_hi, t_lo):
                return three(bank_[:], w_hi[:, w:w + P], w_lo[:, w:w + P], t_hi[:], t_lo[:])

            def ffn0_in(b, e, js):
                for j in js:
                    n = e * FJ + j
                    if e > 0:
                        pe.wait_ge(relu_s.sem, relu_s.at(b, n + 1 - FJ))
                        if j == 2:
                            if exists(b - 2):
                                pe.wait_ge(hu_s.sem, hu_s.at(b - 2, e))
                    else:
                        if j == 0:
                            pe.wait_ge(hi_xt[1].sem, hi_xt[1].at(b))
                            pe.wait_ge(lo_xt[1].sem, lo_xt[1].at(b))
                            if is_step(b, 0):
                                pe.wait_ge(s_act0, ACT_CONSTS - len(w13_raw))
                                pe.wait_ge(s_dve0, DVE_CONSTS - len(w13_raw))
                                pe.wait_ge(s_w2, 48)
                        if j < 2:
                            if exists(b - 1):
                                pe.wait_ge(relu_s.sem, relu_s.at(b - 1, E0 * FJ))
                            if exists(b - 3):
                                pe.wait_ge(hu_s.sem, hu_s.at(b - 3, UNITS - 1))
                        else:
                            if exists(b - 3):
                                pe.wait_ge(hu_s.sem, hu_s.at(b - 3))
                    by_width(Z[j], w1_hi, w1_lo, n * P, xt_hi[1], xt_lo[1]).then_inc(pe_z.sem, 1)

            def ffn0_out(b, e):
                if e > 0:
                    pe.wait_ge(acc_s.sem, acc_s.at(b, acc_step(e - 1)))
                else:
                    if exists(b - 1):
                        pe.wait_ge(acc_s.sem, acc_s.at(b - 1))
                    if exists(b - 3):
                        pe.wait_ge(xd_s.sem, xd_s.at(b - 3))
                pe.wait_ge(relu_s.sem, relu_s.at(b, FJ * (e + 1)))
                for j in range(TILES):
                    js = slice(j * P, (j + 1) * P)
                    for f in range(FJ):
                        last = pe.matmul(Y[:, js], hidden[:, f, js], w2_sb[:, e * FJ + f, :], start=(f == 0), stop=(f == FJ - 1))
                last.then_inc(pe_y.sem, 1)

            def unit_in(d, u):
                if tail(d):
                    if u < 2:
                        if exists(d + 1):
                            pe.wait_ge(relu_s.sem, relu_s.at(d + 1))
                        if exists(d - 1):
                            pe.wait_ge(hu_s.sem, hu_s.at(d - 1))
                    else:
                        pe.wait_ge(hu_s.sem, hu_s.at(d, u - 1))
                elif u < UNITS - 2:
                    if exists(d + 2):
                        pe.wait_ge(relu_s.sem, relu_s.at(d + 2, FJ * (u + 1)))
                    if u > 0:
                        pe.wait_ge(hu_s.sem, hu_s.at(d, u))
                elif u == UNITS - 2:
                    if exists(d + 2):
                        pe.wait_ge(relu_s.sem, relu_s.at(d + 2))
                else:
                    pe.wait_ge(hu_s.sem, hu_s.at(d, u - 1))
                z = unit_bank(d, u)
                by_width(Z[z], w13_hi, w13_lo, 2 * u * P, xt_hi[3], xt_lo[3])
                by_width(Z[z + 1], w13_hi, w13_lo, (2 * u + 1) * P, xt_hi[3], xt_lo[3]).then_inc(pe_ab.sem, 1)

            def unit_out(d, u):
                bank_ = unit_out_bank(d, u)
                if tail(d) and u > 3:
                    pe.wait_ge(xd_s.sem, xd_s.at(d, u - 2))
                elif tail(d) and u == 3:
                    if exists(d + 1):
                        pe.wait_ge(acc_s.sem, acc_s.at(d + 1))
                    if exists(d - 1):
                        pe.wait_ge(xd_s.sem, xd_s.at(d - 1))
                elif u == UNITS - 1:
                    if exists(d + 2):
                        pe.wait_ge(acc_s.sem, acc_s.at(d + 2))
                    if exists(d - 1):
                        pe.wait_ge(xd_s.sem, xd_s.at(d - 1))
                else:
                    pe.wait_ge(xd_s.sem, xd_s.at(d, u - 1))
                pe.wait_ge(hu_s.sem, hu_s.at(d, u + 1))
                for j in range(TILES):
                    js = slice(j * P, (j + 1) * P)
                    last = pe.matmul(bank_[:, js], hu[:, u % 2, js], w2u_sb[:, u, :], start=True, stop=True)
                last.then_inc(pe_f.sem, 1)

            def units(d, u):
                if tail(d):
                    unit_in(d, u)
                    unit_out(d, u - 1)
                else:
                    unit_out(d, u - 1)
                    unit_in(d, u)

            def shared_out(d):
                if exists(d - 1):
                    pe.wait_ge(xd_s.sem, xd_s.at(d - 1, E1))
                pe.wait_ge(hu_s.sem, hu_s.at(d, SHARED))
                for j in range(TILES):
                    js = slice(j * P, (j + 1) * P)
                    for u in range(SHARED):
                        last = pe.matmul(YD[:, js], hu[:, u, js], w2u_sb[:, u, :], start=(u == 0), stop=(u == SHARED - 1))
                last.then_inc(pe_f.sem, 1)

            def body(i):
                p, a, b, c, d = i + 2, i + 1, i, i - 1, i - 2
                A, B, C, DD = exists(a), exists(b), exists(c), exists(d)
                if is_step(i, -2):
                    pe.wait_ge(s_pool, POOL_CONSTS)
                if is_step(i, 1):
                    pe.wait_ge(s_act0, ACT_CONSTS)
                    pe.wait_ge(s_dve0, DVE_CONSTS)
                if B:
                    ffn0_in(b, 0, (2, 3))
                    ffn0_in(b, 1, (0, 1))
                if DD:
                    if exists(d):
                        pe.wait_ge(hi_xt[3].sem, hi_xt[3].at(d))
                    if exists(d):
                        pe.wait_ge(lo_xt[3].sem, lo_xt[3].at(d))
                    for j in range(TILES):
                        js = slice(j * P, (j + 1) * P)
                        cols = slice(2 * j * E1, 2 * (j + 1) * E1)
                        pe.matmul(M[1][:, cols], xt_hi[3][:, js], wg_parts[:], start=True, stop=False)
                        last = pe.matmul(M[1][:, cols], xt_lo[3][:, js], wg_high[:], start=False, stop=True)
                    last.then_inc(pe_lg.sem, 1)
                    unit_in(d, 0)
                if B:
                    ffn0_out(b, 0)
                if B:
                    ffn0_in(b, 1, (2, 3))
                    ffn0_in(b, 2, (0, 1))
                if C:
                    if exists(a):
                        pe.wait_ge(qkv.sem, qkv.at(a))
                    pe.wait_ge(ld_cc.sem, ld_cc.at(c))
                    transposes(M[0], ctx_c).then_inc(pe_ctx2t.sem, 1)
                if DD:
                    unit_in(d, 1)
                if B:
                    ffn0_out(b, 1)
                if C:
                    pe.wait_ge(ln_done[2].sem, ln_done[2].at(c))
                    if exists(d):
                        pe.wait_ge(lsub.sem, lsub.at(d))
                    transposes(M[1], xn[2]).then_inc(pe_xt[2].sem, 1)
                if B:
                    ffn0_in(b, 2, (2, 3))
                    ffn0_in(b, 3, (0, 1))
                if C:
                    pe.wait_ge(xt2_s.sem, xt2_s.at(c))
                    pe.matmul(M[1][:], ws[:, WVK:WVK + P], xt2[:], start=True, stop=True).then_inc(pe_vk.sem, 1)
                if DD:
                    shared_out(d)
                    unit_in(d, 2)
                if B:
                    ffn0_out(b, 2)
                if C:
                    pe.wait_ge(ctx2_s.sem, ctx2_s.at(c))
                    pe.matmul(M[0][:], ws[:, WLK:WLK + P], ctx2_t[:], start=True, stop=True).then_inc(pe_lk.sem, 1)
                if B:
                    if not C:
                        if exists(a):
                            pe.wait_ge(qkv.sem, qkv.at(a))
                    pe.wait_ge(sel_s.sem, sel_s.at(b))
                    if exists(c):
                        pe.wait_ge(vk_s.sem, vk_s.at(c))
                    for j in range(TILES):
                        last = pe.transpose(M[1][0:E0, j * P:(j + 1) * P], sel0[:, j, :], ident[:])
                    last.then_inc(pe_selt.sem, 1)
                if B:
                    ffn0_in(b, 3, (2, 3))
                    ffn0_in(b, 4, (0, 1))
                if C:
                    pe.wait_ge(lk_s.sem, lk_s.at(c))
                    by_token(M[0], xt2, WVV, D).then_inc(pe_vv.sem, 1)
                if DD:
                    units(d, 3)
                if B:
                    ffn0_out(b, 3)
                if C:
                    pe.wait_ge(vk_s.sem, vk_s.at(c))
                    if exists(b):
                        pe.wait_ge(selt_s.sem, selt_s.at(b))
                    by_token(M[1], ctx2_t, WLV, D).then_inc(pe_lv.sem, 1)
                if B:
                    pe.wait_ge(selt_s.sem, selt_s.at(b))
                    if exists(c):
                        pe.wait_ge(vv_s.sem, vv_s.at(c))
                    for j in range(TILES):
                        js = slice(j * P, (j + 1) * P)
                        last = pe.matmul(M[0][:, js], sel_t[:, js], b2_sb[:], start=True, stop=True)
                    last.then_inc(pe_bias.sem, 1)
                if B:
                    ffn0_in(b, 4, (2, 3))
                    ffn0_in(b, 5, (0, 1))
                if C:
                    pe.wait_ge(lv_s.sem, lv_s.at(c))
                    for j in range(TILES):
                        for h in range(2):
                            ts = slice(j * P + h * SEQ, j * P + (h + 1) * SEQ)
                            last = pe.matmul(M[1][h * SEQ:(h + 1) * SEQ, j * SEQ:(j + 1) * SEQ], vk_t[:, ts], lk_t[:, ts],
                                             start=True, stop=True)
                    last.then_inc(pe_sc.sem, 1)
                if DD:
                    units(d, 4)
                if B:
                    ffn0_out(b, 4)
                if exists(p):
                    if not B:
                        if exists(a):
                            pe.wait_ge(qkv.sem, qkv.at(a))
                    if exists(b):
                        pe.wait_ge(acc_s.sem, acc_s.at(b, acc_step(BIAS_AFTER) + 1))
                    pe.wait_ge(ld_ca.sem, ld_ca.at(p))
                    transposes(M[0], ctx_a).then_inc(pe_ctxt.sem, 1)
                    pe.wait_ge(ln_done[0].sem, ln_done[0].at(p))
                    if exists(c):
                        pe.wait_ge(sub1.sem, sub1.at(c))
                    transposes(M[1], xn[0]).then_inc(pe_xt[0].sem, 1)
                if B:
                    ffn0_in(b, 5, (2, 3))
                    ffn0_in(b, 6, (0, 1))
                if C:
                    pe.wait_ge(bd_s.sem, bd_s.at(c))
                    if not exists(p):
                        if exists(b):
                            pe.wait_ge(acc_s.sem, acc_s.at(b, acc_step(BIAS_AFTER) + 1))
                    if exists(p):
                        pe.wait_ge(ctx_s.sem, ctx_s.at(p))
                    transposes(M[0], blockdiag).then_inc(pe_bdt.sem, 1)
                if DD:
                    units(d, 5)
                if B:
                    ffn0_out(b, 5)
                if C:
                    if exists(p):
                        pe.wait_ge(xt0_s.sem, xt0_s.at(p))
                    for j in range(TILES):
                        last = pe.matmul(M[1][:, j * P:(j + 1) * P], blockdiag[:, j, :], vv_sb[:, j, :], start=True, stop=True)
                    last.then_inc(pe_val.sem, 1)
                if B:
                    ffn0_in(b, 6, (2, 3))
                    ffn0_in(b, 7, (0, 1))
                if C:
                    pe.wait_ge(bdt_s.sem, bdt_s.at(c))
                    pe.wait_ge(u_s.sem, u_s.at(c))
                    for j in range(TILES):
                        last = pe.matmul(M[0][:, j * P:(j + 1) * P], blockdiag_t[:, j, :], u_sb[:, j, :], start=True, stop=True)
                    last.then_inc(pe_att.sem, 1)
                if A:
                    if exists(p):
                        pe.wait_ge(xt0_s.sem, xt0_s.at(p))
                    if exists(c):
                        pe.wait_ge(u_s.sem, u_s.at(c))
                    pe.wait_ge(o_ready.sem, o_ready.at(a))
                    transposes(M[1], o_sb).then_inc(pe_ot.sem, 1)
                if DD:
                    units(d, 6)
                if B:
                    ffn0_out(b, 6)
                if A:
                    pe.wait_ge(ot_s.sem, ot_s.at(a))
                    if exists(p):
                        pe.wait_ge(ctx_s.sem, ctx_s.at(p))
                    if exists(c):
                        pe.wait_ge(x3_s.sem, x3_s.at(c))
                    by_token(M[0], ot, WO, D).then_inc(pe_wo.sem, 1)
                if is_step(i, -2):
                    pe.wait_ge(s_ws, 16)
                if exists(p):
                    pe.wait_ge(ctx_s.sem, ctx_s.at(p))
                    pe.wait_ge(xt0_s.sem, xt0_s.at(p))
                    if exists(a):
                        pe.wait_ge(ot_s.sem, ot_s.at(a))
                    by_token(M[1], ctx_t, WKV, 2 * D, (0, 1)).then_inc(pe_kv.sem, 1)
                if B:
                    ffn0_in(b, 7, (2, 3))
                if exists(p):
                    if exists(a):
                        pe.wait_ge(x1_s.sem, x1_s.at(a))
                    by_token(M[0], xt0, WQ, D).then_inc(pe_q.sem, 1)
                    pe.wait_ge(qkv.sem, qkv.at(p, 1))
                    by_token(M[1], ctx_t, WKV, 2 * D, (2, 3)).then_inc(pe_kv.sem, 1)
                if DD:
                    units(d, 7)
                if B:
                    ffn0_out(b, 7)
                if DD:
                    units(d, 8)
                if DD:
                    unit_in(d, 9)
                if DD and tail(d):
                    unit_out(d, 8)
                    unit_out(d, 9)
                if A:
                    pe.wait_ge(ln_done[1].sem, ln_done[1].at(a))
                    if exists(p):
                        pe.wait_ge(qkv.sem, qkv.at(p, 2))
                    transposes(M[0], xn[1]).then_inc(pe_xt[1].sem, 1)
                if C:
                    pe.wait_ge(ln_done[3].sem, ln_done[3].at(c))
                    if exists(a):
                        pe.wait_ge(ot_s.sem, ot_s.at(a))
                    if exists(p):
                        pe.wait_ge(qkv.sem, qkv.at(p, 3))
                    transposes(M[1], xn[3]).then_inc(pe_xt[3].sem, 1)
                if DD and not tail(d):
                    unit_out(d, 8)
                if A:
                    ffn0_in(a, 0, (0, 1))
                if DD and not tail(d):
                    unit_out(d, 9)

            run(pe, body)


def kernel(x, ctx_1024, g_xattn, g_ffn, L0_xattn_Wq, L0_xattn_bq, L0_xattn_Wk, L0_xattn_bk, L0_xattn_Wv, L0_xattn_bv,
           L0_xattn_Wo, L0_xattn_bo, L0_ffn_W1, L0_ffn_b1, L0_ffn_W2, L0_ffn_b2, L1_xattn_W_vk, L1_xattn_b_vk,
           L1_xattn_W_lk, L1_xattn_b_lk, L1_xattn_W_vv, L1_xattn_b_vv, L1_xattn_W_lv, L1_xattn_b_lv, L1_ffn_gate_w,
           L1_ffn_gate_bias, L1_ffn_w1, L1_ffn_w3, L1_ffn_w2, L1_ffn_sw1, L1_ffn_sw3, L1_ffn_sw2):
    import concourse.bacc as bacc
    import numpy as np
    from concourse.bass_utils import run_bass_kernel_spmd

    shape = np.asarray(x).shape
    a = {k: np.asarray(v) for k, v in dict(locals()).items() if k[0] == "L" or k in ("g_xattn", "g_ffn")}

    def width_first(w):
        return np.ascontiguousarray(w.reshape(HEADS, HD, -1).swapaxes(0, 1).reshape(w.shape))

    w_small = np.concatenate([
        a["L0_xattn_Wq"].T, a["L0_xattn_Wk"].T, width_first(a["L0_xattn_Wv"]).T, a["L0_xattn_Wo"].T,
        a["L1_xattn_W_vk"].T, a["L1_xattn_W_lk"].T, a["L1_xattn_W_vv"].T, a["L1_xattn_W_lv"].T, a["L1_ffn_gate_w"].T], axis=1)
    w1 = a["L0_ffn_W1"].transpose(1, 0, 2).reshape(P, -1)
    w2 = a["L0_ffn_W2"].reshape(E0, FJ, P, D).transpose(2, 0, 1, 3).reshape(P, -1)
    up = np.concatenate([a["L1_ffn_sw1"].reshape(SHARED, P, D), a["L1_ffn_w1"]], axis=0)
    gt = np.concatenate([a["L1_ffn_sw3"].reshape(SHARED, P, D), a["L1_ffn_w3"]], axis=0)
    w13 = np.stack([up, gt], axis=1).transpose(3, 0, 1, 2).reshape(P, -1)
    down = np.concatenate([a["L1_ffn_sw2"].reshape(D, SHARED, P).transpose(1, 0, 2), a["L1_ffn_w2"]], axis=0)
    w2u = down.transpose(2, 0, 1).reshape(P, -1)
    rows = np.concatenate([a["L0_xattn_bq"], a["L0_xattn_bk"], width_first(a["L0_xattn_bv"]), a["L0_xattn_bo"],
                           a["L1_xattn_b_vv"], a["L1_xattn_b_lv"], a["L1_ffn_gate_bias"]])
    cols = np.concatenate([a["L0_ffn_b1"].reshape(E0 * FJ, P), a["L1_xattn_b_vk"].reshape(1, P), a["L1_xattn_b_lk"].reshape(1, P)], axis=0).T
    arrays = {
        "x": np.asarray(x).reshape(-1, D), "ctx": np.asarray(ctx_1024).reshape(-1, D), "g_x": a["g_xattn"], "g_f": a["g_ffn"],
        "w_small": w_small, "w1": w1, "w2": w2, "w13": w13, "w2u": w2u, "rows": rows, "cols": cols, "b2": a["L0_ffn_b2"],
    }
    arrays = {f"in_{k}": np.ascontiguousarray(v) for k, v in arrays.items()}
    nc = bacc.Bacc("TRN2", target_bir_lowering=False, num_devices=1)
    ins = [nc.dram_tensor(k, v.shape, mybir.dt.from_np(v.dtype), kind="ExternalInput").ap() for k, v in arrays.items()]
    out = nc.dram_tensor("out_0", arrays["in_x"].shape, F32, kind="ExternalOutput").ap()
    build(nc, *ins, out)
    r = run_bass_kernel_spmd(nc, [arrays], core_ids=[0])
    return r.results[0]["out_0"].reshape(shape)
```
